# Optimizing a Trainium2 kernel written in Bass

```python
import numpy as np
import jax
import jax.numpy as jnp

def _softmax(x, axis=-1):
    return jax.nn.softmax(x, axis=axis)

def _gelu(x):
    return jax.nn.gelu(x, approximate=True)

def _silu(x):
    return jax.nn.silu(x)

def _sigmoid(x):
    return jax.nn.sigmoid(x)

def _layernorm(x, axis=-1, eps=1e-05):
    m = jnp.mean(x, axis=axis, keepdims=True)
    v = jnp.var(x, axis=axis, keepdims=True)
    return (x - m) / jnp.sqrt(v + eps)

def _scatter_add(tgt, idx, src, axis=0):
    return tgt.at[idx].add(src)

def _segment_sum(src, seg, n):
    return jax.ops.segment_sum(src, seg, n)
kernel_name = 'mk_vit_tower_cls_d2_tok_img256_r4_a1542a'

def setup_inputs(seed: int=0):
    np.random.seed(seed)
    _w = jnp.asarray

    def _rec_inputs():
        import jax
        import jax.numpy as jnp
        _rk = jax.random.key(seed)
        x = -0.00016672 + 0.999947 * jax.random.normal(jax.random.fold_in(_rk, 1), (64, 3, 224, 224), jnp.float32)
        cls_tok = 0.02 * jax.random.normal(jax.random.fold_in(_rk, 5), (1, 1, 64), jnp.float32)
        return (x, cls_tok)
    x, cls_tok = _rec_inputs()

    def _L0_tok_setup():
        import jax, jax.numpy as jnp
        import numpy as np
        PATCH = 16
        key = jax.random.key(seed)
        k1, k2, k3 = jax.random.split(key, 3)
        B, C, H, Wd = (64, 3, 96, 96)
        E = 64
        pdim = PATCH * PATCH * C
        x = jax.random.normal(k1, (B, C, H, Wd), dtype=jnp.float32)
        W = jax.random.normal(k2, (E, pdim), dtype=jnp.float32) * pdim ** (-0.5)
        b = jax.random.normal(k3, (E,), dtype=jnp.float32) * 0.01
        return {'x': x, 'W': W, 'b': b}
    _L0_tok_all = _L0_tok_setup()
    _L0_tok_in = {k: v for k, v in _L0_tok_all.items() if k in ('W', 'b')}
    del _L0_tok_all

    def _L0_attn_setup():
        import jax, jax.numpy as jnp
        import numpy as np
        import math
        B, T, D_MODEL = (1, 512, 64)
        N_Q, N_KV = (16, 1)
        D_HEAD = D_MODEL // N_KV
        QPG = N_Q // N_KV
        ROPE_BASE = 10000.0
        WINDOW = 128
        EPS = 1.1920929e-07
        NEG = -1e+30

        def _rope(x, base=ROPE_BASE):
            t, d = (x.shape[-2], x.shape[-1])
            freqs = base ** (-2.0 * jnp.arange(d // 2, dtype=jnp.float32) / d)
            theta = jnp.arange(t, dtype=jnp.float32)[:, None] * freqs[None, :]
            cos, sin = (jnp.cos(theta), jnp.sin(theta))
            x1, x2 = (x[..., 0::2], x[..., 1::2])
            r1 = x1 * cos - x2 * sin
            r2 = x1 * sin + x2 * cos
            return jnp.stack([r1, r2], axis=-1).reshape(x.shape)

        def _rmsnorm(x, w):
            return x * jax.lax.rsqrt(jnp.mean(x * x, axis=-1, keepdims=True) + EPS) * w
        key = jax.random.key(seed)
        k0, k1, k2, k3 = jax.random.split(key, 4)
        x = jax.random.normal(k0, (B, T, D_MODEL), dtype=jnp.float32)
        wq = jax.random.normal(k1, (QPG * N_KV * D_HEAD, D_MODEL), dtype=jnp.float32) * 0.02
        wkv = jax.random.normal(k2, (2 * D_HEAD * N_KV, D_MODEL), dtype=jnp.float32) * 0.02
        wo = jax.random.normal(k3, (D_MODEL, D_HEAD * N_Q * N_KV), dtype=jnp.float32) * 0.02
        q_norm_w = jnp.ones((D_HEAD,), dtype=jnp.float32)
        k_norm_w = jnp.ones((D_HEAD,), dtype=jnp.float32)
        return {'x': x, 'wq': wq, 'wkv': wkv, 'wo': wo, 'q_norm_w': q_norm_w, 'k_norm_w': k_norm_w}
    _L0_attn_all = _L0_attn_setup()
    _L0_attn_in = {k: v for k, v in _L0_attn_all.items() if k in ('wq', 'wkv', 'wo', 'q_norm_w', 'k_norm_w')}
    del _L0_attn_all

    def _L0_ffn_setup():
        import jax, jax.numpy as jnp
        import numpy as np
        B, S, D, F, E, K = (8, 512, 64, 256, 8, 2)
        key = jax.random.key(seed)
        ks = jax.random.split(key, 10)
        s = 0.02
        return {'x': jax.random.normal(ks[0], (B, S, D), dtype=jnp.float32), 'Wr': jax.random.normal(ks[1], (D, E), dtype=jnp.float32) * s, 'W1s': jax.random.normal(ks[2], (D, F), dtype=jnp.float32) * s, 'b1s': jnp.zeros((F,), dtype=jnp.float32), 'W2s': jax.random.normal(ks[3], (F, D), dtype=jnp.float32) * s, 'b2s': jnp.zeros((D,), dtype=jnp.float32), 'W1p': jax.random.normal(ks[4], (E, D, F), dtype=jnp.float32) * s, 'b1p': jnp.zeros((E, F), dtype=jnp.float32), 'W2p': jax.random.normal(ks[5], (E, F, D), dtype=jnp.float32) * s, 'b2p': jnp.zeros((E, D), dtype=jnp.float32)}
    _L0_ffn_all = _L0_ffn_setup()
    _L0_ffn_in = {k: v for k, v in _L0_ffn_all.items() if k in ('Wr', 'W1s', 'b1s', 'W2s', 'b2s', 'W1p', 'b1p', 'W2p', 'b2p')}
    del _L0_ffn_all

    def _L1_attn_setup():
        import jax, jax.numpy as jnp
        import numpy as np
        B, N, C, H = (8, 4096, 64, 8)
        D = C // H
        GH = C // 4
        key = jax.random.key(seed)
        ks = jax.random.split(key, 6)
        s = 0.02
        return {'x': jax.random.normal(ks[0], (B, N, C), dtype=jnp.float32), 'Wqkv': jax.random.normal(ks[1], (C, 3 * C), dtype=jnp.float32) * s, 'Wproj': jax.random.normal(ks[2], (C, C), dtype=jnp.float32) * s, 'bproj': jnp.zeros((C,), dtype=jnp.float32), 'ln_g': jnp.ones((C,), dtype=jnp.float32), 'ln_b': jnp.zeros((C,), dtype=jnp.float32), 'Wg1': jax.random.normal(ks[3], (C, GH), dtype=jnp.float32) * s, 'bg1': jnp.zeros((GH,), dtype=jnp.float32), 'Wg2': jax.random.normal(ks[4], (GH, C), dtype=jnp.float32) * s, 'bg2': jnp.zeros((C,), dtype=jnp.float32)}
    _L1_attn_all = _L1_attn_setup()
    _L1_attn_in = {k: v for k, v in _L1_attn_all.items() if k in ('Wqkv', 'Wproj', 'bproj', 'ln_g', 'ln_b', 'Wg1', 'bg1', 'Wg2', 'bg2')}
    del _L1_attn_all

    def _L1_ffn_setup():
        import jax, jax.numpy as jnp
        import numpy as np
        DIM = 64
        HEADS = 8
        NUM_KEYS = 64
        NUM_KV = NUM_KEYS ** 2
        PK_TOPK = 16
        FINAL_TOPK = 16
        DIM_KEY = DIM // 2
        P = 2

        def _pk(x, Wq_pk, pk_keys):
            b, n, _ = x.shape
            q = (x @ Wq_pk).reshape(b, n, P, HEADS, DIM_KEY).transpose(2, 0, 1, 3, 4)
            sim = jnp.einsum('pbnhd,pkhd->pbnhk', q, pk_keys)
            scores, idx = jax.lax.top_k(sim, PK_TOPK)
            idx0 = idx[0]
            idx1 = idx[1] * NUM_KEYS
            index = (idx0[..., :, None] + idx1[..., None, :]).reshape(b, n, HEADS, PK_TOPK * PK_TOPK)
            score = (scores[0][..., :, None] + scores[1][..., None, :]).reshape(b, n, HEADS, PK_TOPK * PK_TOPK)
            final_scores, pk_idx = jax.lax.top_k(score, FINAL_TOPK)
            final_indices = jnp.take_along_axis(index, pk_idx, axis=-1)
            final_scores = jax.nn.softmax(final_scores, axis=-1)
            return (final_scores, final_indices)
        key = jax.random.key(seed)
        ks = jax.random.split(key, 7)
        b, n = (2, 256)
        std = 0.02
        x = jax.random.normal(ks[0], (b, n, DIM), dtype=jnp.float32)
        Wq_pk = jax.random.normal(ks[1], (DIM, P * HEADS * DIM_KEY), dtype=jnp.float32) * std
        pk_keys = jax.random.normal(ks[2], (P, NUM_KEYS, HEADS, DIM_KEY), dtype=jnp.float32) * std
        Wq = jax.random.normal(ks[3], (DIM, HEADS * DIM), dtype=jnp.float32) * std
        keys_table = jax.random.normal(ks[4], (NUM_KV * HEADS, DIM), dtype=jnp.float32) * std
        values_table = jax.random.normal(ks[5], (NUM_KV * HEADS, DIM), dtype=jnp.float32) * std
        Wo = jax.random.normal(ks[6], (DIM * HEADS, DIM), dtype=jnp.float32) * std
        return {'x': x, 'Wq_pk': Wq_pk, 'pk_keys': pk_keys, 'Wq': Wq, 'keys_table': keys_table, 'values_table': values_table, 'Wo': Wo}
    _L1_ffn_all = _L1_ffn_setup()
    _L1_ffn_in = {k: v for k, v in _L1_ffn_all.items() if k in ('Wq_pk', 'pk_keys', 'Wq', 'keys_table', 'values_table', 'Wo')}
    del _L1_ffn_all
    return {'x': x, 'cls_tok': cls_tok, 'L0_tok_W': _L0_tok_in['W'], 'L0_tok_b': _L0_tok_in['b'], 'L0_attn_wq': _L0_attn_in['wq'], 'L0_attn_wkv': _L0_attn_in['wkv'], 'L0_attn_wo': _L0_attn_in['wo'], 'L0_attn_q_norm_w': _L0_attn_in['q_norm_w'], 'L0_attn_k_norm_w': _L0_attn_in['k_norm_w'], 'L0_ffn_Wr': _L0_ffn_in['Wr'], 'L0_ffn_W1s': _L0_ffn_in['W1s'], 'L0_ffn_b1s': _L0_ffn_in['b1s'], 'L0_ffn_W2s': _L0_ffn_in['W2s'], 'L0_ffn_b2s': _L0_ffn_in['b2s'], 'L0_ffn_W1p': _L0_ffn_in['W1p'], 'L0_ffn_b1p': _L0_ffn_in['b1p'], 'L0_ffn_W2p': _L0_ffn_in['W2p'], 'L0_ffn_b2p': _L0_ffn_in['b2p'], 'L1_attn_Wqkv': _L1_attn_in['Wqkv'], 'L1_attn_Wproj': _L1_attn_in['Wproj'], 'L1_attn_bproj': _L1_attn_in['bproj'], 'L1_attn_ln_g': _L1_attn_in['ln_g'], 'L1_attn_ln_b': _L1_attn_in['ln_b'], 'L1_attn_Wg1': _L1_attn_in['Wg1'], 'L1_attn_bg1': _L1_attn_in['bg1'], 'L1_attn_Wg2': _L1_attn_in['Wg2'], 'L1_attn_bg2': _L1_attn_in['bg2'], 'L1_ffn_Wq_pk': _L1_ffn_in['Wq_pk'], 'L1_ffn_pk_keys': _L1_ffn_in['pk_keys'], 'L1_ffn_Wq': _L1_ffn_in['Wq'], 'L1_ffn_keys_table': _L1_ffn_in['keys_table'], 'L1_ffn_values_table': _L1_ffn_in['values_table'], 'L1_ffn_Wo': _L1_ffn_in['Wo']}

def reference(x, cls_tok, L0_tok_W, L0_tok_b, L0_attn_wq, L0_attn_wkv, L0_attn_wo, L0_attn_q_norm_w, L0_attn_k_norm_w, L0_ffn_Wr, L0_ffn_W1s, L0_ffn_b1s, L0_ffn_W2s, L0_ffn_b2s, L0_ffn_W1p, L0_ffn_b1p, L0_ffn_W2p, L0_ffn_b2p, L1_attn_Wqkv, L1_attn_Wproj, L1_attn_bproj, L1_attn_ln_g, L1_attn_ln_b, L1_attn_Wg1, L1_attn_bg1, L1_attn_Wg2, L1_attn_bg2, L1_ffn_Wq_pk, L1_ffn_pk_keys, L1_ffn_Wq, L1_ffn_keys_table, L1_ffn_values_table, L1_ffn_Wo):
    import jax
    import jax.numpy as jnp

    def _L0_tok_ref(x, W, b):
        import jax, jax.numpy as jnp
        import numpy as np
        PATCH = 16
        B, C, H, Wd = x.shape
        p = PATCH
        nH, nW = (H // p, Wd // p)
        patches = x.reshape(B, C, nH, p, nW, p)
        patches = patches.transpose(0, 2, 4, 1, 3, 5)
        patches = patches.reshape(B, nH * nW, C * p * p)
        return jnp.einsum('bnk,ek->bne', patches, W) + b

    def _L0_attn_ref(x, wq, wkv, wo, q_norm_w, k_norm_w):
        import jax, jax.numpy as jnp
        import numpy as np
        import math
        B, T, D_MODEL = (1, 512, 64)
        N_Q, N_KV = (16, 1)
        D_HEAD = D_MODEL // N_KV
        QPG = N_Q // N_KV
        ROPE_BASE = 10000.0
        WINDOW = 128
        EPS = 1.1920929e-07
        NEG = -1e+30

        def _rope(x, base=ROPE_BASE):
            t, d = (x.shape[-2], x.shape[-1])
            freqs = base ** (-2.0 * jnp.arange(d // 2, dtype=jnp.float32) / d)
            theta = jnp.arange(t, dtype=jnp.float32)[:, None] * freqs[None, :]
            cos, sin = (jnp.cos(theta), jnp.sin(theta))
            x1, x2 = (x[..., 0::2], x[..., 1::2])
            r1 = x1 * cos - x2 * sin
            r2 = x1 * sin + x2 * cos
            return jnp.stack([r1, r2], axis=-1).reshape(x.shape)

        def _rmsnorm(x, w):
            return x * jax.lax.rsqrt(jnp.mean(x * x, axis=-1, keepdims=True) + EPS) * w
        Bx, Tx, C = x.shape
        q = x @ wq.T
        kv = x @ wkv.T
        k, v = (kv[..., :N_KV * D_HEAD], kv[..., N_KV * D_HEAD:])
        q = q.reshape(Bx, Tx, QPG, N_KV, D_HEAD).transpose(0, 2, 3, 1, 4)
        k = k.reshape(Bx, Tx, 1, N_KV, D_HEAD).transpose(0, 2, 3, 1, 4)
        v = v.reshape(Bx, Tx, 1, N_KV, D_HEAD).transpose(0, 2, 3, 1, 4)
        q = _rmsnorm(_rope(q), q_norm_w)
        k = _rmsnorm(_rope(k), k_norm_w)
        rows = jnp.arange(Tx)[:, None]
        cols = jnp.arange(Tx)[None, :]
        mask = (cols <= rows) & (rows - cols <= WINDOW)
        scale = 1.0 / math.sqrt(D_HEAD)
        scores = jnp.einsum('bqgtd,bqgsd->bqgts', q, k) * scale
        scores = jnp.where(mask[None, None, None], scores, NEG)
        attn = jax.nn.softmax(scores, axis=-1)
        out = jnp.einsum('bqgts,bqgsd->bqgtd', attn, v)
        out = out.transpose(0, 3, 1, 2, 4).reshape(Bx, Tx, QPG * N_KV * D_HEAD)
        return out @ wo.T

    def _L0_ffn_ref(x, Wr, W1s, b1s, W2s, b2s, W1p, b1p, W2p, b2p):
        import jax, jax.numpy as jnp
        import numpy as np
        B, S, D, F, E, K = (8, 512, 64, 256, 8, 2)
        gelu = lambda t: jax.nn.gelu(t, approximate=False)
        shared = gelu(x @ W1s + b1s) @ W2s + b2s
        rw = jax.nn.softmax(x @ Wr, axis=-1)
        topw, topi = jax.lax.top_k(rw, K)
        topw = topw / jnp.sum(topw, axis=-1, keepdims=True)
        mask = jnp.sum(jax.nn.one_hot(topi, E, dtype=topw.dtype) * topw[..., None], axis=-2)
        h = gelu(jnp.einsum('bsd,edf->bsef', x, W1p) + b1p)
        priv = jnp.einsum('bsef,efd->bsed', h, W2p) + b2p
        routed = jnp.einsum('bsed,bse->bsd', priv, mask)
        return shared + routed

    def _L1_attn_ref(x, Wqkv, Wproj, bproj, ln_g, ln_b, Wg1, bg1, Wg2, bg2):
        import jax, jax.numpy as jnp
        import numpy as np
        B, N, C, H = (8, 4096, 64, 8)
        D = C // H
        GH = C // 4
        b, n, c = x.shape
        h, d = (H, D)
        qkv = (x @ Wqkv).reshape(b, n, 3, h, d)
        q, k, v = (qkv[:, :, 0], qkv[:, :, 1], qkv[:, :, 2])
        k = jax.nn.softmax(k, axis=1)
        context = jnp.einsum('bnhd,bnhv->bhdv', k, v)
        out = jnp.einsum('bnhd,bhdv->bnhv', q, context).reshape(b, n, c)
        mu = jnp.mean(x, axis=-1, keepdims=True)
        var = jnp.var(x, axis=-1, keepdims=True)
        xn = (x - mu) * jax.lax.rsqrt(var + 1e-05) * ln_g + ln_b
        hgate = jax.nn.gelu(xn @ Wg1 + bg1, approximate=False)
        gate = jax.nn.sigmoid(hgate @ Wg2 + bg2)
        return out * gate @ Wproj + bproj

    def _L1_ffn_ref(x, Wq_pk, pk_keys, Wq, keys_table, values_table, Wo):
        import jax, jax.numpy as jnp
        import numpy as np
        DIM = 64
        HEADS = 8
        NUM_KEYS = 64
        NUM_KV = NUM_KEYS ** 2
        PK_TOPK = 16
        FINAL_TOPK = 16
        DIM_KEY = DIM // 2
        P = 2

        def _pk(x, Wq_pk, pk_keys):
            b, n, _ = x.shape
            q = (x @ Wq_pk).reshape(b, n, P, HEADS, DIM_KEY).transpose(2, 0, 1, 3, 4)
            sim = jnp.einsum('pbnhd,pkhd->pbnhk', q, pk_keys)
            scores, idx = jax.lax.top_k(sim, PK_TOPK)
            idx0 = idx[0]
            idx1 = idx[1] * NUM_KEYS
            index = (idx0[..., :, None] + idx1[..., None, :]).reshape(b, n, HEADS, PK_TOPK * PK_TOPK)
            score = (scores[0][..., :, None] + scores[1][..., None, :]).reshape(b, n, HEADS, PK_TOPK * PK_TOPK)
            final_scores, pk_idx = jax.lax.top_k(score, FINAL_TOPK)
            final_indices = jnp.take_along_axis(index, pk_idx, axis=-1)
            final_scores = jax.nn.softmax(final_scores, axis=-1)
            return (final_scores, final_indices)
        b, n, d = x.shape
        q = (x @ Wq).reshape(b, n, HEADS, DIM) * DIM ** (-0.5)
        kv_scores, indices = _pk(x, Wq_pk, pk_keys)
        offsets = jnp.arange(HEADS, dtype=indices.dtype) * NUM_KV
        ind = indices + offsets[None, None, :, None]
        k = jnp.einsum('bnhk,bnhkd->bnhd', kv_scores, keys_table[ind])
        v = jnp.einsum('bnhk,bnhkd->bnhd', kv_scores, values_table[ind])
        sim = jnp.einsum('bihd,bjhd->bhij', q, k)
        neg = -jnp.finfo(sim.dtype).max
        causal = jnp.tril(jnp.ones((n, n), dtype=bool))
        sim = jnp.where(causal, sim, neg)
        attn = jax.nn.softmax(sim, axis=-1)
        out = jnp.einsum('bhij,bjhd->bhid', attn, v)
        out = out.transpose(0, 2, 1, 3).reshape(b, n, HEADS * DIM)
        return out @ Wo
    h = _L0_tok_ref(x, L0_tok_W, L0_tok_b)
    h = jnp.concatenate([jnp.broadcast_to(cls_tok, (h.shape[0], 1, h.shape[2])), h], axis=1)
    h = h + _L0_attn_ref(_layernorm(h, axis=-1), L0_attn_wq, L0_attn_wkv, L0_attn_wo, L0_attn_q_norm_w, L0_attn_k_norm_w)
    h = h + _L0_ffn_ref(_layernorm(h, axis=-1), L0_ffn_Wr, L0_ffn_W1s, L0_ffn_b1s, L0_ffn_W2s, L0_ffn_b2s, L0_ffn_W1p, L0_ffn_b1p, L0_ffn_W2p, L0_ffn_b2p)
    h = h + _L1_attn_ref(_layernorm(h, axis=-1), L1_attn_Wqkv, L1_attn_Wproj, L1_attn_bproj, L1_attn_ln_g, L1_attn_ln_b, L1_attn_Wg1, L1_attn_bg1, L1_attn_Wg2, L1_attn_bg2)
    h = h + _L1_ffn_ref(_layernorm(h, axis=-1), L1_ffn_Wq_pk, L1_ffn_pk_keys, L1_ffn_Wq, L1_ffn_keys_table, L1_ffn_values_table, L1_ffn_Wo)
    return h

_drawn_inputs = setup_inputs


def setup_inputs(seed=0):
    import zlib

    import numpy as np

    out = dict(_drawn_inputs(seed))
    spreads = {'L0_attn_q_norm_w': (1.0, 0.6),
     'L0_attn_k_norm_w': (1.0, 0.6),
     'L0_ffn_b1s': (0.0, 0.478),
     'L0_ffn_b2s': (0.0, 0.1),
     'L0_ffn_b1p': (0.0, 0.681),
     'L0_ffn_b2p': (0.0, 0.1),
     'L1_attn_bproj': (0.0, 0.1),
     'L1_attn_ln_g': (1.0, 0.6),
     'L1_attn_ln_b': (0.0, 0.8),
     'L1_attn_bg1': (0.0, 0.8),
     'L1_attn_bg2': (0.0, 0.8)}
    factors = {'cls_tok': 4.352,
     'L0_tok_b': 4.588,
     'L0_attn_wq': 2.681,
     'L0_ffn_W1p': 3.044,
     'L1_attn_Wqkv': 8.0,
     'L1_attn_Wproj': 8.0,
     'L1_attn_Wg1': 8.0,
     'L1_attn_Wg2': 8.0,
     'L1_ffn_Wq_pk': 8.0,
     'L1_ffn_pk_keys': 8.0,
     'L1_ffn_Wq': 64.0,
     'L1_ffn_keys_table': 64.0,
     'L1_ffn_values_table': 8.0,
     'L1_ffn_Wo': 8.0}
    for name, (base, spread) in spreads.items():
        noise = np.random.default_rng([zlib.crc32(name.encode()), seed]).standard_normal(out[name].shape)
        drawn = base * np.exp(spread * noise) if base else spread * noise
        out[name] = jnp.asarray(drawn.astype(out[name].dtype))
    for name, factor in factors.items():
        out[name] = (out[name] * factor).astype(out[name].dtype)
    return out
```

```python
from contextlib import ExitStack

import concourse.bass as bass
from concourse import mybir

F32 = mybir.dt.float32
BF16 = mybir.dt.bfloat16
U32 = mybir.dt.uint32
ALU = mybir.AluOpType
ACT = mybir.ActivationFunctionType
AX = mybir.AxisListType

B, CH, IMG, PATCH, D = 64, 3, 224, 16, 64
N = (IMG // PATCH) ** 2 + 1
TT = (N + 1) // 2
NP = 2 * TT
KC = CH * PATCH * PATCH // 128
HQ = 16
WINDOW = 128
NE, FF = 8, 256
GH = D // 4
HV, NK, TOPK = 8, 64, 16
CUTS = [TOPK // (r + 1) for r in range(TOPK)]
NC = sum(CUTS)
TILE = 128
NTILES = (B * N + TILE - 1) // TILE
ROWS = NTILES * TILE
LN_EPS = 1e-5
RMS_EPS = 1.1920929e-07
NEG = -1e30
LOWEST = -3.0e38
EXP_LN = "natural_log_exp_and_others"


def wait_apart(eng, sem, value, met):
    value = value if isinstance(value, int) else eng.to_reg(value)
    eng.wait_ge(*met)
    eng.wait_ge(sem, value)


class Chain:

    def __init__(self, eng, sem, trip, per_trip):
        self.eng, self.sem, self.base, self.per_trip, self.n = eng, sem, trip * per_trip, per_trip, 0

    def step(self, ins):
        ins.then_inc(self.sem, 1)
        self.n += 1

    def wait(self, met=None):
        if met:
            wait_apart(self.eng, self.sem, self.base + self.n, met)
        else:
            self.eng.wait_ge(self.sem, self.base + self.n)

    def link(self, ins):
        self.step(ins)
        self.wait()

    def close(self):
        assert self.n == self.per_trip, (self.n, self.per_trip)


def bcast(ap, axis, shape):
    return ap.unsqueeze(axis).to_broadcast(shape)


A_STEPS = 126
A_ACT_STEPS = 14


def image_phase(nc, c, h3_rows, xn4_rows):
    QG = HQ // 4
    UNITS = QG + HQ // 2
    W = 4 * TT
    with ExitStack() as ctx:
        def sb(name, shape, dt=F32):
            return ctx.enter_context(nc.sbuf_tensor(name, shape, dt))

        def sem(name):
            return ctx.enter_context(nc.semaphore(name))

        def two(name, shape, dt=F32):
            return [sb(f"{name}{u}", shape, dt) for u in range(2)]

        shapes = dict(patch_w=[128, KC, D], embed_add=[TT, 2, D], ident=[128, 128], wqq=[D, HQ, 2 * D], wkkv=[D, 3 * D],
                      rope_q=[2 * D, NP], rope_k=[TT, 2, 2 * D], wo=[128, HQ * D // 128, D], wr=[D, NE], w1=[D, NE + 1, FF],
                      b1=[128, NE + 1, 2], w2=[128, NE + 1, 2, D], b2p=[TT, NE, D], b2s=[TT, D], iota8=[TT, NE],
                      wqkv=[D, 3 * D], wproj=[D, D], bproj=[TT, D], lng=[D, 1], lnb=[D, 1], wg1=[D, GH], bg1=[GH, 1],
                      wg2=[GH, D], bg2=[TT, D], blocks=[D, D], qnw=[TT, D], knw=[TT, D])
        k = {n: sb("c_" + n, s) for n, s in shapes.items()}
        mask = [sb(f"c_mask{t}", [TT, W], BF16) for t in range(2)]
        ident_b = sb("c_ident_b", [128, 128], BF16)
        knq = sb("knq", [TT, D])
        ones = sb("ones", [D, 1])
        eps_ln, eps_rms = sb("eps_ln", [TT, 1]), sb("eps_rms", [TT, 1])
        pix = two("pix", [128, KC, NP])
        h = two("h", [TT, 2, D])
        stats = two("stats", [TT, 2, 6])
        mv = two("mv", [TT, 2, 2])
        logs = two("logs", [TT, 2 * HQ])
        rstd = two("rstd", [TT, 2])
        xn = two("xn", [TT, 2, D])
        xT = two("xT", [D, NP])
        kk = two("kk", [TT, 2, 2 * D])
        kr = two("kr", [TT, 2, D])
        ksq = two("ksq", [TT, 2, D])
        kss = two("kss", [TT, 2])
        krs = two("krs", [TT, 2])
        kdup = two("kdup", [TT, 2, 2, D])
        kT = two("kT", [2 * D, NP])
        v = two("v", [TT, 2, D])
        qr = two("qr", [2 * D, HQ, NP])
        qsq_OT = two("qsq_OT", [128, HQ * NP])
        qsq = [b[0:D, :].rearrange("p (h t) -> p h t", h=HQ) for b in qsq_OT]
        OT = [b[:, 0:4 * W].rearrange("p (n w) -> p n w", n=4) for b in qsq_OT]
        rq = two("rq", [TT, 2, HQ])
        m = two("m", [TT, 2, HQ])
        nb = two("nb", [TT, 2, HQ])
        den = two("den", [TT, 2, HQ])
        rden = two("rden", [TT, 2, HQ])
        P_hid = two("P_hid", [128, UNITS * W])
        P = [b[0:TT, :].rearrange("p (n w) -> p n w", n=UNITS) for b in P_hid]
        hid = [b[:, 0:(NE + 1) * 2 * NP].rearrange("p (e f t) -> p e f t", e=NE + 1, f=2) for b in P_hid]
        PT = [[sb(f"PT{u}_{s}", [TT, W]) for s in range(2)] for u in range(2)]
        O = two("O", [TT, 2, HQ, D])
        lg = two("lg", [TT, 2, NE])
        lmax = two("lmax", [TT, 2])
        el = two("el", [TT, 2, NE])
        top = two("top", [TT, 2, 8])
        topi = two("topi", [TT, 2, 8], U32)
        topf = two("topf", [TT, 2, 2])
        tsum = two("tsum", [TT, 2])
        trec = two("trec", [TT, 2])
        tw = two("tw", [TT, 2, 2])
        oh = two("oh", [TT, 2, 2, NE])
        gate = two("gate", [TT, 2, NE])
        mo = two("mo", [TT, 2, NE, D])
        mr = two("mr", [TT, 2, D])
        qT = two("qT", [D, NP])
        kmx = two("kmx", [D, 1])
        ksum = two("ksum", [D, 1])
        krec = two("krec", [D, 1])
        eT = two("eT", [D, NP])
        ek = two("ek", [TT, 2, D])
        ctxs = two("ctxs", [D, D])
        xgT = two("xgT", [D, NP])
        hg = two("hg", [GH, NP])
        g = two("g", [TT, 2, D])
        ps = [[ctx.enter_context(nc.psum_tensor(f"psa{u}_{s}", [128, 512], F32)) for s in range(4)] for u in range(2)]

        SETUP = 9
        consts_in, setup = sem("a_consts_in"), sem("a_setup")
        pix_in = [sem(f"pix_in{u}") for u in range(2)]
        rows_out = [sem(f"rows_out{u}") for u in range(2)]
        vstep = sem("a_vector_step")
        astep = sem("a_scalar_step")
        met = (consts_in, 16 * (len(shapes) + 2))
        S = {}
        NAMES = """emb_sum var1 rstd1 xn1 xT1_ps xT1 kv_ps kss krs kdup kT_ps kT q_ps q_rot q_sq qss rq s_ps nb p_ready
                   pt_ps pt_ready o_ps o_ready oT_ps oT_ready wo_ps var2 rstd2 xn2 xT2_ps xT2 lg_ps lmax el hid_ps hid_ready
                   moe_ps var3 rstd3 xn3 xT3_ps xT3 qkv_ps kmx ek_ready ek_ps ek lin_v ctx_ps ctx lin_ps var5 rstd5 xg xgT_ps xgT
                   hg_ps hg g_ps g_in g_exp og ogT_ps ogT proj_ps var4 rstd4 xn4""".split()
        for s in NAMES:
            S[s] = sem("a_" + s)

        def tok(t):
            return slice(t * TT, (t + 1) * TT)

        def unit_heads(n):
            return (0, 4 * n, 4) if n < QG else (1, 2 * (n - QG), 2)

        with nc.Block() as block:
            @block.sync
            def _(sp):
                for name in shapes:
                    sp.dma_start(k[name][:], c[name]).then_inc(consts_in, 16)
                for t in range(2):
                    sp.dma_start(P[0][:, t, :], c["mask"][t]).then_inc(consts_in, 16)
                with sp.Fori(0, B // 2) as i:
                    for u in range(2):
                        sp.wait_ge(S["emb_sum"], i * 2)
                        sp.dma_start(pix[u][:], c["pixT"][bass.ds(2 * i + u, 1)].rearrange("o p k t -> (o p) k t")).then_inc(pix_in[u], 16)
                    for u in range(2):
                        sp.wait_ge(S["xn4"], i * 2 + u + 1)
                        for src, dst in ((h[u], h3_rows), (xn[u], xn4_rows)):
                            for t, rows in ((0, TT), (1, N - TT)):
                                sp.dma_start(dst[bass.ds((2 * i + u) * N + t * TT, rows), :], src[0:rows, t, :]).then_inc(rows_out[u], 16)
                for u in range(2):
                    sp.wait_ge(rows_out[u], 64 * (B // 2))

            @block.tensor
            def _(pe):
                pe.wait_ge(consts_in, 16 * (len(shapes) + 2))
                pe.wait_ge(setup, SETUP)

                def done(mm, name):
                    mm.then_inc(S[name], 1)

                with pe.Fori(0, B // 2) as i:
                    def need(name, u, per=1, n=0, met=None):
                        if met:
                            wait_apart(pe, S[name], i * 2 * per + 2 * n + u + 1, met)
                        else:
                            pe.wait_ge(S[name], i * 2 * per + 2 * n + u + 1)

                    def turn(src, name, ready, bank, u, out=None, ident=None):
                        need(ready, u, met=met)
                        for t in range(2):
                            mm = nc.tensor.transpose(ps[u][bank][0:D, tok(t)], src[u][:, t, :], k["ident"][0:TT, 0:TT])
                        done(mm, name)

                    for u in range(2):
                        pe.wait_ge(pix_in[u], (i + 1) * 16)
                        pe.wait_ge(S["xn4"], i * 2 + 0 if u == 0 else i * 2)
                        for t in range(2):
                            for kc in range(KC):
                                mm = nc.tensor.matmul(ps[u][0][0:TT, t * D:(t + 1) * D], pix[u][:, kc, tok(t)], k["patch_w"][:, kc, :],
                                                      start=(kc == 0), stop=(kc == KC - 1))
                        done(mm, "emb_sum")
                    for u in range(2):
                        turn(xn, "xT1_ps", "xn1", 1, u)
                    for u in range(2):
                        need("xT1", u)
                        for t in range(2):
                            mm = nc.tensor.matmul(ps[u][0][0:TT, t * 3 * D:(t + 1) * 3 * D], xT[u][:, tok(t)], k["wkkv"][:], start=True, stop=True)
                        done(mm, "kv_ps")
                    for n in range(HQ // 2):
                        for u in range(2):
                            if n >= 2:
                                need("q_sq", u, HQ // 2, n - 2)
                            for a in range(2):
                                mm = nc.tensor.matmul(ps[u][2 + n % 2][:, a * NP:(a + 1) * NP], k["wqq"][:, 2 * n + a, :], xT[u][:], start=True, stop=True)
                            done(mm, "q_ps")
                    for u in range(2):
                        need("kdup", u)
                        for t in range(2):
                            mm = nc.tensor.transpose(ps[u][1][:, tok(t)], kdup[u][:, t].rearrange("p a d -> p (a d)"), k["ident"][0:TT, 0:TT])
                        done(mm, "kT_ps")
                    for u in range(2):
                        need("q_sq", u, HQ // 2, HQ // 2 - 1)
                        for t in range(2):
                            for hh in range(HQ):
                                mm = nc.tensor.matmul(ps[u][0][0:TT, t * HQ + hh:t * HQ + hh + 1], qsq[u][:, hh, tok(t)], ones[:], start=True, stop=True)
                        done(mm, "qss")

                    def scores(n, u):
                        t, h0, nh = unit_heads(n)
                        if n == 0:
                            need("kT", u)
                            need("q_rot", u, HQ // 2, HQ // 2 - 1)
                        if n >= 2:
                            need("p_ready", u, UNITS, n - 2)
                        bank = ps[u][2 + n % 2]
                        nc.tensor.matmul(bank[0:TT, 0:W], ident_b[0:TT, 0:TT], mask[t][:], start=True, stop=False)
                        w = (t + 1) * TT
                        for a in range(nh):
                            mm = nc.tensor.matmul(bank[0:TT, a * w:(a + 1) * w], qr[u][:, h0 + a, tok(t)], kT[u][:, 0:w], start=False, stop=(a == nh - 1))
                        done(mm, "s_ps")

                    def turn_p(n, u):
                        need("p_ready", u, UNITS, n)
                        if n >= 1:
                            need("pt_ready", u, UNITS, n - 1)
                        else:
                            need("rq", u)
                        for a in range(4):
                            mm = nc.tensor.transpose(ps[u][0][0:TT, a * TT:(a + 1) * TT], P[u][:, n, a * TT:(a + 1) * TT], k["ident"][0:TT, 0:TT])
                        done(mm, "pt_ps")

                    def values(n, u):
                        t, h0, nh = unit_heads(n)
                        need("pt_ready", u, UNITS, n)
                        if h0 % 8 == 0 and n:
                            need("o_ready", u, 4, t * 2 + h0 // 8 - 1)
                        if n == 0:
                            need("kT", u)
                        for a in range(nh):
                            o = ps[u][1][0:TT, (h0 + a) % 8 * D:((h0 + a) % 8 + 1) * D]
                            for s in range(t + 1):
                                col = (a * (t + 1) + s) * TT
                                mm = nc.tensor.matmul(o, PT[u][n % 2][:, col:col + TT], v[u][:, s, :], start=(s == 0), stop=(s == t))
                        done(mm, "o_ps")

                    for n in range(UNITS + 2):
                        for u in range(2):
                            if n < UNITS:
                                scores(n, u)
                        for u in range(2):
                            if 1 <= n <= UNITS:
                                turn_p(n - 1, u)
                        for u in range(2):
                            if n >= 2:
                                values(n - 2, u)
                    for n in range(4):
                        for u in range(2):
                            if n % 2 == 0:
                                need("o_ready", u, 4, 1 + n)
                            if n >= 2:
                                need("oT_ready", u, 4, n - 2)
                            flat = O[u][:, n // 2].rearrange("p h d -> p (h d)")
                            for a in range(4):
                                ch = (n % 2) * 4 + a
                                mm = nc.tensor.transpose(ps[u][2 + n % 2][:, a * TT:(a + 1) * TT], flat[:, ch * 128:(ch + 1) * 128], k["ident"][0:TT, 0:TT])
                            done(mm, "oT_ps")
                    for u in range(2):
                        need("oT_ready", u, 4, 3)
                        for t in range(2):
                            for ch in range(8):
                                mm = nc.tensor.matmul(ps[u][0][0:TT, t * D:(t + 1) * D], OT[u][:, 2 * t + ch // 4, (ch % 4) * TT:(ch % 4 + 1) * TT],
                                                      k["wo"][:, ch, :], start=(ch == 0), stop=(ch == 7))
                        done(mm, "wo_ps")
                    for u in range(2):
                        turn(xn, "xT2_ps", "xn2", 1, u)
                    for u in range(2):
                        need("xT2", u)
                        for t in range(2):
                            mm = nc.tensor.matmul(ps[u][0][0:TT, t * NE:(t + 1) * NE], xT[u][:, tok(t)], k["wr"][:], start=True, stop=True)
                        done(mm, "lg_ps")
                    for e in range(NE + 1):
                        for u in range(2):
                            if e >= 2:
                                need("hid_ready", u, NE + 1, e - 2)
                            for f in range(2):
                                mm = nc.tensor.matmul(ps[u][2 + e % 2][:, f * NP:(f + 1) * NP], k["w1"][:, e, f * 128:(f + 1) * 128], xT[u][:], start=True, stop=True)
                            done(mm, "hid_ps")
                    for u in range(2):
                        need("hid_ready", u, NE + 1, NE)
                        for t in range(2):
                            for e in range(NE + 1):
                                out = ps[u][2 + t][0:TT, e * D:(e + 1) * D] if e < NE else ps[u][1][0:TT, t * D:(t + 1) * D]
                                for f in range(2):
                                    mm = nc.tensor.matmul(out, hid[u][:, e, f, tok(t)], k["w2"][:, e, f, :], start=(f == 0), stop=(f == 1))
                        done(mm, "moe_ps")
                    for u in range(2):
                        turn(xn, "xT3_ps", "xn3", 0, u)
                    for u in range(2):
                        need("xT3", u, met=met)
                        for a in range(2):
                            nc.tensor.matmul(ps[u][1][0:D, a * NP:(a + 1) * NP], k["wqkv"][:, a * D:(a + 1) * D], xT[u][:], start=True, stop=True)
                        for t in range(2):
                            mm = nc.tensor.matmul(ps[u][2][0:TT, t * D:(t + 1) * D], xT[u][:, tok(t)], k["wqkv"][:, 2 * D:3 * D], start=True, stop=True)
                        done(mm, "qkv_ps")
                    for u in range(2):
                        turn(g, "xgT_ps", "xg", 0, u)
                    for u in range(2):
                        need("xgT", u, met=met)
                        done(nc.tensor.matmul(ps[u][3][0:GH, 0:NP], k["wg1"][:], xgT[u][:], start=True, stop=True), "hg_ps")
                    for u in range(2):
                        need("ek_ready", u, met=met)
                        need("lin_v", u, met=met)
                        for t in range(2):
                            mm = nc.tensor.transpose(ps[u][2][0:TT, t * D:(t + 1) * D], eT[u][:, tok(t)], k["ident"][0:D, 0:D])
                        done(mm, "ek_ps")
                    for u in range(2):
                        need("ek", u)
                        for t in range(2):
                            mm = nc.tensor.matmul(ps[u][0][0:D, 0:D], ek[u][:, t, :], v[u][:, t, :], start=(t == 0), stop=(t == 1))
                        done(mm, "ctx_ps")
                    for u in range(2):
                        need("ctx", u)
                        for t in range(2):
                            mm = nc.tensor.matmul(ps[u][1][0:TT, t * D:(t + 1) * D], qT[u][:, tok(t)], ctxs[u][:], start=True, stop=True)
                        done(mm, "lin_ps")
                    for u in range(2):
                        need("hg", u)
                        for t in range(2):
                            mm = nc.tensor.matmul(ps[u][2][0:TT, t * D:(t + 1) * D], hg[u][:, tok(t)], k["wg2"][:], start=True, stop=True)
                        done(mm, "g_ps")
                    for u in range(2):
                        turn(g, "ogT_ps", "og", 3, u)
                    for u in range(2):
                        need("ogT", u)
                        for t in range(2):
                            mm = nc.tensor.matmul(ps[u][2][0:TT, t * D:(t + 1) * D], xgT[u][:, tok(t)], k["wproj"][:], start=True, stop=True)
                        done(mm, "proj_ps")

            @block.scalar
            def _(act):
                act.wait_ge(consts_in, 16 * (len(shapes) + 2))
                act.wait_ge(setup, SETUP)
                act.preload_act_table_set(EXP_LN)
                with act.Fori(0, B // 2) as i:
                    own = Chain(act, astep, i, A_ACT_STEPS)

                    def need(name, u, per=1, n=0, met=None):
                        if met:
                            wait_apart(act, S[name], i * 2 * per + 2 * n + u + 1, met)
                        else:
                            act.wait_ge(S[name], i * 2 * per + 2 * n + u + 1)

                    def inv_root(src, dst, name, ready, u, scale, bias):
                        need(ready, u)
                        tmp = logs[u][:, 0:src.free_size()]
                        own.link(nc.scalar.activation(tmp, src, ACT.Ln, scale=scale, bias=bias[:, 0:1]))
                        nc.scalar.activation(dst, tmp, ACT.Exp, scale=-0.5).then_inc(S[name], 1)

                    def ln_root(j, u):
                        inv_root(mv[u][:, :, 1], rstd[u][:], f"rstd{j}", f"var{j}", u, 1.0, eps_ln)

                    for u in range(2):
                        ln_root(1, u)
                    for u in range(2):
                        inv_root(kss[u][:], krs[u][:], "krs", "kss", u, 1.0 / D, eps_rms)
                    for n in range(HQ // 2):
                        for u in range(2):
                            need("q_rot", u, HQ // 2, n)
                            nc.scalar.activation(qsq[u][:, 2 * n:2 * n + 2, :].rearrange("p a t -> p (a t)"), ps[u][2 + n % 2][0:D, 0:2 * NP], ACT.Square).then_inc(S["q_sq"], 1)
                    for u in range(2):
                        inv_root(ps[u][0][0:TT, 0:2 * HQ], rq[u][:].rearrange("p t h -> p (t h)"), "rq", "qss", u, 1.0 / D, eps_rms)

                    def exps(n, u):
                        t, h0, nh = unit_heads(n)
                        need("nb", u, UNITS, n)
                        need("rq", u)
                        w = (t + 1) * TT
                        for a in range(nh):
                            hh = h0 + a
                            e = nc.scalar.activation(P[u][:, n, a * w:(a + 1) * w], ps[u][2 + n % 2][0:TT, a * w:(a + 1) * w], ACT.Exp,
                                                     scale=rq[u][:, t, hh:hh + 1], bias=nb[u][:, t, hh:hh + 1], accum_out=den[u][:, t, hh:hh + 1])
                        e.then_inc(S["p_ready"], 1)

                    def copy_pt(n, u):
                        need("pt_ps", u, UNITS, n)
                        if n >= 2:
                            need("o_ps", u, UNITS, n - 2)
                        nc.scalar.activation(PT[u][n % 2][:], ps[u][0][0:TT, 0:W], ACT.Copy).then_inc(S["pt_ready"], 1)

                    for n in range(UNITS + 1):
                        for u in range(2):
                            if n < UNITS:
                                exps(n, u)
                        for u in range(2):
                            if n >= 1:
                                copy_pt(n - 1, u)
                    for n in range(4):
                        for u in range(2):
                            need("oT_ps", u, 4, n)
                            nc.scalar.activation(OT[u][:, n, :], ps[u][2 + n % 2][:, 0:W], ACT.Copy).then_inc(S["oT_ready"], 1)
                    for u in range(2):
                        ln_root(2, u)
                    for u in range(2):
                        need("lmax", u)
                        nc.scalar.activation(el[u][:], lg[u][:], ACT.Exp).then_inc(S["el"], 1)
                    for e in range(NE + 1):
                        for u in range(2):
                            need("hid_ps", u, NE + 1, e)
                            for f in range(2):
                                last = nc.scalar.activation(hid[u][:, e, f, :], ps[u][2 + e % 2][:, f * NP:(f + 1) * NP], ACT.Gelu, bias=k["b1"][:, e, f:f + 1])
                            last.then_inc(S["hid_ready"], 1)
                    act.preload_act_table_set(EXP_LN)
                    for u in range(2):
                        ln_root(3, u)
                    for u in range(2):
                        ln_root(5, u)
                    for u in range(2):
                        need("kmx", u)
                        nc.scalar.activation(eT[u][:, 0:N], ps[u][1][0:D, NP:NP + N], ACT.Exp, bias=kmx[u][:, 0:1], accum_out=ksum[u][:, 0:1]).then_inc(S["ek_ready"], 1)
                    for u in range(2):
                        need("hg_ps", u)
                        nc.scalar.activation(hg[u][:], ps[u][3][0:GH, 0:NP], ACT.Gelu, bias=k["bg1"][:, 0:1]).then_inc(S["hg"], 1)
                    act.preload_act_table_set(EXP_LN)
                    for u in range(2):
                        need("g_in", u)
                        nc.scalar.activation(g[u][:], g[u][:], ACT.Exp, scale=-1.0).then_inc(S["g_exp"], 1)
                    for u in range(2):
                        ln_root(4, u)
                    own.close()

            @block.vector
            def _(dve):
                dve.wait_ge(consts_in, 16 * (len(shapes) + 2))
                nc.vector.memset(ones[:], 1.0).then_inc(setup, 1)
                for t in range(2):
                    nc.vector.tensor_copy(mask[t][:], P[0][:, t, :]).then_inc(setup, 1)
                nc.vector.tensor_copy(ident_b[:], k["ident"][:]).then_inc(setup, 1)
                nc.vector.memset(eps_ln[:], LN_EPS).then_inc(setup, 1)
                nc.vector.memset(eps_rms[:], RMS_EPS).then_inc(setup, 1)
                for u in range(2):
                    nc.vector.memset(eT[u][:], 0.0).then_inc(setup, 1)
                nc.vector.scalar_tensor_tensor(out=knq[:], in0=k["qnw"][:], scalar=D ** -0.5, in1=k["knw"][:], op0=ALU.mult, op1=ALU.mult).then_inc(setup, 1)
                dve.wait_ge(setup, SETUP)
                with dve.Fori(0, B // 2) as i:
                    own = Chain(dve, vstep, i, A_STEPS)

                    def need(name, u, per=1, n=0, met=None):
                        if met:
                            wait_apart(dve, S[name], i * 2 * per + 2 * n + u + 1, met)
                        else:
                            dve.wait_ge(S[name], i * 2 * per + 2 * n + u + 1)

                    def ln_stats(src, j, u):
                        for t in range(2):
                            own.step(nc.vector.bn_stats(stats[u][:, t, :], src[:, t, :]))
                        own.wait(met)
                        nc.vector.bn_aggr(mv[u][:, 0, :], stats[u][:, 0, :])
                        nc.vector.bn_aggr(mv[u][:, 1, :], stats[u][:, 1, :]).then_inc(S[f"var{j}"], 1)

                    def ln_apply(src, dst, j, u, ready):
                        need(f"rstd{j}", u)
                        need(f"var{j}", u)
                        nc.vector.tensor_scalar(dst[:, 0, :], src[:, 0, :], mv[u][:, 0, 0:1], rstd[u][:, 0:1], ALU.subtract, ALU.mult)
                        nc.vector.tensor_scalar(dst[:, 1, :], src[:, 1, :], mv[u][:, 1, 0:1], rstd[u][:, 1:2], ALU.subtract, ALU.mult).then_inc(S[ready], 1)

                    def copy_xT(j, bank, u):
                        need(f"xT{j}_ps", u)
                        nc.vector.tensor_copy(xT[u][:], ps[u][bank][0:D, 0:NP]).then_inc(S[f"xT{j}"], 1)

                    for u in range(2):
                        need("emb_sum", u)
                        dve.wait_ge(rows_out[u], i * 64)
                        own.link(nc.vector.tensor_tensor(h[u][:], ps[u][0][0:TT, 0:2 * D].rearrange("p (t d) -> p t d", t=2), k["embed_add"][:], ALU.add))
                        ln_stats(h[u], 1, u)
                    for u in range(2):
                        ln_apply(h[u], xn[u], 1, u, "xn1")
                    for u in range(2):
                        copy_xT(1, 1, u)

                    def rotate_q(n):
                        for u in range(2):
                            need("q_ps", u, HQ // 2, n)
                            nc.vector.tensor_tensor(qr[u][:, 2 * n:2 * n + 2, :], ps[u][2 + n % 2][:, 0:2 * NP].rearrange("p (a t) -> p a t", a=2),
                                                    bcast(k["rope_q"][:], 1, [2 * D, 2, NP]), ALU.mult).then_inc(S["q_rot"], 1)
                    for u in range(2):
                        need("kv_ps", u)
                        kv = ps[u][0][0:TT, 0:6 * D].rearrange("p (t d) -> p t d", t=2)
                        own.step(nc.vector.tensor_tensor(kk[u][:], kv[:, :, 0:2 * D], k["rope_k"][:], ALU.mult))
                        own.link(nc.vector.tensor_copy(v[u][:], kv[:, :, 2 * D:3 * D]))
                        own.link(nc.vector.tensor_tensor(kr[u][:], kk[u][:, :, 0:D], kk[u][:, :, D:2 * D], ALU.add))
                        own.link(nc.vector.tensor_tensor(ksq[u][:], kr[u][:], kr[u][:], ALU.mult))
                        nc.vector.tensor_reduce(kss[u][:], ksq[u][:], AX.X, ALU.add).then_inc(S["kss"], 1)
                    rotate_q(0)
                    rotate_q(1)
                    for u in range(2):
                        need("krs", u)
                        for t in range(2):
                            own.step(nc.vector.tensor_scalar(kr[u][:, t, :], kr[u][:, t, :], krs[u][:, t:t + 1], None, ALU.mult))
                        own.wait()
                        own.step(nc.vector.tensor_tensor(kdup[u][:, :, 0, :], kr[u][:], bcast(knq[:], 1, [TT, 2, D]), ALU.mult))
                        nc.vector.tensor_tensor(kdup[u][:, :, 1, :], kr[u][:], bcast(knq[:], 1, [TT, 2, D]), ALU.mult).then_inc(S["kdup"], 1)
                    for n in range(2, HQ // 2):
                        rotate_q(n)
                    for u in range(2):
                        need("kT_ps", u)
                        nc.vector.tensor_copy(kT[u][:], ps[u][1][:, 0:NP]).then_inc(S["kT"], 1)

                    def unit_max(n, u):
                        t, h0, nh = unit_heads(n)
                        need("s_ps", u, UNITS, n)
                        own.link(nc.vector.tensor_reduce(m[u][:, t, h0:h0 + nh], ps[u][2 + n % 2][0:TT, 0:W].rearrange("p (a s) -> p a s", a=nh), AX.X, ALU.max))
                        if n == 0:
                            need("rq", u)
                        nc.vector.scalar_tensor_tensor(out=nb[u][:, t, h0:h0 + nh], in0=m[u][:, t, h0:h0 + nh], scalar=-1.0, in1=rq[u][:, t, h0:h0 + nh],
                                                       op0=ALU.mult, op1=ALU.mult).then_inc(S["nb"], 1)

                    def scale_o(n, u):
                        t, h0, nh = unit_heads(n)
                        h8 = h0 // 8 * 8
                        need("o_ps", u, UNITS, n)
                        own.link(nc.vector.reciprocal(rden[u][:, t, h8:h8 + 8], den[u][:, t, h8:h8 + 8]))
                        nc.vector.tensor_tensor(O[u][:, t, h8:h8 + 8, :], ps[u][1][0:TT, :].rearrange("p (a d) -> p a d", a=8),
                                                bcast(rden[u][:, t, h8:h8 + 8], 2, [TT, 8, D]), ALU.mult).then_inc(S["o_ready"], 1)

                    for n in range(UNITS + 2):
                        for u in range(2):
                            if n < UNITS:
                                unit_max(n, u)
                        if n >= 2:
                            t, h0, nh = unit_heads(n - 2)
                            if (h0 + nh) % 8 == 0:
                                for u in range(2):
                                    scale_o(n - 2, u)
                    for u in range(2):
                        need("wo_ps", u)
                        own.link(nc.vector.tensor_tensor(h[u][:], ps[u][0][0:TT, 0:2 * D].rearrange("p (t d) -> p t d", t=2), h[u][:], ALU.add))
                        ln_stats(h[u], 2, u)
                    for u in range(2):
                        ln_apply(h[u], xn[u], 2, u, "xn2")
                    for u in range(2):
                        copy_xT(2, 1, u)
                    for u in range(2):
                        need("lg_ps", u)
                        l2 = ps[u][0][0:TT, 0:2 * NE].rearrange("p (t e) -> p t e", t=2)
                        own.link(nc.vector.tensor_reduce(lmax[u][:], l2, AX.X, ALU.max))
                        nc.vector.tensor_tensor(lg[u][:], l2, bcast(lmax[u][:], 2, [TT, 2, NE]), ALU.subtract).then_inc(S["lmax"], 1)
                    for u in range(2):
                        need("el", u, met=met)
                        for t in range(2):
                            own.step(nc.vector.max(top[u][:, t, :], el[u][:, t, :]))
                        own.wait(met)
                        for t in range(2):
                            own.step(nc.vector.max_index(topi[u][:, t, :], top[u][:, t, :], el[u][:, t, :]))
                        own.link(nc.vector.tensor_tensor(tsum[u][:], top[u][:, :, 0], top[u][:, :, 1], ALU.add))
                        own.step(nc.vector.tensor_copy(topf[u][:], topi[u][:, :, 0:2]))
                        own.link(nc.vector.reciprocal(trec[u][:], tsum[u][:]))
                        own.step(nc.vector.tensor_tensor(tw[u][:], top[u][:, :, 0:2], bcast(trec[u][:], 2, [TT, 2, 2]), ALU.mult))
                        for t in range(2):
                            own.step(nc.vector.tensor_tensor(oh[u][:, t], bcast(k["iota8"][:], 1, [TT, 2, NE]), bcast(topf[u][:, t, :], 2, [TT, 2, NE]), ALU.is_equal))
                        own.wait()
                        own.link(nc.vector.tensor_tensor(oh[u][:], oh[u][:], bcast(tw[u][:], 3, [TT, 2, 2, NE]), ALU.mult))
                        own.step(nc.vector.tensor_tensor(gate[u][:], oh[u][:, :, 0, :], oh[u][:, :, 1, :], ALU.add))
                        own.wait(met)
                    for u in range(2):
                        need("moe_ps", u)
                        for t in range(2):
                            own.step(nc.vector.tensor_tensor(mo[u][:, t], ps[u][2 + t][0:TT, :].rearrange("p (e d) -> p e d", e=NE), k["b2p"][:], ALU.add))
                        own.step(nc.vector.tensor_tensor(h[u][:], ps[u][1][0:TT, 0:2 * D].rearrange("p (t d) -> p t d", t=2), h[u][:], ALU.add))
                        own.wait()
                        own.step(nc.vector.tensor_tensor(h[u][:], h[u][:], bcast(k["b2s"][:], 1, [TT, 2, D]), ALU.add))
                        for t in range(2):
                            own.step(nc.vector.tensor_tensor(mo[u][:, t], mo[u][:, t], bcast(gate[u][:, t, :], 2, [TT, NE, D]), ALU.mult))
                        own.wait()
                        own.link(nc.vector.tensor_reduce(mr[u][:], mo[u][:].rearrange("p t e d -> p t d e"), AX.X, ALU.add))
                        own.link(nc.vector.tensor_tensor(h[u][:], h[u][:], mr[u][:], ALU.add))
                        ln_stats(h[u], 3, u)
                    for u in range(2):
                        ln_apply(h[u], xn[u], 3, u, "xn3")
                    for u in range(2):
                        copy_xT(3, 0, u)
                        ln_stats(xn[u], 5, u)
                    for u in range(2):
                        need("qkv_ps", u)
                        own.step(nc.vector.tensor_copy(qT[u][:], ps[u][1][0:D, 0:NP]))
                        own.link(nc.vector.tensor_reduce(kmx[u][:], ps[u][1][0:D, NP:NP + N], AX.X, ALU.max))
                        nc.vector.tensor_scalar(kmx[u][:], kmx[u][:], -1.0, None, ALU.mult).then_inc(S["kmx"], 1)
                        nc.vector.tensor_copy(v[u][:], ps[u][2][0:TT, 0:2 * D].rearrange("p (t d) -> p t d", t=2)).then_inc(S["lin_v"], 1)
                    for u in range(2):
                        ln_apply(xn[u], g[u], 5, u, "xg")
                    for u in range(2):
                        need("xgT_ps", u)
                        nc.vector.tensor_scalar(xgT[u][:], ps[u][0][0:D, 0:NP], k["lng"][:, 0:1], k["lnb"][:, 0:1], ALU.mult, ALU.add).then_inc(S["xgT"], 1)
                    for u in range(2):
                        need("ek_ps", u)
                        nc.vector.tensor_copy(ek[u][:], ps[u][2][0:TT, 0:2 * D].rearrange("p (t d) -> p t d", t=2)).then_inc(S["ek"], 1)
                        own.link(nc.vector.reciprocal(krec[u][:], ksum[u][:]))
                    for u in range(2):
                        need("ctx_ps", u)
                        nc.vector.scalar_tensor_tensor(out=ctxs[u][:], in0=ps[u][0][0:D, 0:D], scalar=krec[u][:, 0:1], in1=k["blocks"][:],
                                                       op0=ALU.mult, op1=ALU.mult).then_inc(S["ctx"], 1)
                    for u in range(2):
                        need("g_ps", u)
                        nc.vector.tensor_tensor(g[u][:], ps[u][2][0:TT, 0:2 * D].rearrange("p (t d) -> p t d", t=2), bcast(k["bg2"][:], 1, [TT, 2, D]), ALU.add).then_inc(S["g_in"], 1)
                    for u in range(2):
                        need("g_exp", u)
                        own.link(nc.vector.tensor_scalar(g[u][:], g[u][:], 1.0, None, ALU.add))
                        own.link(nc.vector.reciprocal(g[u][:], g[u][:]))
                        need("lin_ps", u)
                        nc.vector.tensor_tensor(g[u][:], ps[u][1][0:TT, 0:2 * D].rearrange("p (t d) -> p t d", t=2), g[u][:], ALU.mult).then_inc(S["og"], 1)
                    for u in range(2):
                        need("ogT_ps", u)
                        nc.vector.tensor_copy(xgT[u][:], ps[u][3][0:D, 0:NP]).then_inc(S["ogT"], 1)
                        own.link(nc.vector.tensor_tensor(h[u][:], h[u][:], bcast(k["bproj"][:], 1, [TT, 2, D]), ALU.add))
                    for u in range(2):
                        need("proj_ps", u)
                        own.link(nc.vector.tensor_tensor(h[u][:], ps[u][2][0:TT, 0:2 * D].rearrange("p (t d) -> p t d", t=2), h[u][:], ALU.add))
                        ln_stats(h[u], 4, u)
                    for u in range(2):
                        ln_apply(h[u], xn[u], 4, u, "xn4")
                    own.close()


FRONT_STEPS = 135


def memory_phase(nc, c, xn4_rows, kv_rows):
    assert NTILES % 2 == 1
    with ExitStack() as ctx:
        def sb(name, shape, dt=F32):
            return ctx.enter_context(nc.sbuf_tensor(name, shape, dt))

        def sem(name):
            return ctx.enter_context(nc.semaphore("b_" + name))

        def two(name, shape, dt=F32):
            return [sb(f"{name}{u}", shape, dt) for u in range(2)]

        R = 2 * HV
        ident = sb("b_ident", [128, 128])
        wpkT = sb("wpkT", [D // 2, R, D])
        keysT = sb("keysT", [D // 2, R, NK])
        offs = sb("offs", [TILE, HV, TOPK])
        iota = sb("iota", [TILE, NC])
        wk = sb("wk", [D, R * NK])
        xb = two("xb", [TILE, D])
        xT = two("b_xT", [D, TILE])
        sim = sb("sim", [TILE, R, NK])
        sim2 = sb("sim2", [TILE, R, NK])
        ranks = sb("ranks", [TILE, R, TOPK], U32)
        half = [sb(f"half{p}", [TILE, 2, HV, TOPK]) for p in range(2)]
        pairs = sb("pairs", [TILE, 2, HV, NC])
        pairs2 = sb("pairs2", [TILE, HV, NC])
        best = sb("best", [TILE, HV, TOPK])
        place = sb("place", [TILE, HV, TOPK], U32)
        placef = sb("placef", [TILE, HV, TOPK])
        onehot = sb("onehot", [TILE, HV, TOPK, NC])
        rowf = sb("rowf", [TILE, HV, TOPK])
        rows = two("rows", [TILE, HV * TOPK], U32)
        ex = sb("ex", [TILE, HV, TOPK])
        ssum = sb("ssum", [TILE, HV])
        weight = two("weight", [TILE, HV, TOPK])
        G = [sb(f"G{h}", [TILE, TOPK * 2 * D]) for h in range(HV)]
        kv = two("kv", [TILE, 2, HV, D])
        ps_x = ctx.enter_context(nc.psum_tensor("ps_x", [128, 512], F32))
        ps_s = [ctx.enter_context(nc.psum_tensor(f"ps_s{p}", [128, 512], F32)) for p in range(2)]
        ps_kv = [[ctx.enter_context(nc.psum_tensor(f"ps_kv{u}_{q}", [128, 512], F32)) for q in range(2)] for u in range(2)]

        consts_in, wk_ps, wk_ready = sem("consts_in"), sem("wk_ps"), sem("wk_ready")
        x_in = [sem(f"x_in{u}") for u in range(2)]
        xT_ps, xT_ready, sim_ps, sim_in, rows_ready, shifted, exped, weight_ready = (
            sem(s) for s in ("xT_ps", "xT_ready", "sim_ps", "sim_in", "rows_ready", "shifted", "exped", "weight_ready"))
        landed = [sem(f"landed{h}") for h in range(HV)]
        weighed, summed, kv_ready = sem("weighed"), sem("summed"), sem("kv_ready")
        kv_out = [sem(f"kv_out{u}") for u in range(2)]
        vstep = sem("vector_step")
        met = (consts_in, 16 * 5)

        def schedule(eng, front, back):
            front(0, 0, 0)
            with eng.Fori(0, NTILES // 2) as i:
                front(2 * i + 1, 1, i)
                back(2 * i, 0, i)
                front(2 * i + 2, 0, i + 1)
                back(2 * i + 1, 1, i)
            back(NTILES - 1, 0, NTILES // 2)

        with nc.Block() as block:
            @block.sync
            def _(sp):
                for dst, name in ((ident, "ident"), (wpkT, "wpkT"), (keysT, "keysT"), (offs, "offs"), (iota, "iota")):
                    sp.dma_start(dst[:], c[name]).then_inc(consts_in, 16)

                def front(t, u, n):
                    sp.wait_ge(xT_ps, t)
                    sp.dma_start(xb[u][:], xn4_rows[bass.ds(t * TILE, TILE), :]).then_inc(x_in[u], 16)

                def back(t, u, n):
                    sp.wait_ge(kv_ready, t + 1)
                    sp.dma_start(kv_rows[bass.ds(t * TILE, TILE), :], kv[u][:].rearrange("p a h d -> p (a h d)")).then_inc(kv_out[u], 16)

                schedule(sp, front, back)
                sp.wait_ge(kv_out[0], 16 * (NTILES // 2 + 1))
                sp.wait_ge(kv_out[1], 16 * (NTILES // 2))

            @block.tensor
            def _(pe):
                pe.wait_ge(consts_in, 16 * 5)
                for r in range(R):
                    mm = nc.tensor.matmul(ps_s[r // HV][0:D, (r % HV) * NK:(r % HV + 1) * NK], wpkT[:, r, :], keysT[:, r, :], start=True, stop=True)
                mm.then_inc(wk_ps, 1)
                pe.wait_ge(wk_ready, 1)

                def front(t, u, n):
                    wait_apart(pe, x_in[u], 16 * (n + 1), met)
                    nc.tensor.transpose(ps_x[0:D, 0:TILE], xb[u][:], ident[:]).then_inc(xT_ps, 1)
                    pe.wait_ge(xT_ready, t + 1)
                    for p in range(2):
                        if p == 0:
                            pe.wait_ge(sim_in, t)
                        mm = nc.tensor.matmul(ps_s[p][:], xT[u][:], wk[:, p * 512:(p + 1) * 512], start=True, stop=True)
                    mm.then_inc(sim_ps, 1)

                def back(t, u, n):
                    for h in range(HV):
                        pe.wait_ge(weighed, t * HV + h + 1)
                        if h == 0:
                            pe.wait_ge(kv_ready, 2 * n)
                        for j in range(TOPK):
                            mm = nc.tensor.matmul(ps_kv[u][h // 4][:, (h % 4) * 128:(h % 4 + 1) * 128], ident[:], G[h][:, j * 128:(j + 1) * 128],
                                                  start=(j == 0), stop=(j == TOPK - 1))
                        mm.then_inc(summed, 1)

                schedule(pe, front, back)

            @block.scalar
            def _(act):
                act.wait_ge(wk_ps, 1)
                for p in range(2):
                    a = nc.scalar.activation(wk[:, p * 512:(p + 1) * 512], ps_s[p][0:D, :], ACT.Copy)
                a.then_inc(wk_ready, 1)

                def front(t, u, n):
                    act.wait_ge(xT_ps, t + 1)
                    nc.scalar.activation(xT[u][:], ps_x[0:D, 0:TILE], ACT.Copy).then_inc(xT_ready, 1)
                    act.wait_ge(sim_ps, t + 1)
                    act.wait_ge(rows_ready, t)
                    for p in range(2):
                        a = nc.scalar.activation(sim[:, p * HV:(p + 1) * HV, :].rearrange("p r k -> p (r k)"), ps_s[p][:], ACT.Copy)
                    a.then_inc(sim_in, 1)
                    act.wait_ge(shifted, t + 1)
                    nc.scalar.activation(ex[:], ex[:], ACT.Exp).then_inc(exped, 1)

                def back(t, u, n):
                    act.wait_ge(summed, (t + 2) * HV)
                    act.wait_ge(kv_out[u], 16 * n)
                    for q in range(2):
                        a = nc.scalar.activation(kv[u][:, :, 4 * q:4 * q + 4, :], ps_kv[u][q][:].rearrange("p (h a d) -> p a h d", h=4, a=2), ACT.Copy)
                    a.then_inc(kv_ready, 1)

                schedule(act, front, back)

            @block.gpsimd
            def _(pool):
                pool.sem_inc(summed, HV)

                def front(t, u, n):
                    pass

                def back(t, u, n):
                    pool.wait_ge(rows_ready, t + 1)
                    for h in range(HV):
                        wait_apart(pool, summed, t * HV + h + 1, met)
                        for j in range(TOPK):
                            pool.indirect_dma_start(G[h][:, j * 128:(j + 1) * 128], None, c["table"],
                                                    bass.IndirectOffsetOnAxis(ap=rows[u][:, h * TOPK + j:h * TOPK + j + 1], axis=0)).then_inc(landed[h], 16)

                schedule(pool, front, back)

            @block.vector
            def _(dve):
                dve.wait_ge(consts_in, 16 * 5)

                def front(t, u, n):
                    own = Chain(dve, vstep, t, FRONT_STEPS)
                    wait_apart(dve, sim_in, t + 1, met)
                    val = [half[p][:, 0] for p in range(2)]
                    for a in range(2):
                        src = sim if a == 0 else sim2
                        cols = slice(8 * a, 8 * a + 8)
                        for r in range(R):
                            own.step(nc.vector.max(val[r // HV][:, r % HV, cols], src[:, r, :]))
                        own.wait(met)
                        for r in range(R):
                            own.step(nc.vector.max_index(ranks[:, r, cols], val[r // HV][:, r % HV, cols], src[:, r, :]))
                        if a == 0:
                            for r in range(R):
                                own.step(nc.vector.match_replace(sim2[:, r, :], val[r // HV][:, r % HV, cols], sim[:, r, :], LOWEST))
                        own.wait(met if a == 0 else None)
                    own.step(nc.vector.tensor_copy(half[0][:, 1], ranks[:, 0:HV, :]))
                    own.link(nc.vector.scalar_tensor_tensor(out=half[1][:, 1].rearrange("p h k -> p (h k)"), in0=ranks[:, HV:R, :].rearrange("p h k -> p (h k)"), scalar=float(NK),
                                                            in1=offs[:].rearrange("p h k -> p (h k)"), op0=ALU.mult, op1=ALU.add))
                    f0 = half[0][:].rearrange("p a h k -> p (a h) k")
                    f1 = half[1][:].rearrange("p a h k -> p (a h) k")
                    pr = pairs[:].rearrange("p a h k -> p (a h) k")
                    at = r0 = 0
                    while r0 < TOPK:
                        n = CUTS[r0]
                        rn = CUTS.count(n)
                        out = pr[:, :, at:at + rn * n].rearrange("p g (r n) -> p g r n", r=rn)
                        own.step(nc.vector.tensor_tensor(out, f0[:, :, r0:r0 + rn].unsqueeze(3).to_broadcast([TILE, R, rn, n]),
                                                         f1[:, :, 0:n].unsqueeze(2).to_broadcast([TILE, R, rn, n]), ALU.add))
                        at += rn * n
                        r0 += rn
                    own.wait(met)
                    for a in range(2):
                        src = pairs[:, 0] if a == 0 else pairs2[:]
                        cols = slice(8 * a, 8 * a + 8)
                        for hh in range(HV):
                            own.step(nc.vector.max(best[:, hh, cols], src[:, hh, :]))
                        own.wait(met)
                        for hh in range(HV):
                            own.step(nc.vector.max_index(place[:, hh, cols], best[:, hh, cols], src[:, hh, :]))
                        if a == 0:
                            for hh in range(HV):
                                own.step(nc.vector.match_replace(pairs2[:, hh, :], best[:, hh, cols], pairs[:, 0, hh, :], LOWEST))
                        own.wait(met if a == 0 else None)
                    own.step(nc.vector.tensor_copy(placef[:], place[:]))
                    nc.vector.tensor_tensor(ex[:], best[:], best[:, :, 0:1].to_broadcast([TILE, HV, TOPK]), ALU.subtract).then_inc(shifted, 1)
                    own.wait()
                    own.link(nc.vector.tensor_tensor(onehot[:].rearrange("p h k c -> p (h k) c"), iota[:].unsqueeze(1).to_broadcast([TILE, HV * TOPK, NC]),
                                                     placef[:].rearrange("p h k -> p (h k)").unsqueeze(2).to_broadcast([TILE, HV * TOPK, NC]), ALU.is_equal))
                    own.link(nc.vector.tensor_tensor(onehot[:], onehot[:], pairs[:, 1].unsqueeze(2).to_broadcast([TILE, HV, TOPK, NC]), ALU.mult))
                    own.link(nc.vector.tensor_reduce(rowf[:], onehot[:], AX.X, ALU.add))
                    nc.vector.tensor_copy(rows[u][:], rowf[:].rearrange("p h k -> p (h k)")).then_inc(rows_ready, 1)
                    dve.wait_ge(exped, t + 1)
                    own.link(nc.vector.tensor_reduce(ssum[:], ex[:], AX.X, ALU.add))
                    own.link(nc.vector.reciprocal(ssum[:], ssum[:]))
                    nc.vector.tensor_tensor(weight[u][:], ex[:], ssum[:].unsqueeze(2).to_broadcast([TILE, HV, TOPK]), ALU.mult).then_inc(weight_ready, 1)
                    own.close()

                def back(t, u, n):
                    dve.wait_ge(weight_ready, t + 1)
                    for h in range(HV):
                        dve.wait_ge(landed[h], (t + 1) * (16 * TOPK))
                        g = G[h][:].rearrange("p (k d) -> p k d", k=TOPK)
                        nc.vector.tensor_tensor(g, g, weight[u][:, h, :].unsqueeze(2).to_broadcast([TILE, TOPK, 2 * D]), ALU.mult).then_inc(weighed, 1)

                schedule(dve, front, back)


C_STEPS = 16


def readout_phase(nc, c, h3_rows, xn4_rows, kv_rows, out):
    UT = HV // 4
    UNITS = UT + HV // 2
    W = 4 * TT
    with ExitStack() as ctx:
        def sb(name, shape, dt=F32):
            return ctx.enter_context(nc.sbuf_tensor("r_" + name, shape, dt))

        def two(name, shape, dt=F32):
            return [sb(f"{name}{u}", shape, dt) for u in range(2)]

        ident = sb("ident", [128, 128])
        ident_b = sb("ident_b", [128, 128], BF16)
        mask = [sb(f"mask{t}", [TT, W], BF16) for t in range(2)]
        wq = sb("wq", [D, HV * D])
        wo = sb("wo", [128, HV * D // 128, D])
        h = two("h", [TT, 2, D])
        x = two("x", [TT, 2, D])
        kv = two("kv", [TT, 2, 2, HV * D])
        xT = two("xT", [D, NP])
        qT = two("qT", [D, HV, NP])
        kT = two("kT", [D, HV, NP])
        m = two("m", [TT, 2, HV])
        nb = two("nb", [TT, 2, HV])
        den = two("den", [TT, 2, HV])
        rden = two("rden", [TT, 2, HV])
        P = two("P", [TT, UNITS, W])
        PT = [[sb(f"PT{u}_{s}", [TT, W]) for s in range(2)] for u in range(2)]
        O = two("O", [TT, 2, HV, D])
        OT = two("OT", [128, 2, W])
        y = two("y", [TT, 2, D])
        ps = [[ctx.enter_context(nc.psum_tensor(f"psr{u}_{s}", [128, 512], F32)) for s in range(4)] for u in range(2)]
        consts_in = ctx.enter_context(nc.semaphore("c_consts_in"))
        setup = ctx.enter_context(nc.semaphore("c_setup"))
        rows_in = [ctx.enter_context(nc.semaphore(f"c_rows_in{u}")) for u in range(2)]
        rows_out = [ctx.enter_context(nc.semaphore(f"c_rows_out{u}")) for u in range(2)]
        vstep = ctx.enter_context(nc.semaphore("c_vector_step"))
        S = {s: ctx.enter_context(nc.semaphore("c_" + s)) for s in
             "xT_ps xT q_ps qT k_ps kT s_ps nb p_ready pt_ps pt_ready o_ps o_ready oT_ps oT_ready wo_ps y".split()}

        met = (consts_in, 16 * 5)

        def tok(t):
            return slice(t * TT, (t + 1) * TT)

        def unit_heads(n):
            return (0, 4 * n, 4) if n < UT else (1, 2 * (n - UT), 2)

        with nc.Block() as block:
            @block.sync
            def _(sp):
                for dst, name in ((ident, "ident"), (wq, "wq_mem"), (wo, "wo_mem")):
                    sp.dma_start(dst[:], c[name]).then_inc(consts_in, 16)
                for t in range(2):
                    sp.dma_start(P[0][:, t, :], c["causal"][t]).then_inc(consts_in, 16)
                with sp.Fori(0, B // 2) as i:
                    for u in range(2):
                        sp.wait_ge(S["y"], i * 2)
                        for dst, src in ((h[u][:], h3_rows), (x[u][:], xn4_rows), (kv[u][:].rearrange("p t a f -> p t (a f)"), kv_rows)):
                            sp.dma_start(dst, src[bass.ds((2 * i + u) * N, NP), :].rearrange("(t p) f -> p t f", t=2)).then_inc(rows_in[u], 16)
                    for u in range(2):
                        sp.wait_ge(S["y"], i * 2 + u + 1)
                        for t, rows in ((0, TT), (1, N - TT)):
                            sp.dma_start(out[bass.ds(2 * i + u, 1), t * TT:t * TT + rows, :].rearrange("o p d -> (o p) d"), y[u][0:rows, t, :]).then_inc(rows_out[u], 16)
                for u in range(2):
                    sp.wait_ge(rows_out[u], 32 * (B // 2))

            @block.tensor
            def _(pe):
                pe.wait_ge(consts_in, 16 * 5)
                pe.wait_ge(setup, 3)

                def done(mm, name):
                    mm.then_inc(S[name], 1)

                with pe.Fori(0, B // 2) as i:
                    def need(name, u, per=1, n=0, met=None):
                        if met:
                            wait_apart(pe, S[name], i * 2 * per + 2 * n + u + 1, met)
                        else:
                            pe.wait_ge(S[name], i * 2 * per + 2 * n + u + 1)

                    for u in range(2):
                        wait_apart(pe, rows_in[u], (i + 1) * 48, met)
                        wait_apart(pe, S["y"], i * 2, met)
                        for t in range(2):
                            mm = nc.tensor.transpose(ps[u][0][0:D, tok(t)], x[u][:, t, :], ident[0:TT, 0:TT])
                        done(mm, "xT_ps")
                    for g in range(HV // 2):
                        for u in range(2):
                            if g >= 2:
                                need("kT", u, HV // 2, g - 2, met=met)
                            for a in range(2):
                                for t in range(2):
                                    mm = nc.tensor.transpose(ps[u][2 + g % 2][0:D, (2 * a + t) * TT:(2 * a + t + 1) * TT],
                                                             kv[u][:, t, 0, (2 * g + a) * D:(2 * g + a + 1) * D], ident[0:TT, 0:TT])
                            done(mm, "k_ps")
                    for g in range(HV // 2):
                        for u in range(2):
                            if g == 0:
                                need("xT", u, met=met)
                            else:
                                need("qT", u, HV // 2, g - 1, met=met)
                            for a in range(2):
                                mm = nc.tensor.matmul(ps[u][1][0:D, a * NP:(a + 1) * NP], wq[:, (2 * g + a) * D:(2 * g + a + 1) * D], xT[u][:], start=True, stop=True)
                            done(mm, "q_ps")

                    def scores(n, u):
                        t, h0, nh = unit_heads(n)
                        if n == 0:
                            need("qT", u, HV // 2, HV // 2 - 1)
                            need("kT", u, HV // 2, HV // 2 - 1)
                        if n >= 2:
                            need("p_ready", u, UNITS, n - 2)
                        bank = ps[u][2 + n % 2]
                        nc.tensor.matmul(bank[0:TT, 0:W], ident_b[0:TT, 0:TT], mask[t][:], start=True, stop=False)
                        w = (t + 1) * TT
                        for a in range(nh):
                            hh = h0 + a
                            mm = nc.tensor.matmul(bank[0:TT, a * w:(a + 1) * w], qT[u][:, hh, tok(t)], kT[u][:, hh, 0:w],
                                                  start=False, stop=(a == nh - 1))
                        done(mm, "s_ps")

                    def turn_p(n, u):
                        need("p_ready", u, UNITS, n)
                        if n >= 1:
                            need("pt_ready", u, UNITS, n - 1)
                        for a in range(4):
                            mm = nc.tensor.transpose(ps[u][0][0:TT, a * TT:(a + 1) * TT], P[u][:, n, a * TT:(a + 1) * TT], ident[0:TT, 0:TT])
                        done(mm, "pt_ps")

                    def values(n, u):
                        t, h0, nh = unit_heads(n)
                        need("pt_ready", u, UNITS, n)
                        if h0 == 0 and n:
                            need("o_ready", u, 2, 0)
                        for a in range(nh):
                            hh = h0 + a
                            for s in range(t + 1):
                                col = (a * (t + 1) + s) * TT
                                mm = nc.tensor.matmul(ps[u][1][0:TT, hh * D:(hh + 1) * D], PT[u][n % 2][:, col:col + TT],
                                                      kv[u][:, s, 1, hh * D:(hh + 1) * D], start=(s == 0), stop=(s == t))
                        done(mm, "o_ps")

                    for n in range(UNITS + 2):
                        for u in range(2):
                            if n < UNITS:
                                scores(n, u)
                        for u in range(2):
                            if 1 <= n <= UNITS:
                                turn_p(n - 1, u)
                        for u in range(2):
                            if n >= 2:
                                values(n - 2, u)
                    for t in range(2):
                        for u in range(2):
                            need("o_ready", u, 2, t)
                            flat = O[u][:, t].rearrange("p h d -> p (h d)")
                            for a in range(4):
                                mm = nc.tensor.transpose(ps[u][2 + t][:, a * TT:(a + 1) * TT], flat[:, a * 128:(a + 1) * 128], ident[0:TT, 0:TT])
                            done(mm, "oT_ps")
                    for u in range(2):
                        need("oT_ready", u, 2, 1)
                        for t in range(2):
                            for a in range(4):
                                mm = nc.tensor.matmul(ps[u][0][0:TT, t * D:(t + 1) * D], OT[u][:, t, a * TT:(a + 1) * TT], wo[:, a, :], start=(a == 0), stop=(a == 3))
                        done(mm, "wo_ps")

            @block.scalar
            def _(act):
                act.wait_ge(setup, 3)
                with act.Fori(0, B // 2) as i:
                    def need(name, u, per=1, n=0, met=None):
                        if met:
                            wait_apart(act, S[name], i * 2 * per + 2 * n + u + 1, met)
                        else:
                            act.wait_ge(S[name], i * 2 * per + 2 * n + u + 1)

                    for g in range(HV // 2):
                        for u in range(2):
                            need("k_ps", u, HV // 2, g)
                            nc.scalar.activation(kT[u][:, 2 * g:2 * g + 2, :].rearrange("p a t -> p (a t)"), ps[u][2 + g % 2][0:D, 0:2 * NP], ACT.Copy).then_inc(S["kT"], 1)

                    def exps(n, u):
                        t, h0, nh = unit_heads(n)
                        need("nb", u, UNITS, n)
                        w = (t + 1) * TT
                        for a in range(nh):
                            hh = h0 + a
                            e = nc.scalar.activation(P[u][:, n, a * w:(a + 1) * w], ps[u][2 + n % 2][0:TT, a * w:(a + 1) * w], ACT.Exp,
                                                     scale=D ** -0.5, bias=nb[u][:, t, hh:hh + 1], accum_out=den[u][:, t, hh:hh + 1])
                        e.then_inc(S["p_ready"], 1)

                    def copy_pt(n, u):
                        need("pt_ps", u, UNITS, n)
                        if n >= 2:
                            need("o_ps", u, UNITS, n - 2)
                        nc.scalar.activation(PT[u][n % 2][:], ps[u][0][0:TT, 0:W], ACT.Copy).then_inc(S["pt_ready"], 1)

                    for n in range(UNITS + 1):
                        for u in range(2):
                            if n < UNITS:
                                exps(n, u)
                        for u in range(2):
                            if n >= 1:
                                copy_pt(n - 1, u)
                    for t in range(2):
                        for u in range(2):
                            need("oT_ps", u, 2, t)
                            nc.scalar.activation(OT[u][:, t, :], ps[u][2 + t][:, 0:W], ACT.Copy).then_inc(S["oT_ready"], 1)

            @block.vector
            def _(dve):
                dve.wait_ge(consts_in, 16 * 5)
                for t in range(2):
                    nc.vector.tensor_copy(mask[t][:], P[0][:, t, :]).then_inc(setup, 1)
                nc.vector.tensor_copy(ident_b[:], ident[:]).then_inc(setup, 1)
                with dve.Fori(0, B // 2) as i:
                    own = Chain(dve, vstep, i, C_STEPS)

                    def need(name, u, per=1, n=0, met=None):
                        if met:
                            wait_apart(dve, S[name], i * 2 * per + 2 * n + u + 1, met)
                        else:
                            dve.wait_ge(S[name], i * 2 * per + 2 * n + u + 1)

                    for u in range(2):
                        need("xT_ps", u)
                        nc.vector.tensor_copy(xT[u][:], ps[u][0][0:D, 0:NP]).then_inc(S["xT"], 1)
                    for g in range(HV // 2):
                        for u in range(2):
                            need("q_ps", u, HV // 2, g)
                            nc.vector.tensor_copy(qT[u][:, 2 * g:2 * g + 2, :].rearrange("p a t -> p (a t)"), ps[u][1][0:D, 0:2 * NP]).then_inc(S["qT"], 1)

                    def unit_max(n, u):
                        t, h0, nh = unit_heads(n)
                        need("s_ps", u, UNITS, n)
                        own.link(nc.vector.tensor_reduce(m[u][:, t, h0:h0 + nh], ps[u][2 + n % 2][0:TT, 0:W].rearrange("p (a s) -> p a s", a=nh), AX.X, ALU.max))
                        nc.vector.tensor_scalar(nb[u][:, t, h0:h0 + nh], m[u][:, t, h0:h0 + nh], -(D ** -0.5), None, ALU.mult).then_inc(S["nb"], 1)

                    def scale_o(t, u):
                        need("o_ps", u, UNITS, UT - 1 if t == 0 else UNITS - 1)
                        own.link(nc.vector.reciprocal(rden[u][:, t, :], den[u][:, t, :]))
                        nc.vector.tensor_tensor(O[u][:, t], ps[u][1][0:TT, :].rearrange("p (a d) -> p a d", a=HV),
                                                bcast(rden[u][:, t, :], 2, [TT, HV, D]), ALU.mult).then_inc(S["o_ready"], 1)

                    for n in range(UNITS + 2):
                        for u in range(2):
                            if n < UNITS:
                                unit_max(n, u)
                        if n - 2 in (UT - 1, UNITS - 1):
                            for u in range(2):
                                scale_o(int(n - 2 == UNITS - 1), u)
                    for u in range(2):
                        need("wo_ps", u)
                        dve.wait_ge(rows_out[u], i * 32)
                        nc.vector.tensor_tensor(y[u][:], ps[u][0][0:TT, 0:2 * D].rearrange("p (t d) -> p t d", t=2), h[u][:], ALU.add).then_inc(S["y"], 1)
                    own.close()


def vit_tower(nc, c, out):
    h3 = nc.dram_tensor("h3_rows", (ROWS, D), F32, kind="Internal").ap()
    xn4 = nc.dram_tensor("xn4_rows", (ROWS, D), F32, kind="Internal").ap()
    kv = nc.dram_tensor("kv_rows", (ROWS, 2 * HV * D), F32, kind="Internal").ap()
    with nc.sbuf_tensor("pad", [ROWS - B * N, D], F32) as pad, nc.semaphore("pad_set") as pad_set, nc.semaphore("pad_out") as pad_out:
        with nc.Block() as block:
            @block.gpsimd
            def _(pool):
                nc.gpsimd.memset(pad[:], 0.0).then_inc(pad_set, 1)

            @block.sync
            def _(sp):
                sp.wait_ge(pad_set, 1)
                for rows in (h3, xn4):
                    sp.dma_start(rows[B * N:ROWS, :], pad[:]).then_inc(pad_out, 16)
                sp.wait_ge(pad_out, 32)
    image_phase(nc, c, h3, xn4)
    memory_phase(nc, c, xn4, kv)
    readout_phase(nc, c, h3, xn4, kv, out)


def _layout(inp):
    import numpy as np

    a = {k: np.asarray(v) for k, v in inp.items()}
    G = IMG // PATCH
    px = a["x"].reshape(B, CH, G, PATCH, G, PATCH).transpose(0, 1, 3, 5, 2, 4).reshape(B, KC, 128, G * G)
    pixT = np.zeros((B, 128, KC, NP), np.float32)
    pixT[:, :, :, 1:N] = px.transpose(0, 2, 1, 3)
    rows = lambda v, n: np.repeat(v.reshape(1, -1), n, axis=0)
    add = rows(a["L0_tok_b"], NP)
    add[0] = a["cls_tok"].reshape(-1)
    swap = np.arange(D) ^ 1
    wq = a["L0_attn_wq"].reshape(HQ, D, D)
    wqq = np.concatenate([wq, wq[:, swap]], axis=1).transpose(2, 0, 1)
    wk, wv = a["L0_attn_wkv"][:D], a["L0_attn_wkv"][D:]
    t = np.arange(NP, dtype=np.float32)
    freqs = np.float32(10000.0) ** (np.float32(-2.0) * np.arange(D // 2, dtype=np.float32) / np.float32(D))
    theta = t[:, None] * freqs[None, :]
    cos = np.repeat(np.cos(theta), 2, axis=1)
    sin = np.repeat(np.sin(theta), 2, axis=1) * np.where(np.arange(D) % 2 == 0, np.float32(-1), np.float32(1))
    rope = np.concatenate([cos, sin], axis=1).astype(np.float32)
    tiles = lambda v: v.reshape(2, TT, -1).transpose(1, 0, 2)
    q, s = np.arange(NP)[:, None], np.arange(NP)[None, :]

    def masks(ok):
        m = np.where(ok, np.float32(0), np.float32(NEG))
        return np.stack([np.tile(m[:TT, :TT], (1, 4)), np.tile(m[TT:, :], (1, 2))])
    w1 = np.concatenate([a["L0_ffn_W1p"], a["L0_ffn_W1s"][None]]).transpose(1, 0, 2)
    b1 = np.concatenate([a["L0_ffn_b1p"], a["L0_ffn_b1s"][None]]).reshape(NE + 1, 2, 128).transpose(2, 0, 1)
    w2 = np.concatenate([a["L0_ffn_W2p"], a["L0_ffn_W2s"][None]]).reshape(NE + 1, 2, 128, D).transpose(2, 0, 1, 3)
    col = lambda v: v.reshape(-1, 1)
    return {k: np.ascontiguousarray(v) for k, v in dict(
        pixT=pixT, patch_w=a["L0_tok_W"].T.reshape(KC, 128, D).transpose(1, 0, 2), embed_add=tiles(add),
        ident=np.eye(128, dtype=np.float32), wqq=wqq,
        wkkv=np.concatenate([wk, wk[swap], wv]).T, rope_q=rope.T, rope_k=tiles(rope),
        wo=a["L0_attn_wo"].T.reshape(HQ * D // 128, 128, D).transpose(1, 0, 2), wr=a["L0_ffn_Wr"], w1=w1, b1=b1, w2=w2,
        b2p=np.repeat(a["L0_ffn_b2p"][None], TT, axis=0), b2s=rows(a["L0_ffn_b2s"], TT),
        iota8=rows(np.arange(NE, dtype=np.float32), TT), wqkv=a["L1_attn_Wqkv"], wproj=a["L1_attn_Wproj"],
        bproj=rows(a["L1_attn_bproj"], TT), lng=col(a["L1_attn_ln_g"]), lnb=col(a["L1_attn_ln_b"]), wg1=a["L1_attn_Wg1"],
        bg1=col(a["L1_attn_bg1"]), wg2=a["L1_attn_Wg2"], bg2=rows(a["L1_attn_bg2"], TT),
        blocks=np.kron(np.eye(8, dtype=np.float32), np.ones((D // 8, D // 8), np.float32)),
        qnw=rows(a["L0_attn_q_norm_w"], TT), knw=rows(a["L0_attn_k_norm_w"], TT),
        mask=masks((s <= q) & (q - s <= WINDOW)), causal=masks(s <= q),
        wpkT=a["L1_ffn_Wq_pk"].T.reshape(2 * HV, D // 2, D).transpose(1, 0, 2),
        keysT=a["L1_ffn_pk_keys"].transpose(3, 0, 2, 1).reshape(D // 2, 2 * HV, NK),
        offs=np.broadcast_to((np.arange(HV, dtype=np.float32) * (NK * NK))[None, :, None], (TILE, HV, TOPK)),
        iota=rows(np.arange(NC, dtype=np.float32), TILE),
        table=np.concatenate([a["L1_ffn_keys_table"], a["L1_ffn_values_table"]], axis=1),
        wq_mem=a["L1_ffn_Wq"], wo_mem=a["L1_ffn_Wo"].reshape(HV * D // 128, 128, D).transpose(1, 0, 2),
    ).items()}


def kernel(**inputs):
    import concourse.bacc as bacc
    from concourse import mybir as _mybir
    from concourse.bass_utils import run_bass_kernel_spmd as run

    nc = bacc.Bacc("TRN2", target_bir_lowering=False, num_devices=1)
    arrays = _layout(inputs)
    c = {k: nc.dram_tensor("in_" + k, v.shape, _mybir.dt.from_np(v.dtype), kind="ExternalInput").ap() for k, v in arrays.items()}
    out = nc.dram_tensor("out", (B, N, D), F32, kind="ExternalOutput").ap()
    vit_tower(nc, c, out)
    r = run(nc, [{"in_" + k: v for k, v in arrays.items()}], core_ids=[0])
    return r.results[0]["out"]
```

```python
from contextlib import ExitStack

import concourse.bass as bass
from concourse import mybir

F32 = mybir.dt.float32
BF16 = mybir.dt.bfloat16
U32 = mybir.dt.uint32
ALU = mybir.AluOpType
ACT = mybir.ActivationFunctionType
AX = mybir.AxisListType

B, CH, IMG, PATCH, D = 64, 3, 224, 16, 64
N = (IMG // PATCH) ** 2 + 1
TT = (N + 1) // 2
NP = 2 * TT
KC = CH * PATCH * PATCH // 128
HQ = 16
WINDOW = 128
NE, FF = 8, 256
GH = D // 4
HV, NK, TOPK = 8, 64, 16
CUTS = [TOPK // (r + 1) for r in range(TOPK)]
NC = sum(CUTS)
TILE = 128
NTILES = (B * N + TILE - 1) // TILE
ROWS = NTILES * TILE
LN_EPS = 1e-5
RMS_EPS = 1.1920929e-07
NEG = -1e30
LOWEST = -3.0e38
EXP_LN = "natural_log_exp_and_others"


def wait_apart(eng, sem, value, met):
    value = value if isinstance(value, int) else eng.to_reg(value)
    eng.wait_ge(*met)
    eng.wait_ge(sem, value)


class Chain:

    def __init__(self, eng, sem, trip, per_trip):
        self.eng, self.sem, self.base, self.per_trip, self.n = eng, sem, trip * per_trip, per_trip, 0

    def step(self, ins):
        ins.then_inc(self.sem, 1)
        self.n += 1

    def wait(self, met=None):
        if met:
            wait_apart(self.eng, self.sem, self.base + self.n, met)
        else:
            self.eng.wait_ge(self.sem, self.base + self.n)

    def link(self, ins):
        self.step(ins)
        self.wait()

    def close(self):
        assert self.n == self.per_trip, (self.n, self.per_trip)


def bcast(ap, axis, shape):
    return ap.unsqueeze(axis).to_broadcast(shape)


A_STEPS = 126
A_ACT_STEPS = 14
FRONT_STEPS = 144

STAGES = 48
PIECES = 32
TRIP = 3
SLOTS = 4


def run(gen, steps):
    for _ in range(steps):
        next(gen)


def schedule(eng, pair, front, head, after):
    run(pair(0), 2 * STAGES)
    run(front(0, 0, -1), PIECES)
    slot = HV * TRIP

    def tile(t, b, images, ahead):
        for hh in range(HV):
            for part in range(PIECES // HV):
                if images:
                    run(images, 2 * STAGES // slot // (PIECES // HV))
                if ahead:
                    run(ahead, 1)
                if part == 0 and hh:
                    after(t, b, hh - 1)
            head(t, b, hh)
        after(t, b, HV - 1)

    with eng.Fori(0, B // 2 - 1) as i:
        images = pair(i + 1)
        for b in range(TRIP):
            tile(TRIP * i + b, b, images, front(TRIP * i + b + 1, (b + 1) % TRIP, i))
    for t in range(TRIP * (B // 2 - 1), NTILES):
        tile(t, t % TRIP, None, front(t + 1, (t + 1) % TRIP, B // 2 - 1 - (t % TRIP == TRIP - 1)) if t + 1 < NTILES else None)


def image_and_memory_phase(nc, c, h3_rows, xn4_rows, kv_rows):
    QG = HQ // 4
    UNITS = QG + HQ // 2
    W = 4 * TT
    with ExitStack() as ctx:
        def sb(name, shape, dt=F32):
            return ctx.enter_context(nc.sbuf_tensor(name, shape, dt))

        def sem(name):
            return ctx.enter_context(nc.semaphore(name))

        def two(name, shape, dt=F32):
            return [sb(f"{name}{u}", shape, dt) for u in range(2)]

        shapes = dict(patch_w=[128, KC, D], embed_add=[TT, 2, D], ident=[128, 128], wqq=[D, HQ, 2 * D], wkkv=[D, 3 * D],
                      rope_q=[2 * D, NP], rope_k=[TT, 2, 2 * D], wo=[128, HQ * D // 128, D], wr=[D, NE], w1=[D, NE + 1, FF],
                      b1=[128, NE + 1, 2], w2=[128, NE + 1, 2, D], b2p=[TT, NE, D], b2s=[TT, D], iota8=[TT, NE],
                      wqkv=[D, 3 * D], wproj=[D, D], bproj=[TT, D], lng=[D, 1], lnb=[D, 1], wg1=[D, GH], bg1=[GH, 1],
                      wg2=[GH, D], bg2=[TT, D], blocks=[D, D], qnw=[TT, D], knw=[TT, D])
        k = {n: sb("c_" + n, s) for n, s in shapes.items()}
        mask = [sb(f"c_mask{t}", [TT, W], BF16) for t in range(2)]
        ident_b = sb("c_ident_b", [128, 128], BF16)
        knq = sb("knq", [TT, D])
        ones = sb("ones", [D, 1])
        eps_ln, eps_rms = sb("eps_ln", [TT, 1]), sb("eps_rms", [TT, 1])
        pix = two("pix", [128, KC, NP])
        h = two("h", [TT, 2, D])
        stats = sb("stats", [TT, 2, 6])
        mv = sb("mv", [TT, 2, 2])
        logs = sb("logs", [TT, 2 * HQ])
        rstd = sb("rstd", [TT, 2])
        xn = two("xn", [TT, 2, D])
        xT = sb("xT", [D, NP])
        kk = sb("kk", [TT, 2, 2 * D])
        kr = sb("kr", [TT, 2, D])
        ksq = sb("ksq", [TT, 2, D])
        kss = sb("kss", [TT, 2])
        krs = sb("krs", [TT, 2])
        kdup = sb("kdup", [TT, 2, 2, D])
        kT = sb("kT", [2 * D, NP])
        v = sb("v", [TT, 2, D])
        qr = sb("qr", [2 * D, HQ, NP])
        qsq_OT = sb("qsq_OT", [128, HQ * NP])
        qsq = qsq_OT[0:D, :].rearrange("p (h t) -> p h t", h=HQ)
        OT = qsq_OT[:, 0:4 * W].rearrange("p (n w) -> p n w", n=4)
        rq = sb("rq", [TT, 2, HQ])
        m = sb("m", [TT, 2, HQ])
        nb = sb("nb", [TT, 2, HQ])
        den = sb("den", [TT, 2, HQ])
        rden = sb("rden", [TT, 2, HQ])
        P_hid = sb("P_hid", [128, UNITS * W])
        P = P_hid[0:TT, :].rearrange("p (n w) -> p n w", n=UNITS)
        hid = P_hid[:, 0:(NE + 1) * 2 * NP].rearrange("p (e f t) -> p e f t", e=NE + 1, f=2)
        PT = [sb(f"PT{s}", [TT, W]) for s in range(2)]
        O = sb("O", [TT, 2, HQ, D])
        lg = sb("lg", [TT, 2, NE])
        lmax = sb("lmax", [TT, 2])
        el = sb("el", [TT, 2, NE])
        top = sb("top", [TT, 2, 8])
        topi = sb("topi", [TT, 2, 8], U32)
        topf = sb("topf", [TT, 2, 2])
        tsum = sb("tsum", [TT, 2])
        trec = sb("trec", [TT, 2])
        tw = sb("tw", [TT, 2, 2])
        oh = sb("oh", [TT, 2, 2, NE])
        gate = sb("gate", [TT, 2, NE])
        mo = sb("mo", [TT, 2, NE, D])
        mr = sb("mr", [TT, 2, D])
        qT = sb("qT", [D, NP])
        kmx = sb("kmx", [D, 1])
        ksum = sb("ksum", [D, 1])
        krec = sb("krec", [D, 1])
        eT = sb("eT", [D, NP])
        ek = sb("ek", [TT, 2, D])
        ctxs = sb("ctxs", [D, D])
        xgT = sb("xgT", [D, NP])
        hg = sb("hg", [GH, NP])
        g = sb("g", [TT, 2, D])
        ps = [ctx.enter_context(nc.psum_tensor(f"ps{s}", [128, 512], F32)) for s in range(4)]

        R = 2 * HV
        HG = 2
        offs = sb("offs", [TILE, HV, TOPK])
        iota = sb("iota", [TILE, NC])
        wk = sb("wk", [D, R * NK])
        xb = sb("xb", [TILE, D])
        xbT = sb("xbT", [D, TILE])
        sims = sb("sims", [TILE, 2 * R * NK])
        sim, sim2 = (sims[:, a * R * NK:(a + 1) * R * NK].rearrange("p (r k) -> p r k", r=R) for a in range(2))
        onehot = sims[:, 0:HG * TOPK * NC].rearrange("p (h k c) -> p h k c", h=HG, k=TOPK)
        ranks = sb("ranks", [TILE, R, TOPK], U32)
        half = [sb(f"half{p}", [TILE, 2, HV, TOPK]) for p in range(2)]
        pairs = sb("pairs", [TILE, 2, HV, NC])
        pairs2 = sb("pairs2", [TILE, HV, NC])
        best = sb("best", [TILE, HV, TOPK])
        place = sb("place", [TILE, HV, TOPK], U32)
        placef = sb("placef", [TILE, HV, TOPK])
        rowf = sb("rowf", [TILE, HV, TOPK])
        rows_at = [sb(f"rows_at{b}", [TILE, HV * TOPK], U32) for b in range(TRIP)]
        ex = sb("ex", [TILE, HV, TOPK])
        ssum = sb("ssum", [TILE, HV])
        weight = [sb(f"weight{b}", [TILE, HV, TOPK]) for b in range(TRIP)]
        G = [sb(f"G{s}", [TILE, TOPK * 2 * D]) for s in range(SLOTS)]
        wpkT = G[0][0:D // 2, 0:R * D].rearrange("p (r d) -> p r d", r=R)
        keysT = G[1][0:D // 2, 0:R * NK].rearrange("p (r k) -> p r k", r=R)
        kv_sum = sb("kv_sum", [TILE, 2, HV, D])
        ps_s = [ctx.enter_context(nc.psum_tensor(f"ps_s{p}", [128, 512], F32)) for p in range(2)]
        ps_kv = [ctx.enter_context(nc.psum_tensor(f"ps_kv{q}", [128, 512], F32)) for q in range(2)]

        x_in, wk_ps, wk_ready = sem("x_in"), sem("wk_ps"), sem("wk_ready")
        xT_ps, xT_ready, sim_ps, sim_in, rows_ready, shifted, exped, weight_ready = (
            sem("b_" + s) for s in ("xT_ps", "xT_ready", "sim_ps", "sim_in", "rows_ready", "shifted", "exped", "weight_ready"))
        landed = [sem(f"landed{hh}") for hh in range(HV)]
        weighed, summed = sem("weighed"), sem("summed")
        kv_ready = [sem(f"kv_ready{q}") for q in range(2)]
        kv_out = sem("kv_out")
        bstep = sem("b_vector_step")

        SETUP = 8
        consts_in, setup = sem("a_consts_in"), sem("a_setup")
        pix_in = [sem(f"pix_in{u}") for u in range(2)]
        rows_out = [sem(f"rows_out{u}") for u in range(2)]
        vstep = sem("a_vector_step")
        astep = sem("a_scalar_step")
        CONSTS = 16 * (len(shapes) + 2 + 4)
        met = (consts_in, CONSTS)
        S = {}
        NAMES = """emb_sum var1 rstd1 xn1 xT1_ps xT1 kv_ps kss krs kdup kT_ps kT q_ps q_rot q_sq qss rq s_ps nb p_ready
                   pt_ps pt_ready o_ps o_ready oT_ps oT_ready wo_ps var2 rstd2 xn2 xT2_ps xT2 lg_ps lmax el hid_ps hid_ready
                   moe_ps var3 rstd3 xn3 xT3_ps xT3 qkv_ps kmx ek_ready ek_ps ek lin_v ctx_ps ctx lin_ps var5 rstd5 xg xgT_ps xgT
                   hg_ps hg g_ps g_in g_exp og ogT_ps ogT proj_ps var4 rstd4 xn4""".split()
        for s in NAMES:
            S[s] = sem("a_" + s)

        def tok(t):
            return slice(t * TT, (t + 1) * TT)

        def unit_heads(n):
            return (0, 4 * n, 4) if n < QG else (1, 2 * (n - QG), 2)

        with nc.Block() as block:
            @block.sync
            def _(sp):
                for name in shapes:
                    sp.dma_start(k[name][:], c[name]).then_inc(consts_in, 16)
                for t in range(2):
                    sp.dma_start(P[:, t, :], c["mask"][t]).then_inc(consts_in, 16)
                for dst, name in ((wpkT, "wpkT"), (keysT, "keysT"), (offs[:], "offs"), (iota[:], "iota")):
                    sp.dma_start(dst, c[name]).then_inc(consts_in, 16)

                def pair(i):
                    for u in range(2):
                        sp.wait_ge(S["emb_sum"], i * 2)
                        sp.dma_start(pix[u][:], c["pixT"][bass.ds(2 * i + u, 1)].rearrange("o p k t -> (o p) k t")).then_inc(pix_in[u], 16)
                    for u in range(2):
                        for _ in range(STAGES - 1):
                            yield
                        sp.wait_ge(S["xn4"], i * 2 + u + 1)
                        for src, dst in ((h[u], h3_rows), (xn[u], xn4_rows)):
                            for t, rows in ((0, TT), (1, N - TT)):
                                sp.dma_start(dst[bass.ds((2 * i + u) * N + t * TT, rows), :], src[0:rows, t, :]).then_inc(rows_out[u], 16)
                        yield

                def front(t, b, i):
                    wait_apart(sp, rows_out[0], (i + 2) * 64 if b == 0 else (i + 1) * 64, met)
                    wait_apart(sp, rows_out[1], (i + 1) * 64, met)
                    sp.wait_ge(xT_ps, t)
                    sp.dma_start(xb[:], xn4_rows[bass.ds(t * TILE, TILE), :]).then_inc(x_in, 16)
                    for _ in range(PIECES):
                        yield

                def head(t, b, hh):
                    pass

                def after(t, b, hh):
                    if hh == HV - 1:
                        for q in range(2):
                            wait_apart(sp, kv_ready[q], t + 1, met)
                        sp.dma_start(kv_rows[bass.ds(t * TILE, TILE), :], kv_sum[:].rearrange("p a h d -> p (a h d)")).then_inc(kv_out, 16)

                schedule(sp, pair, front, head, after)
                sp.wait_ge(kv_out, 16 * NTILES)

            @block.tensor
            def _(pe):
                pe.wait_ge(consts_in, CONSTS)
                pe.wait_ge(setup, SETUP)

                for r in range(R):
                    mm = nc.tensor.matmul(ps_s[r // HV][0:D, (r % HV) * NK:(r % HV + 1) * NK], wpkT[:, r, :], keysT[:, r, :], start=True, stop=True)
                mm.then_inc(wk_ps, 1)
                pe.wait_ge(wk_ready, 1)

                def done(mm, name):
                    mm.then_inc(S[name], 1)

                def pair(i):
                    for u in range(2):
                        def need(name, per=1, n=0, met=None):
                            if met:
                                wait_apart(pe, S[name], i * (2 * per) + u * per + n + 1, met)
                            else:
                                pe.wait_ge(S[name], i * (2 * per) + u * per + n + 1)

                        def turn(src, name, ready, bank):
                            need(ready, met=met)
                            for t in range(2):
                                mm = nc.tensor.transpose(ps[bank][0:D, tok(t)], src[:, t, :], k["ident"][0:TT, 0:TT])
                            done(mm, name)

                        pe.wait_ge(pix_in[u], (i + 1) * 16)
                        for t in range(2):
                            for kc in range(KC):
                                mm = nc.tensor.matmul(ps[0][0:TT, t * D:(t + 1) * D], pix[u][:, kc, tok(t)], k["patch_w"][:, kc, :],
                                                      start=(kc == 0), stop=(kc == KC - 1))
                        done(mm, "emb_sum")
                        yield
                        turn(xn[u], "xT1_ps", "xn1", 1)
                        yield
                        need("xT1")
                        for t in range(2):
                            mm = nc.tensor.matmul(ps[0][0:TT, t * 3 * D:(t + 1) * 3 * D], xT[:, tok(t)], k["wkkv"][:], start=True, stop=True)
                        done(mm, "kv_ps")
                        for n in range(HQ // 2):
                            yield
                            if n >= 2:
                                need("q_sq", HQ // 2, n - 2)
                            for a in range(2):
                                mm = nc.tensor.matmul(ps[2 + n % 2][:, a * NP:(a + 1) * NP], k["wqq"][:, 2 * n + a, :], xT[:], start=True, stop=True)
                            done(mm, "q_ps")
                        yield
                        need("kdup")
                        for t in range(2):
                            mm = nc.tensor.transpose(ps[1][:, tok(t)], kdup[:, t].rearrange("p a d -> p (a d)"), k["ident"][0:TT, 0:TT])
                        done(mm, "kT_ps")
                        need("q_sq", HQ // 2, HQ // 2 - 1)
                        for t in range(2):
                            for hh in range(HQ):
                                mm = nc.tensor.matmul(ps[0][0:TT, t * HQ + hh:t * HQ + hh + 1], qsq[:, hh, tok(t)], ones[:], start=True, stop=True)
                        done(mm, "qss")

                        def scores(n):
                            t, h0, nh = unit_heads(n)
                            if n == 0:
                                need("kT")
                                need("q_rot", HQ // 2, HQ // 2 - 1)
                            if n >= 2:
                                need("p_ready", UNITS, n - 2)
                            bank = ps[2 + n % 2]
                            nc.tensor.matmul(bank[0:TT, 0:W], ident_b[0:TT, 0:TT], mask[t][:], start=True, stop=False)
                            w = (t + 1) * TT
                            for a in range(nh):
                                mm = nc.tensor.matmul(bank[0:TT, a * w:(a + 1) * w], qr[:, h0 + a, tok(t)], kT[:, 0:w], start=False, stop=(a == nh - 1))
                            done(mm, "s_ps")

                        def turn_p(n):
                            need("p_ready", UNITS, n)
                            if n >= 1:
                                need("pt_ready", UNITS, n - 1)
                            else:
                                need("rq")
                            for a in range(4):
                                mm = nc.tensor.transpose(ps[0][0:TT, a * TT:(a + 1) * TT], P[:, n, a * TT:(a + 1) * TT], k["ident"][0:TT, 0:TT])
                            done(mm, "pt_ps")

                        def values(n):
                            t, h0, nh = unit_heads(n)
                            need("pt_ready", UNITS, n)
                            if h0 % 8 == 0 and n:
                                need("o_ready", 4, t * 2 + h0 // 8 - 1)
                            if n == 0:
                                need("kT")
                            for a in range(nh):
                                o = ps[1][0:TT, (h0 + a) % 8 * D:((h0 + a) % 8 + 1) * D]
                                for s in range(t + 1):
                                    col = (a * (t + 1) + s) * TT
                                    mm = nc.tensor.matmul(o, PT[n % 2][:, col:col + TT], v[:, s, :], start=(s == 0), stop=(s == t))
                            done(mm, "o_ps")

                        for n in range(UNITS + 2):
                            yield
                            if n < UNITS:
                                scores(n)
                            if 1 <= n <= UNITS:
                                turn_p(n - 1)
                            if n >= 2:
                                values(n - 2)
                        yield
                        for n in range(4):
                            if n % 2 == 0:
                                need("o_ready", 4, 1 + n)
                            if n >= 2:
                                need("oT_ready", 4, n - 2)
                            flat = O[:, n // 2].rearrange("p h d -> p (h d)")
                            for a in range(4):
                                ch = (n % 2) * 4 + a
                                mm = nc.tensor.transpose(ps[2 + n % 2][:, a * TT:(a + 1) * TT], flat[:, ch * 128:(ch + 1) * 128], k["ident"][0:TT, 0:TT])
                            done(mm, "oT_ps")
                        yield
                        need("oT_ready", 4, 3)
                        for t in range(2):
                            for ch in range(8):
                                mm = nc.tensor.matmul(ps[0][0:TT, t * D:(t + 1) * D], OT[:, 2 * t + ch // 4, (ch % 4) * TT:(ch % 4 + 1) * TT],
                                                      k["wo"][:, ch, :], start=(ch == 0), stop=(ch == 7))
                        done(mm, "wo_ps")
                        yield
                        turn(xn[u], "xT2_ps", "xn2", 1)
                        yield
                        need("xT2")
                        for t in range(2):
                            mm = nc.tensor.matmul(ps[0][0:TT, t * NE:(t + 1) * NE], xT[:, tok(t)], k["wr"][:], start=True, stop=True)
                        done(mm, "lg_ps")
                        for e in range(NE + 1):
                            if e:
                                yield
                            if e >= 2:
                                need("hid_ready", NE + 1, e - 2)
                            for f in range(2):
                                mm = nc.tensor.matmul(ps[2 + e % 2][:, f * NP:(f + 1) * NP], k["w1"][:, e, f * 128:(f + 1) * 128], xT[:], start=True, stop=True)
                            done(mm, "hid_ps")
                        yield
                        need("hid_ready", NE + 1, NE)
                        for t in range(2):
                            for e in range(NE + 1):
                                out = ps[2 + t][0:TT, e * D:(e + 1) * D] if e < NE else ps[1][0:TT, t * D:(t + 1) * D]
                                for f in range(2):
                                    mm = nc.tensor.matmul(out, hid[:, e, f, tok(t)], k["w2"][:, e, f, :], start=(f == 0), stop=(f == 1))
                        done(mm, "moe_ps")
                        yield
                        yield
                        turn(xn[u], "xT3_ps", "xn3", 0)
                        yield
                        need("xT3", met=met)
                        for a in range(2):
                            nc.tensor.matmul(ps[1][0:D, a * NP:(a + 1) * NP], k["wqkv"][:, a * D:(a + 1) * D], xT[:], start=True, stop=True)
                        for t in range(2):
                            mm = nc.tensor.matmul(ps[2][0:TT, t * D:(t + 1) * D], xT[:, tok(t)], k["wqkv"][:, 2 * D:3 * D], start=True, stop=True)
                        done(mm, "qkv_ps")
                        yield
                        turn(g, "xgT_ps", "xg", 0)
                        yield
                        need("xgT", met=met)
                        done(nc.tensor.matmul(ps[3][0:GH, 0:NP], k["wg1"][:], xgT[:], start=True, stop=True), "hg_ps")
                        need("ek_ready", met=met)
                        need("lin_v", met=met)
                        for t in range(2):
                            mm = nc.tensor.transpose(ps[2][0:TT, t * D:(t + 1) * D], eT[:, tok(t)], k["ident"][0:D, 0:D])
                        done(mm, "ek_ps")
                        yield
                        need("ek")
                        for t in range(2):
                            mm = nc.tensor.matmul(ps[0][0:D, 0:D], ek[:, t, :], v[:, t, :], start=(t == 0), stop=(t == 1))
                        done(mm, "ctx_ps")
                        need("ctx")
                        for t in range(2):
                            mm = nc.tensor.matmul(ps[1][0:TT, t * D:(t + 1) * D], qT[:, tok(t)], ctxs[:], start=True, stop=True)
                        done(mm, "lin_ps")
                        need("hg")
                        for t in range(2):
                            mm = nc.tensor.matmul(ps[2][0:TT, t * D:(t + 1) * D], hg[:, tok(t)], k["wg2"][:], start=True, stop=True)
                        done(mm, "g_ps")
                        yield
                        turn(g, "ogT_ps", "og", 3)
                        yield
                        need("ogT")
                        for t in range(2):
                            mm = nc.tensor.matmul(ps[2][0:TT, t * D:(t + 1) * D], xgT[:, tok(t)], k["wproj"][:], start=True, stop=True)
                        done(mm, "proj_ps")
                        yield
                        yield

                def front(t, b, i):
                    yield
                    wait_apart(pe, x_in, 16 * (t + 1), met)
                    wait_apart(pe, sim_in, t, met)
                    nc.tensor.transpose(ps_s[0][0:D, 0:TILE], xb[:], k["ident"][:]).then_inc(xT_ps, 1)
                    yield
                    pe.wait_ge(xT_ready, t + 1)
                    for p in range(2):
                        mm = nc.tensor.matmul(ps_s[p][:], xbT[:], wk[:, p * 512:(p + 1) * 512], start=True, stop=True)
                    mm.then_inc(sim_ps, 1)
                    for _ in range(PIECES - 2):
                        yield

                def head(t, b, hh):
                    pass

                def after(t, b, hh):
                    pe.wait_ge(weighed, t * HV + hh + 1)
                    if hh % 4 == 0:
                        pe.wait_ge(kv_ready[hh // 4], t)
                    for j in range(TOPK):
                        mm = nc.tensor.matmul(ps_kv[hh // 4][:, (hh % 4) * 128:(hh % 4 + 1) * 128], k["ident"][:], G[hh % SLOTS][:, j * 128:(j + 1) * 128],
                                              start=(j == 0), stop=(j == TOPK - 1))
                    mm.then_inc(summed, 1)

                schedule(pe, pair, front, head, after)

            @block.scalar
            def _(act):
                act.wait_ge(consts_in, CONSTS)
                act.wait_ge(setup, SETUP)
                act.preload_act_table_set(EXP_LN)
                act.wait_ge(wk_ps, 1)
                for p in range(2):
                    a = nc.scalar.activation(wk[:, p * 512:(p + 1) * 512], ps_s[p][0:D, :], ACT.Copy)
                a.then_inc(wk_ready, 1)

                def pair(i):
                    own = Chain(act, astep, i, A_ACT_STEPS)

                    for u in range(2):
                        def need(name, per=1, n=0, met=None):
                            if met:
                                wait_apart(act, S[name], i * (2 * per) + u * per + n + 1, met)
                            else:
                                act.wait_ge(S[name], i * (2 * per) + u * per + n + 1)

                        def inv_root(src, dst, name, ready, scale, bias):
                            need(ready)
                            tmp = logs[:, 0:src.free_size()]
                            own.link(nc.scalar.activation(tmp, src, ACT.Ln, scale=scale, bias=bias[:, 0:1]))
                            nc.scalar.activation(dst, tmp, ACT.Exp, scale=-0.5).then_inc(S[name], 1)

                        def ln_root(j):
                            inv_root(mv[:, :, 1], rstd[:], f"rstd{j}", f"var{j}", 1.0, eps_ln)

                        ln_root(1)
                        yield
                        yield
                        yield
                        inv_root(kss[:], krs[:], "krs", "kss", 1.0 / D, eps_rms)
                        for n in range(HQ // 2):
                            yield
                            need("q_rot", HQ // 2, n)
                            nc.scalar.activation(qsq[:, 2 * n:2 * n + 2, :].rearrange("p a t -> p (a t)"), ps[2 + n % 2][0:D, 0:2 * NP], ACT.Square).then_inc(S["q_sq"], 1)
                        inv_root(ps[0][0:TT, 0:2 * HQ], rq[:].rearrange("p t h -> p (t h)"), "rq", "qss", 1.0 / D, eps_rms)

                        def exps(n):
                            t, h0, nh = unit_heads(n)
                            need("nb", UNITS, n)
                            need("rq")
                            w = (t + 1) * TT
                            for a in range(nh):
                                hh = h0 + a
                                e = nc.scalar.activation(P[:, n, a * w:(a + 1) * w], ps[2 + n % 2][0:TT, a * w:(a + 1) * w], ACT.Exp,
                                                         scale=rq[:, t, hh:hh + 1], bias=nb[:, t, hh:hh + 1], accum_out=den[:, t, hh:hh + 1])
                            e.then_inc(S["p_ready"], 1)

                        def copy_pt(n):
                            need("pt_ps", UNITS, n)
                            if n >= 2:
                                need("o_ps", UNITS, n - 2)
                            nc.scalar.activation(PT[n % 2][:], ps[0][0:TT, 0:W], ACT.Copy).then_inc(S["pt_ready"], 1)

                        for n in range(UNITS + 1):
                            yield
                            if n < UNITS:
                                exps(n)
                            if n >= 1:
                                copy_pt(n - 1)
                        yield
                        yield
                        for n in range(4):
                            need("oT_ps", 4, n)
                            nc.scalar.activation(OT[:, n, :], ps[2 + n % 2][:, 0:W], ACT.Copy).then_inc(S["oT_ready"], 1)
                        yield
                        ln_root(2)
                        yield
                        yield
                        need("lmax")
                        nc.scalar.activation(el[:], lg[:], ACT.Exp).then_inc(S["el"], 1)
                        for e in range(NE + 1):
                            yield
                            need("hid_ps", NE + 1, e)
                            for f in range(2):
                                last = nc.scalar.activation(hid[:, e, f, :], ps[2 + e % 2][:, f * NP:(f + 1) * NP], ACT.Gelu, bias=k["b1"][:, e, f:f + 1])
                            last.then_inc(S["hid_ready"], 1)
                        yield
                        act.preload_act_table_set(EXP_LN)
                        ln_root(3)
                        yield
                        yield
                        ln_root(5)
                        yield
                        need("kmx")
                        nc.scalar.activation(eT[:, 0:N], ps[1][0:D, NP:NP + N], ACT.Exp, bias=kmx[:, 0:1], accum_out=ksum[:, 0:1]).then_inc(S["ek_ready"], 1)
                        yield
                        need("hg_ps")
                        nc.scalar.activation(hg[:], ps[3][0:GH, 0:NP], ACT.Gelu, bias=k["bg1"][:, 0:1]).then_inc(S["hg"], 1)
                        act.preload_act_table_set(EXP_LN)
                        yield
                        need("g_in")
                        nc.scalar.activation(g[:], g[:], ACT.Exp, scale=-1.0).then_inc(S["g_exp"], 1)
                        yield
                        yield
                        yield
                        ln_root(4)
                        yield
                    own.close()

                def front(t, b, i):
                    yield
                    act.wait_ge(xT_ps, t + 1)
                    nc.scalar.activation(xbT[:], ps_s[0][0:D, 0:TILE], ACT.Copy).then_inc(xT_ready, 1)
                    for _ in range(2):
                        yield
                    act.wait_ge(sim_ps, t + 1)
                    act.wait_ge(rows_ready, t)
                    for p in range(2):
                        a = nc.scalar.activation(sim[:, p * HV:(p + 1) * HV, :].rearrange("p r k -> p (r k)"), ps_s[p][:], ACT.Copy)
                    a.then_inc(sim_in, 1)
                    for _ in range(19):
                        yield
                    act.wait_ge(shifted, t + 1)
                    nc.scalar.activation(ex[:], ex[:], ACT.Exp).then_inc(exped, 1)
                    for _ in range(PIECES - 22):
                        yield

                def head(t, b, hh):
                    pass

                def after(t, b, hh):
                    if hh in (HV // 2 + 1, HV - 1):
                        q = 0 if hh < HV - 1 else 1
                        act.wait_ge(summed, SLOTS + HV * t + 4 * (q + 1))
                        act.wait_ge(kv_out, 16 * t)
                        nc.scalar.activation(kv_sum[:, :, 4 * q:4 * q + 4, :], ps_kv[q][:].rearrange("p (h a d) -> p a h d", h=4, a=2), ACT.Copy).then_inc(kv_ready[q], 1)

                schedule(act, pair, front, head, after)

            @block.gpsimd
            def _(pool):
                pool.sem_inc(summed, SLOTS)

                def pair(i):
                    for _ in range(2 * STAGES):
                        yield

                def front(t, b, i):
                    for _ in range(PIECES):
                        yield

                def head(t, b, hh):
                    if hh == 0:
                        pool.wait_ge(rows_ready, t + 1)
                    wait_apart(pool, summed, t * HV + hh + 1, met)
                    for j in range(TOPK):
                        pool.indirect_dma_start(G[hh % SLOTS][:, j * 128:(j + 1) * 128], None, c["table"],
                                                bass.IndirectOffsetOnAxis(ap=rows_at[b][:, hh * TOPK + j:hh * TOPK + j + 1], axis=0)).then_inc(landed[hh], 16)

                def after(t, b, hh):
                    pass

                schedule(pool, pair, front, head, after)

            @block.vector
            def _(dve):
                dve.wait_ge(consts_in, CONSTS)
                nc.vector.memset(ones[:], 1.0).then_inc(setup, 1)
                for t in range(2):
                    nc.vector.tensor_copy(mask[t][:], P[:, t, :]).then_inc(setup, 1)
                nc.vector.tensor_copy(ident_b[:], k["ident"][:]).then_inc(setup, 1)
                nc.vector.memset(eps_ln[:], LN_EPS).then_inc(setup, 1)
                nc.vector.memset(eps_rms[:], RMS_EPS).then_inc(setup, 1)
                nc.vector.memset(eT[:], 0.0).then_inc(setup, 1)
                nc.vector.scalar_tensor_tensor(out=knq[:], in0=k["qnw"][:], scalar=D ** -0.5, in1=k["knw"][:], op0=ALU.mult, op1=ALU.mult).then_inc(setup, 1)
                dve.wait_ge(setup, SETUP)
                def pair(i):
                    own = Chain(dve, vstep, i, A_STEPS)

                    for u in range(2):
                        def need(name, per=1, n=0, met=None):
                            if met:
                                wait_apart(dve, S[name], i * (2 * per) + u * per + n + 1, met)
                            else:
                                dve.wait_ge(S[name], i * (2 * per) + u * per + n + 1)

                        def ln_stats(src, j):
                            for t in range(2):
                                own.step(nc.vector.bn_stats(stats[:, t, :], src[:, t, :]))
                            own.wait(met)
                            nc.vector.bn_aggr(mv[:, 0, :], stats[:, 0, :])
                            nc.vector.bn_aggr(mv[:, 1, :], stats[:, 1, :]).then_inc(S[f"var{j}"], 1)

                        def ln_apply(src, dst, j, ready):
                            need(f"rstd{j}")
                            need(f"var{j}")
                            nc.vector.tensor_scalar(dst[:, 0, :], src[:, 0, :], mv[:, 0, 0:1], rstd[:, 0:1], ALU.subtract, ALU.mult)
                            nc.vector.tensor_scalar(dst[:, 1, :], src[:, 1, :], mv[:, 1, 0:1], rstd[:, 1:2], ALU.subtract, ALU.mult).then_inc(S[ready], 1)

                        def copy_xT(j, bank):
                            need(f"xT{j}_ps")
                            nc.vector.tensor_copy(xT[:], ps[bank][0:D, 0:NP]).then_inc(S[f"xT{j}"], 1)

                        need("emb_sum")
                        dve.wait_ge(rows_out[u], i * 64)
                        own.link(nc.vector.tensor_tensor(h[u][:], ps[0][0:TT, 0:2 * D].rearrange("p (t d) -> p t d", t=2), k["embed_add"][:], ALU.add))
                        ln_stats(h[u], 1)
                        yield
                        ln_apply(h[u], xn[u], 1, "xn1")
                        yield
                        copy_xT(1, 1)

                        def rotate_q(n):
                            need("q_ps", HQ // 2, n)
                            nc.vector.tensor_tensor(qr[:, 2 * n:2 * n + 2, :], ps[2 + n % 2][:, 0:2 * NP].rearrange("p (a t) -> p a t", a=2),
                                                    bcast(k["rope_q"][:], 1, [2 * D, 2, NP]), ALU.mult).then_inc(S["q_rot"], 1)
                        yield
                        need("kv_ps")
                        kv = ps[0][0:TT, 0:6 * D].rearrange("p (t d) -> p t d", t=2)
                        own.step(nc.vector.tensor_tensor(kk[:], kv[:, :, 0:2 * D], k["rope_k"][:], ALU.mult))
                        own.link(nc.vector.tensor_copy(v[:], kv[:, :, 2 * D:3 * D]))
                        own.link(nc.vector.tensor_tensor(kr[:], kk[:, :, 0:D], kk[:, :, D:2 * D], ALU.add))
                        own.link(nc.vector.tensor_tensor(ksq[:], kr[:], kr[:], ALU.mult))
                        nc.vector.tensor_reduce(kss[:], ksq[:], AX.X, ALU.add).then_inc(S["kss"], 1)
                        yield
                        rotate_q(0)
                        yield
                        rotate_q(1)
                        need("krs")
                        for t in range(2):
                            own.step(nc.vector.tensor_scalar(kr[:, t, :], kr[:, t, :], krs[:, t:t + 1], None, ALU.mult))
                        own.wait()
                        own.step(nc.vector.tensor_tensor(kdup[:, :, 0, :], kr[:], bcast(knq[:], 1, [TT, 2, D]), ALU.mult))
                        nc.vector.tensor_tensor(kdup[:, :, 1, :], kr[:], bcast(knq[:], 1, [TT, 2, D]), ALU.mult).then_inc(S["kdup"], 1)
                        for n in range(2, HQ // 2):
                            yield
                            rotate_q(n)
                        need("kT_ps")
                        nc.vector.tensor_copy(kT[:], ps[1][:, 0:NP]).then_inc(S["kT"], 1)

                        def unit_max(n):
                            t, h0, nh = unit_heads(n)
                            need("s_ps", UNITS, n)
                            own.link(nc.vector.tensor_reduce(m[:, t, h0:h0 + nh], ps[2 + n % 2][0:TT, 0:W].rearrange("p (a s) -> p a s", a=nh), AX.X, ALU.max))
                            if n == 0:
                                need("rq")
                            nc.vector.scalar_tensor_tensor(out=nb[:, t, h0:h0 + nh], in0=m[:, t, h0:h0 + nh], scalar=-1.0, in1=rq[:, t, h0:h0 + nh],
                                                           op0=ALU.mult, op1=ALU.mult).then_inc(S["nb"], 1)

                        def scale_o(n):
                            t, h0, nh = unit_heads(n)
                            h8 = h0 // 8 * 8
                            need("o_ps", UNITS, n)
                            own.link(nc.vector.reciprocal(rden[:, t, h8:h8 + 8], den[:, t, h8:h8 + 8]))
                            nc.vector.tensor_tensor(O[:, t, h8:h8 + 8, :], ps[1][0:TT, :].rearrange("p (a d) -> p a d", a=8),
                                                    bcast(rden[:, t, h8:h8 + 8], 2, [TT, 8, D]), ALU.mult).then_inc(S["o_ready"], 1)

                        for n in range(UNITS + 2):
                            yield
                            if n < UNITS:
                                unit_max(n)
                            if n >= 2:
                                t, h0, nh = unit_heads(n - 2)
                                if (h0 + nh) % 8 == 0:
                                    scale_o(n - 2)
                        yield
                        yield
                        need("wo_ps")
                        own.link(nc.vector.tensor_tensor(h[u][:], ps[0][0:TT, 0:2 * D].rearrange("p (t d) -> p t d", t=2), h[u][:], ALU.add))
                        ln_stats(h[u], 2)
                        yield
                        ln_apply(h[u], xn[u], 2, "xn2")
                        yield
                        copy_xT(2, 1)
                        need("lg_ps")
                        l2 = ps[0][0:TT, 0:2 * NE].rearrange("p (t e) -> p t e", t=2)
                        own.link(nc.vector.tensor_reduce(lmax[:], l2, AX.X, ALU.max))
                        nc.vector.tensor_tensor(lg[:], l2, bcast(lmax[:], 2, [TT, 2, NE]), ALU.subtract).then_inc(S["lmax"], 1)
                        yield
                        need("el", met=met)
                        for t in range(2):
                            own.step(nc.vector.max(top[:, t, :], el[:, t, :]))
                        own.wait(met)
                        for t in range(2):
                            own.step(nc.vector.max_index(topi[:, t, :], top[:, t, :], el[:, t, :]))
                        own.link(nc.vector.tensor_tensor(tsum[:], top[:, :, 0], top[:, :, 1], ALU.add))
                        own.step(nc.vector.tensor_copy(topf[:], topi[:, :, 0:2]))
                        own.link(nc.vector.reciprocal(trec[:], tsum[:]))
                        own.step(nc.vector.tensor_tensor(tw[:], top[:, :, 0:2], bcast(trec[:], 2, [TT, 2, 2]), ALU.mult))
                        for t in range(2):
                            own.step(nc.vector.tensor_tensor(oh[:, t], bcast(k["iota8"][:], 1, [TT, 2, NE]), bcast(topf[:, t, :], 2, [TT, 2, NE]), ALU.is_equal))
                        own.wait()
                        own.link(nc.vector.tensor_tensor(oh[:], oh[:], bcast(tw[:], 3, [TT, 2, 2, NE]), ALU.mult))
                        own.step(nc.vector.tensor_tensor(gate[:], oh[:, :, 0, :], oh[:, :, 1, :], ALU.add))
                        own.wait(met)
                        yield
                        yield
                        yield
                        yield
                        yield
                        yield
                        yield
                        yield
                        yield
                        need("moe_ps")
                        for t in range(2):
                            own.step(nc.vector.tensor_tensor(mo[:, t], ps[2 + t][0:TT, :].rearrange("p (e d) -> p e d", e=NE), k["b2p"][:], ALU.add))
                        own.step(nc.vector.tensor_tensor(h[u][:], ps[1][0:TT, 0:2 * D].rearrange("p (t d) -> p t d", t=2), h[u][:], ALU.add))
                        own.wait()
                        own.step(nc.vector.tensor_tensor(h[u][:], h[u][:], bcast(k["b2s"][:], 1, [TT, 2, D]), ALU.add))
                        for t in range(2):
                            own.step(nc.vector.tensor_tensor(mo[:, t], mo[:, t], bcast(gate[:, t, :], 2, [TT, NE, D]), ALU.mult))
                        own.wait()
                        own.link(nc.vector.tensor_reduce(mr[:], mo[:].rearrange("p t e d -> p t d e"), AX.X, ALU.add))
                        own.link(nc.vector.tensor_tensor(h[u][:], h[u][:], mr[:], ALU.add))
                        ln_stats(h[u], 3)
                        yield
                        ln_apply(h[u], xn[u], 3, "xn3")
                        yield
                        copy_xT(3, 0)
                        ln_stats(xn[u], 5)
                        yield
                        need("qkv_ps")
                        own.step(nc.vector.tensor_copy(qT[:], ps[1][0:D, 0:NP]))
                        own.link(nc.vector.tensor_reduce(kmx[:], ps[1][0:D, NP:NP + N], AX.X, ALU.max))
                        nc.vector.tensor_scalar(kmx[:], kmx[:], -1.0, None, ALU.mult).then_inc(S["kmx"], 1)
                        nc.vector.tensor_copy(v[:], ps[2][0:TT, 0:2 * D].rearrange("p (t d) -> p t d", t=2)).then_inc(S["lin_v"], 1)
                        ln_apply(xn[u], g, 5, "xg")
                        yield
                        need("xgT_ps")
                        nc.vector.tensor_scalar(xgT[:], ps[0][0:D, 0:NP], k["lng"][:, 0:1], k["lnb"][:, 0:1], ALU.mult, ALU.add).then_inc(S["xgT"], 1)
                        need("ek_ps")
                        nc.vector.tensor_copy(ek[:], ps[2][0:TT, 0:2 * D].rearrange("p (t d) -> p t d", t=2)).then_inc(S["ek"], 1)
                        own.step(nc.vector.reciprocal(krec[:], ksum[:]))
                        own.wait(met)
                        yield
                        need("ctx_ps")
                        nc.vector.scalar_tensor_tensor(out=ctxs[:], in0=ps[0][0:D, 0:D], scalar=krec[:, 0:1], in1=k["blocks"][:],
                                                       op0=ALU.mult, op1=ALU.mult).then_inc(S["ctx"], 1)
                        need("g_ps")
                        nc.vector.tensor_tensor(g[:], ps[2][0:TT, 0:2 * D].rearrange("p (t d) -> p t d", t=2), bcast(k["bg2"][:], 1, [TT, 2, D]), ALU.add).then_inc(S["g_in"], 1)
                        yield
                        need("g_exp")
                        own.link(nc.vector.tensor_scalar(g[:], g[:], 1.0, None, ALU.add))
                        own.link(nc.vector.reciprocal(g[:], g[:]))
                        need("lin_ps")
                        nc.vector.tensor_tensor(g[:], ps[1][0:TT, 0:2 * D].rearrange("p (t d) -> p t d", t=2), g[:], ALU.mult).then_inc(S["og"], 1)
                        yield
                        need("ogT_ps")
                        nc.vector.tensor_copy(xgT[:], ps[3][0:D, 0:NP]).then_inc(S["ogT"], 1)
                        own.step(nc.vector.tensor_tensor(h[u][:], h[u][:], bcast(k["bproj"][:], 1, [TT, 2, D]), ALU.add))
                        own.wait(met)
                        yield
                        need("proj_ps")
                        own.link(nc.vector.tensor_tensor(h[u][:], ps[2][0:TT, 0:2 * D].rearrange("p (t d) -> p t d", t=2), h[u][:], ALU.add))
                        ln_stats(h[u], 4)
                        ln_apply(h[u], xn[u], 4, "xn4")
                        yield
                    own.close()

                def front(t, b, i):
                    own = Chain(dve, bstep, t, FRONT_STEPS)
                    for _ in range(4):
                        yield
                    wait_apart(dve, sim_in, t + 1, met)
                    val = [half[p][:, 0] for p in range(2)]
                    for a in range(2):
                        src = sim if a == 0 else sim2
                        cols = slice(8 * a, 8 * a + 8)
                        for r in range(R):
                            own.step(nc.vector.max(val[r // HV][:, r % HV, cols], src[:, r, :]))
                            if r == HV - 1:
                                yield
                        yield
                        own.wait(met)
                        for r in range(R):
                            own.step(nc.vector.max_index(ranks[:, r, cols], val[r // HV][:, r % HV, cols], src[:, r, :]))
                            if r == HV - 1:
                                yield
                        yield
                        if a == 0:
                            for r in range(R):
                                own.step(nc.vector.match_replace(sim2[:, r, :], val[r // HV][:, r % HV, cols], sim[:, r, :], LOWEST))
                                if r == HV - 1:
                                    yield
                            yield
                        own.wait(met if a == 0 else None)
                    own.step(nc.vector.tensor_copy(half[0][:, 1], ranks[:, 0:HV, :]))
                    own.link(nc.vector.scalar_tensor_tensor(out=half[1][:, 1].rearrange("p h k -> p (h k)"), in0=ranks[:, HV:R, :].rearrange("p h k -> p (h k)"), scalar=float(NK),
                                                            in1=offs[:].rearrange("p h k -> p (h k)"), op0=ALU.mult, op1=ALU.add))
                    yield
                    f0 = half[0][:].rearrange("p a h k -> p (a h) k")
                    f1 = half[1][:].rearrange("p a h k -> p (a h) k")
                    pr = pairs[:].rearrange("p a h k -> p (a h) k")
                    at = r0 = 0
                    while r0 < TOPK:
                        n = CUTS[r0]
                        rn = CUTS.count(n)
                        out = pr[:, :, at:at + rn * n].rearrange("p g (r n) -> p g r n", r=rn)
                        own.step(nc.vector.tensor_tensor(out, f0[:, :, r0:r0 + rn].unsqueeze(3).to_broadcast([TILE, R, rn, n]),
                                                         f1[:, :, 0:n].unsqueeze(2).to_broadcast([TILE, R, rn, n]), ALU.add))
                        at += rn * n
                        r0 += rn
                    yield
                    own.wait(met)
                    for a in range(2):
                        src = pairs[:, 0] if a == 0 else pairs2[:]
                        cols = slice(8 * a, 8 * a + 8)
                        for hh in range(HV):
                            own.step(nc.vector.max(best[:, hh, cols], src[:, hh, :]))
                        yield
                        own.wait(met)
                        for hh in range(HV):
                            own.step(nc.vector.max_index(place[:, hh, cols], best[:, hh, cols], src[:, hh, :]))
                        if a == 0:
                            yield
                            for hh in range(HV):
                                own.step(nc.vector.match_replace(pairs2[:, hh, :], best[:, hh, cols], pairs[:, 0, hh, :], LOWEST))
                            yield
                        own.wait(met if a == 0 else None)
                    yield
                    own.step(nc.vector.tensor_copy(placef[:], place[:]))
                    nc.vector.tensor_tensor(ex[:], best[:], best[:, :, 0:1].to_broadcast([TILE, HV, TOPK]), ALU.subtract).then_inc(shifted, 1)
                    own.wait()
                    for g0 in range(0, HV, HG):
                        gh = slice(g0, g0 + HG)
                        own.link(nc.vector.tensor_tensor(onehot.rearrange("p h k c -> p (h k) c"), iota[:].unsqueeze(1).to_broadcast([TILE, HG * TOPK, NC]),
                                                         placef[:, gh, :].rearrange("p h k -> p (h k)").unsqueeze(2).to_broadcast([TILE, HG * TOPK, NC]), ALU.is_equal))
                        yield
                        own.link(nc.vector.tensor_tensor(onehot, onehot, pairs[:, 1, gh, :].unsqueeze(2).to_broadcast([TILE, HG, TOPK, NC]), ALU.mult))
                        own.link(nc.vector.tensor_reduce(rowf[:, gh, :], onehot, AX.X, ALU.add))
                        if g0 + HG < HV:
                            yield
                    nc.vector.tensor_copy(rows_at[b][:], rowf[:].rearrange("p h k -> p (h k)")).then_inc(rows_ready, 1)
                    yield
                    dve.wait_ge(exped, t + 1)
                    own.link(nc.vector.tensor_reduce(ssum[:], ex[:], AX.X, ALU.add))
                    own.link(nc.vector.reciprocal(ssum[:], ssum[:]))
                    nc.vector.tensor_tensor(weight[b][:], ex[:], ssum[:].unsqueeze(2).to_broadcast([TILE, HV, TOPK]), ALU.mult).then_inc(weight_ready, 1)
                    own.close()
                    for _ in range(3):
                        yield

                def head(t, b, hh):
                    if hh == 0:
                        dve.wait_ge(weight_ready, t + 1)
                    dve.wait_ge(landed[hh], (t + 1) * (16 * TOPK))
                    rows = G[hh % SLOTS][:].rearrange("p (k d) -> p k d", k=TOPK)
                    nc.vector.tensor_tensor(rows, rows, weight[b][:, hh, :].unsqueeze(2).to_broadcast([TILE, TOPK, 2 * D]), ALU.mult).then_inc(weighed, 1)

                def after(t, b, hh):
                    pass

                schedule(dve, pair, front, head, after)

C_STEPS = 16


def readout_phase(nc, c, h3_rows, xn4_rows, kv_rows, out):
    UT = HV // 4
    UNITS = UT + HV // 2
    W = 4 * TT
    with ExitStack() as ctx:
        def sb(name, shape, dt=F32):
            return ctx.enter_context(nc.sbuf_tensor("r_" + name, shape, dt))

        def two(name, shape, dt=F32):
            return [sb(f"{name}{u}", shape, dt) for u in range(2)]

        ident = sb("ident", [128, 128])
        ident_b = sb("ident_b", [128, 128], BF16)
        mask = [sb(f"mask{t}", [TT, W], BF16) for t in range(2)]
        wq = sb("wq", [D, HV * D])
        wo = sb("wo", [128, HV * D // 128, D])
        h = two("h", [TT, 2, D])
        x = two("x", [TT, 2, D])
        kv = two("kv", [TT, 2, 2, HV * D])
        xT = two("xT", [D, NP])
        qT = two("qT", [D, HV, NP])
        kT = two("kT", [D, HV, NP])
        m = two("m", [TT, 2, HV])
        nb = two("nb", [TT, 2, HV])
        den = two("den", [TT, 2, HV])
        rden = two("rden", [TT, 2, HV])
        P = two("P", [TT, UNITS, W])
        PT = [[sb(f"PT{u}_{s}", [TT, W]) for s in range(2)] for u in range(2)]
        O = two("O", [TT, 2, HV, D])
        OT = two("OT", [128, 2, W])
        y = two("y", [TT, 2, D])
        ps = [[ctx.enter_context(nc.psum_tensor(f"psr{u}_{s}", [128, 512], F32)) for s in range(4)] for u in range(2)]
        consts_in = ctx.enter_context(nc.semaphore("c_consts_in"))
        setup = ctx.enter_context(nc.semaphore("c_setup"))
        rows_in = [ctx.enter_context(nc.semaphore(f"c_rows_in{u}")) for u in range(2)]
        rows_out = [ctx.enter_context(nc.semaphore(f"c_rows_out{u}")) for u in range(2)]
        vstep = ctx.enter_context(nc.semaphore("c_vector_step"))
        S = {s: ctx.enter_context(nc.semaphore("c_" + s)) for s in
             "xT_ps xT q_ps qT k_ps kT s_ps nb p_ready pt_ps pt_ready o_ps o_ready oT_ps oT_ready wo_ps y".split()}

        met = (consts_in, 16 * 5)

        def tok(t):
            return slice(t * TT, (t + 1) * TT)

        def unit_heads(n):
            return (0, 4 * n, 4) if n < UT else (1, 2 * (n - UT), 2)

        with nc.Block() as block:
            @block.sync
            def _(sp):
                for dst, name in ((ident, "ident"), (wq, "wq_mem"), (wo, "wo_mem")):
                    sp.dma_start(dst[:], c[name]).then_inc(consts_in, 16)
                for t in range(2):
                    sp.dma_start(P[0][:, t, :], c["causal"][t]).then_inc(consts_in, 16)
                with sp.Fori(0, B // 2) as i:
                    for u in range(2):
                        sp.wait_ge(S["y"], i * 2)
                        for dst, src in ((h[u][:], h3_rows), (x[u][:], xn4_rows), (kv[u][:].rearrange("p t a f -> p t (a f)"), kv_rows)):
                            sp.dma_start(dst, src[bass.ds((2 * i + u) * N, NP), :].rearrange("(t p) f -> p t f", t=2)).then_inc(rows_in[u], 16)
                    for u in range(2):
                        sp.wait_ge(S["y"], i * 2 + u + 1)
                        for t, rows in ((0, TT), (1, N - TT)):
                            sp.dma_start(out[bass.ds(2 * i + u, 1), t * TT:t * TT + rows, :].rearrange("o p d -> (o p) d"), y[u][0:rows, t, :]).then_inc(rows_out[u], 16)
                for u in range(2):
                    sp.wait_ge(rows_out[u], 32 * (B // 2))

            @block.tensor
            def _(pe):
                pe.wait_ge(consts_in, 16 * 5)
                pe.wait_ge(setup, 3)

                def done(mm, name):
                    mm.then_inc(S[name], 1)

                with pe.Fori(0, B // 2) as i:
                    def need(name, u, per=1, n=0, met=None):
                        if met:
                            wait_apart(pe, S[name], i * 2 * per + 2 * n + u + 1, met)
                        else:
                            pe.wait_ge(S[name], i * 2 * per + 2 * n + u + 1)

                    for u in range(2):
                        wait_apart(pe, rows_in[u], (i + 1) * 48, met)
                        wait_apart(pe, S["y"], i * 2, met)
                        for t in range(2):
                            mm = nc.tensor.transpose(ps[u][0][0:D, tok(t)], x[u][:, t, :], ident[0:TT, 0:TT])
                        done(mm, "xT_ps")
                    for g in range(HV // 2):
                        for u in range(2):
                            if g >= 2:
                                need("kT", u, HV // 2, g - 2, met=met)
                            for a in range(2):
                                for t in range(2):
                                    mm = nc.tensor.transpose(ps[u][2 + g % 2][0:D, (2 * a + t) * TT:(2 * a + t + 1) * TT],
                                                             kv[u][:, t, 0, (2 * g + a) * D:(2 * g + a + 1) * D], ident[0:TT, 0:TT])
                            done(mm, "k_ps")
                    for g in range(HV // 2):
                        for u in range(2):
                            if g == 0:
                                need("xT", u, met=met)
                            else:
                                need("qT", u, HV // 2, g - 1, met=met)
                            for a in range(2):
                                mm = nc.tensor.matmul(ps[u][1][0:D, a * NP:(a + 1) * NP], wq[:, (2 * g + a) * D:(2 * g + a + 1) * D], xT[u][:], start=True, stop=True)
                            done(mm, "q_ps")

                    def scores(n, u):
                        t, h0, nh = unit_heads(n)
                        if n == 0:
                            need("qT", u, HV // 2, HV // 2 - 1)
                            need("kT", u, HV // 2, HV // 2 - 1)
                        if n >= 2:
                            need("p_ready", u, UNITS, n - 2)
                        bank = ps[u][2 + n % 2]
                        nc.tensor.matmul(bank[0:TT, 0:W], ident_b[0:TT, 0:TT], mask[t][:], start=True, stop=False)
                        w = (t + 1) * TT
                        for a in range(nh):
                            hh = h0 + a
                            mm = nc.tensor.matmul(bank[0:TT, a * w:(a + 1) * w], qT[u][:, hh, tok(t)], kT[u][:, hh, 0:w],
                                                  start=False, stop=(a == nh - 1))
                        done(mm, "s_ps")

                    def turn_p(n, u):
                        need("p_ready", u, UNITS, n)
                        if n >= 1:
                            need("pt_ready", u, UNITS, n - 1)
                        for a in range(4):
                            mm = nc.tensor.transpose(ps[u][0][0:TT, a * TT:(a + 1) * TT], P[u][:, n, a * TT:(a + 1) * TT], ident[0:TT, 0:TT])
                        done(mm, "pt_ps")

                    def values(n, u):
                        t, h0, nh = unit_heads(n)
                        need("pt_ready", u, UNITS, n)
                        if h0 == 0 and n:
                            need("o_ready", u, 2, 0)
                        for a in range(nh):
                            hh = h0 + a
                            for s in range(t + 1):
                                col = (a * (t + 1) + s) * TT
                                mm = nc.tensor.matmul(ps[u][1][0:TT, hh * D:(hh + 1) * D], PT[u][n % 2][:, col:col + TT],
                                                      kv[u][:, s, 1, hh * D:(hh + 1) * D], start=(s == 0), stop=(s == t))
                        done(mm, "o_ps")

                    for n in range(UNITS + 2):
                        for u in range(2):
                            if n < UNITS:
                                scores(n, u)
                        for u in range(2):
                            if 1 <= n <= UNITS:
                                turn_p(n - 1, u)
                        for u in range(2):
                            if n >= 2:
                                values(n - 2, u)
                    for t in range(2):
                        for u in range(2):
                            need("o_ready", u, 2, t)
                            flat = O[u][:, t].rearrange("p h d -> p (h d)")
                            for a in range(4):
                                mm = nc.tensor.transpose(ps[u][2 + t][:, a * TT:(a + 1) * TT], flat[:, a * 128:(a + 1) * 128], ident[0:TT, 0:TT])
                            done(mm, "oT_ps")
                    for u in range(2):
                        need("oT_ready", u, 2, 1)
                        for t in range(2):
                            for a in range(4):
                                mm = nc.tensor.matmul(ps[u][0][0:TT, t * D:(t + 1) * D], OT[u][:, t, a * TT:(a + 1) * TT], wo[:, a, :], start=(a == 0), stop=(a == 3))
                        done(mm, "wo_ps")

            @block.scalar
            def _(act):
                act.wait_ge(setup, 3)
                with act.Fori(0, B // 2) as i:
                    def need(name, u, per=1, n=0, met=None):
                        if met:
                            wait_apart(act, S[name], i * 2 * per + 2 * n + u + 1, met)
                        else:
                            act.wait_ge(S[name], i * 2 * per + 2 * n + u + 1)

                    for g in range(HV // 2):
                        for u in range(2):
                            need("k_ps", u, HV // 2, g)
                            nc.scalar.activation(kT[u][:, 2 * g:2 * g + 2, :].rearrange("p a t -> p (a t)"), ps[u][2 + g % 2][0:D, 0:2 * NP], ACT.Copy).then_inc(S["kT"], 1)

                    def exps(n, u):
                        t, h0, nh = unit_heads(n)
                        need("nb", u, UNITS, n)
                        w = (t + 1) * TT
                        for a in range(nh):
                            hh = h0 + a
                            e = nc.scalar.activation(P[u][:, n, a * w:(a + 1) * w], ps[u][2 + n % 2][0:TT, a * w:(a + 1) * w], ACT.Exp,
                                                     scale=D ** -0.5, bias=nb[u][:, t, hh:hh + 1], accum_out=den[u][:, t, hh:hh + 1])
                        e.then_inc(S["p_ready"], 1)

                    def copy_pt(n, u):
                        need("pt_ps", u, UNITS, n)
                        if n >= 2:
                            need("o_ps", u, UNITS, n - 2)
                        nc.scalar.activation(PT[u][n % 2][:], ps[u][0][0:TT, 0:W], ACT.Copy).then_inc(S["pt_ready"], 1)

                    for n in range(UNITS + 1):
                        for u in range(2):
                            if n < UNITS:
                                exps(n, u)
                        for u in range(2):
                            if n >= 1:
                                copy_pt(n - 1, u)
                    for t in range(2):
                        for u in range(2):
                            need("oT_ps", u, 2, t)
                            nc.scalar.activation(OT[u][:, t, :], ps[u][2 + t][:, 0:W], ACT.Copy).then_inc(S["oT_ready"], 1)

            @block.vector
            def _(dve):
                dve.wait_ge(consts_in, 16 * 5)
                for t in range(2):
                    nc.vector.tensor_copy(mask[t][:], P[0][:, t, :]).then_inc(setup, 1)
                nc.vector.tensor_copy(ident_b[:], ident[:]).then_inc(setup, 1)
                with dve.Fori(0, B // 2) as i:
                    own = Chain(dve, vstep, i, C_STEPS)

                    def need(name, u, per=1, n=0, met=None):
                        if met:
                            wait_apart(dve, S[name], i * 2 * per + 2 * n + u + 1, met)
                        else:
                            dve.wait_ge(S[name], i * 2 * per + 2 * n + u + 1)

                    for u in range(2):
                        need("xT_ps", u)
                        nc.vector.tensor_copy(xT[u][:], ps[u][0][0:D, 0:NP]).then_inc(S["xT"], 1)
                    for g in range(HV // 2):
                        for u in range(2):
                            need("q_ps", u, HV // 2, g)
                            nc.vector.tensor_copy(qT[u][:, 2 * g:2 * g + 2, :].rearrange("p a t -> p (a t)"), ps[u][1][0:D, 0:2 * NP]).then_inc(S["qT"], 1)

                    def unit_max(n, u):
                        t, h0, nh = unit_heads(n)
                        need("s_ps", u, UNITS, n)
                        own.link(nc.vector.tensor_reduce(m[u][:, t, h0:h0 + nh], ps[u][2 + n % 2][0:TT, 0:W].rearrange("p (a s) -> p a s", a=nh), AX.X, ALU.max))
                        nc.vector.tensor_scalar(nb[u][:, t, h0:h0 + nh], m[u][:, t, h0:h0 + nh], -(D ** -0.5), None, ALU.mult).then_inc(S["nb"], 1)

                    def scale_o(t, u):
                        need("o_ps", u, UNITS, UT - 1 if t == 0 else UNITS - 1)
                        own.link(nc.vector.reciprocal(rden[u][:, t, :], den[u][:, t, :]))
                        nc.vector.tensor_tensor(O[u][:, t], ps[u][1][0:TT, :].rearrange("p (a d) -> p a d", a=HV),
                                                bcast(rden[u][:, t, :], 2, [TT, HV, D]), ALU.mult).then_inc(S["o_ready"], 1)

                    for n in range(UNITS + 2):
                        for u in range(2):
                            if n < UNITS:
                                unit_max(n, u)
                        if n - 2 in (UT - 1, UNITS - 1):
                            for u in range(2):
                                scale_o(int(n - 2 == UNITS - 1), u)
                    for u in range(2):
                        need("wo_ps", u)
                        dve.wait_ge(rows_out[u], i * 32)
                        nc.vector.tensor_tensor(y[u][:], ps[u][0][0:TT, 0:2 * D].rearrange("p (t d) -> p t d", t=2), h[u][:], ALU.add).then_inc(S["y"], 1)
                    own.close()


def vit_tower(nc, c, out):
    h3 = nc.dram_tensor("h3_rows", (ROWS, D), F32, kind="Internal").ap()
    xn4 = nc.dram_tensor("xn4_rows", (ROWS, D), F32, kind="Internal").ap()
    kv = nc.dram_tensor("kv_rows", (ROWS, 2 * HV * D), F32, kind="Internal").ap()
    with nc.sbuf_tensor("pad", [ROWS - B * N, D], F32) as pad, nc.semaphore("pad_set") as pad_set, nc.semaphore("pad_out") as pad_out:
        with nc.Block() as block:
            @block.gpsimd
            def _(pool):
                nc.gpsimd.memset(pad[:], 0.0).then_inc(pad_set, 1)

            @block.sync
            def _(sp):
                sp.wait_ge(pad_set, 1)
                for rows in (h3, xn4):
                    sp.dma_start(rows[B * N:ROWS, :], pad[:]).then_inc(pad_out, 16)
                sp.wait_ge(pad_out, 32)
    image_and_memory_phase(nc, c, h3, xn4, kv)
    readout_phase(nc, c, h3, xn4, kv, out)


def _layout(inp):
    import numpy as np

    a = {k: np.asarray(v) for k, v in inp.items()}
    G = IMG // PATCH
    px = a["x"].reshape(B, CH, G, PATCH, G, PATCH).transpose(0, 1, 3, 5, 2, 4).reshape(B, KC, 128, G * G)
    pixT = np.zeros((B, 128, KC, NP), np.float32)
    pixT[:, :, :, 1:N] = px.transpose(0, 2, 1, 3)
    rows = lambda v, n: np.repeat(v.reshape(1, -1), n, axis=0)
    add = rows(a["L0_tok_b"], NP)
    add[0] = a["cls_tok"].reshape(-1)
    swap = np.arange(D) ^ 1
    wq = a["L0_attn_wq"].reshape(HQ, D, D)
    wqq = np.concatenate([wq, wq[:, swap]], axis=1).transpose(2, 0, 1)
    wk, wv = a["L0_attn_wkv"][:D], a["L0_attn_wkv"][D:]
    t = np.arange(NP, dtype=np.float32)
    freqs = np.float32(10000.0) ** (np.float32(-2.0) * np.arange(D // 2, dtype=np.float32) / np.float32(D))
    theta = t[:, None] * freqs[None, :]
    cos = np.repeat(np.cos(theta), 2, axis=1)
    sin = np.repeat(np.sin(theta), 2, axis=1) * np.where(np.arange(D) % 2 == 0, np.float32(-1), np.float32(1))
    rope = np.concatenate([cos, sin], axis=1).astype(np.float32)
    tiles = lambda v: v.reshape(2, TT, -1).transpose(1, 0, 2)
    q, s = np.arange(NP)[:, None], np.arange(NP)[None, :]

    def masks(ok):
        m = np.where(ok, np.float32(0), np.float32(NEG))
        return np.stack([np.tile(m[:TT, :TT], (1, 4)), np.tile(m[TT:, :], (1, 2))])
    w1 = np.concatenate([a["L0_ffn_W1p"], a["L0_ffn_W1s"][None]]).transpose(1, 0, 2)
    b1 = np.concatenate([a["L0_ffn_b1p"], a["L0_ffn_b1s"][None]]).reshape(NE + 1, 2, 128).transpose(2, 0, 1)
    w2 = np.concatenate([a["L0_ffn_W2p"], a["L0_ffn_W2s"][None]]).reshape(NE + 1, 2, 128, D).transpose(2, 0, 1, 3)
    col = lambda v: v.reshape(-1, 1)
    return {k: np.ascontiguousarray(v) for k, v in dict(
        pixT=pixT, patch_w=a["L0_tok_W"].T.reshape(KC, 128, D).transpose(1, 0, 2), embed_add=tiles(add),
        ident=np.eye(128, dtype=np.float32), wqq=wqq,
        wkkv=np.concatenate([wk, wk[swap], wv]).T, rope_q=rope.T, rope_k=tiles(rope),
        wo=a["L0_attn_wo"].T.reshape(HQ * D // 128, 128, D).transpose(1, 0, 2), wr=a["L0_ffn_Wr"], w1=w1, b1=b1, w2=w2,
        b2p=np.repeat(a["L0_ffn_b2p"][None], TT, axis=0), b2s=rows(a["L0_ffn_b2s"], TT),
        iota8=rows(np.arange(NE, dtype=np.float32), TT), wqkv=a["L1_attn_Wqkv"], wproj=a["L1_attn_Wproj"],
        bproj=rows(a["L1_attn_bproj"], TT), lng=col(a["L1_attn_ln_g"]), lnb=col(a["L1_attn_ln_b"]), wg1=a["L1_attn_Wg1"],
        bg1=col(a["L1_attn_bg1"]), wg2=a["L1_attn_Wg2"], bg2=rows(a["L1_attn_bg2"], TT),
        blocks=np.kron(np.eye(8, dtype=np.float32), np.ones((D // 8, D // 8), np.float32)),
        qnw=rows(a["L0_attn_q_norm_w"], TT), knw=rows(a["L0_attn_k_norm_w"], TT),
        mask=masks((s <= q) & (q - s <= WINDOW)), causal=masks(s <= q),
        wpkT=a["L1_ffn_Wq_pk"].T.reshape(2 * HV, D // 2, D).transpose(1, 0, 2),
        keysT=a["L1_ffn_pk_keys"].transpose(3, 0, 2, 1).reshape(D // 2, 2 * HV, NK),
        offs=np.broadcast_to((np.arange(HV, dtype=np.float32) * (NK * NK))[None, :, None], (TILE, HV, TOPK)),
        iota=rows(np.arange(NC, dtype=np.float32), TILE),
        table=np.concatenate([a["L1_ffn_keys_table"], a["L1_ffn_values_table"]], axis=1),
        wq_mem=a["L1_ffn_Wq"], wo_mem=a["L1_ffn_Wo"].reshape(HV * D // 128, 128, D).transpose(1, 0, 2),
    ).items()}


def kernel(**inputs):
    import concourse.bacc as bacc
    from concourse import mybir as _mybir
    from concourse.bass_utils import run_bass_kernel_spmd as run

    nc = bacc.Bacc("TRN2", target_bir_lowering=False, num_devices=1)
    arrays = _layout(inputs)
    c = {k: nc.dram_tensor("in_" + k, v.shape, _mybir.dt.from_np(v.dtype), kind="ExternalInput").ap() for k, v in arrays.items()}
    out = nc.dram_tensor("out", (B, N, D), F32, kind="ExternalOutput").ap()
    vit_tower(nc, c, out)
    r = run(nc, [{"in_" + k: v for k, v in arrays.items()}], core_ids=[0])
    return r.results[0]["out"]
```

```python
from contextlib import ExitStack

import concourse.bass as bass
from concourse import mybir

F32 = mybir.dt.float32
BF16 = mybir.dt.bfloat16
U32 = mybir.dt.uint32
ALU = mybir.AluOpType
ACT = mybir.ActivationFunctionType
AX = mybir.AxisListType

B, CH, IMG, PATCH, D = 64, 3, 224, 16, 64
N = (IMG // PATCH) ** 2 + 1
TT = (N + 1) // 2
NP = 2 * TT
KC = CH * PATCH * PATCH // 128
HQ = 16
WINDOW = 128
NE, FF = 8, 256
GH = D // 4
HV, NK, TOPK = 8, 64, 16
CUTS = [TOPK // (r + 1) for r in range(TOPK)]
NC = sum(CUTS)
TILE = 128
NTILES = (B * N + TILE - 1) // TILE
ROWS = NTILES * TILE
LN_EPS = 1e-5
RMS_EPS = 1.1920929e-07
NEG = -1e30
LOWEST = -3.0e38
EXP_LN = "natural_log_exp_and_others"


def wait_apart(eng, sem, value, met):
    value = value if isinstance(value, int) else eng.to_reg(value)
    eng.wait_ge(*met)
    eng.wait_ge(sem, value)


class Chain:

    def __init__(self, eng, sem, trip, per_trip):
        self.eng, self.sem, self.base, self.per_trip, self.n = eng, sem, trip * per_trip, per_trip, 0

    def step(self, ins):
        ins.then_inc(self.sem, 1)
        self.n += 1

    def wait(self, met=None):
        if met:
            wait_apart(self.eng, self.sem, self.base + self.n, met)
        else:
            self.eng.wait_ge(self.sem, self.base + self.n)

    def link(self, ins):
        self.step(ins)
        self.wait()

    def close(self):
        assert self.n == self.per_trip, (self.n, self.per_trip)


def bcast(ap, axis, shape):
    return ap.unsqueeze(axis).to_broadcast(shape)


A_STEPS = 126
A_ACT_STEPS = 14
FRONT_STEPS = 144

R_STEPS = 24

STAGES = 48
PIECES = 32
READS = 48
TRIP = 3
PARTS = 4
SLOTS = 4


def run(gen, steps):
    for _ in range(steps if gen else 0):
        next(gen)


def schedule(eng, pair, front, head, after, reader):
    images = pair(0)
    run(images, STAGES)
    run(front(0, 0, -1), PIECES)
    run(images, STAGES)
    slots = HV * TRIP

    def trip(i, images, ahead, read):
        last = None
        for b in range(TRIP):
            t, nxt = TRIP * i + b, ahead(b)
            for hh in range(HV):
                for part in range(PARTS):
                    run(images, 2 * STAGES // (slots * PARTS))
                    q = hh * PARTS + part
                    run(nxt, min(PIECES, (q + 1) * 9 // 8) - min(PIECES, q * 9 // 8))
                    if part == 1 and last:
                        after(*last)
                    run(read, 2 * READS // (slots * PARTS))
                head(t, b, hh)
                last = t, b, hh
        after(*last)

    def full_trip(i, read):
        trip(i, pair(i + 1), lambda b: front(TRIP * i + b + 1, (b + 1) % TRIP, i), read)

    PAIRS = B // 2
    with eng.Fori(0, 2) as i:
        full_trip(i, None)
    with eng.Fori(0, PAIRS - 3) as r:
        full_trip(r + 2, reader(r, TRIP * (r + 2)))
    for i in range(PAIRS - 1, NTILES // TRIP):
        trip(i, None, lambda b: front(TRIP * i + b + 1, (b + 1) % TRIP, None) if TRIP * i + b + 1 < NTILES else None, reader(i - 2, TRIP * i))
    run(reader(PAIRS - 1, NTILES), 2 * READS)


def tower(nc, c, h3_rows, xn4_rows, kv_rows, out):
    QG = HQ // 4
    UNITS = QG + HQ // 2
    W = 4 * TT
    with ExitStack() as ctx:
        def sb(name, shape, dt=F32):
            return ctx.enter_context(nc.sbuf_tensor(name, shape, dt))

        def sem(name):
            return ctx.enter_context(nc.semaphore(name))

        def two(name, shape, dt=F32):
            return [sb(f"{name}{u}", shape, dt) for u in range(2)]

        shapes = dict(patch_w=[128, KC, D], embed_add=[TT, 2, D], ident=[128, 128], wqq=[D, HQ, 2 * D], wkkv=[D, 3 * D],
                      rope_q=[2 * D, NP], rope_k=[TT, 2, 2 * D], wo=[128, HQ * D // 128, D], wr=[D, NE], w1=[D, NE + 1, FF],
                      b1=[128, NE + 1, 2], w2=[128, NE + 1, 2, D], b2p=[TT, NE, D], b2s=[TT, D], iota8=[TT, NE],
                      wqkv=[D, 3 * D], wproj=[D, D], bproj=[TT, D], lng=[D, 1], lnb=[D, 1], wg1=[D, GH], bg1=[GH, 1],
                      wg2=[GH, D], bg2=[TT, D], blocks=[D, D], qnw=[TT, D], knw=[TT, D])
        k = {n: sb("c_" + n, s) for n, s in shapes.items()}
        mask = [sb(f"c_mask{t}", [TT, W], BF16) for t in range(2)]
        ident_b = sb("c_ident_b", [128, 128], BF16)
        knq = sb("knq", [TT, D])
        ones = sb("ones", [D, 1])
        eps_ln, eps_rms = sb("eps_ln", [TT, 1]), sb("eps_rms", [TT, 1])
        pix = two("pix", [128, KC, NP])
        h = two("h", [TT, 2, D])
        stats = sb("stats", [TT, 2, 6])
        mv = sb("mv", [TT, 2, 2])
        logs = sb("logs", [TT, 2 * HQ])
        rstd = sb("rstd", [TT, 2])
        xn = two("xn", [TT, 2, D])
        xT = sb("xT", [D, NP])
        kk = sb("kk", [TT, 2, 2 * D])
        kr = sb("kr", [TT, 2, D])
        ksq = sb("ksq", [TT, 2, D])
        kss = sb("kss", [TT, 2])
        krs = sb("krs", [TT, 2])
        kdup = sb("kdup", [TT, 2, 2, D])
        kT = sb("kT", [2 * D, NP])
        v = sb("v", [TT, 2, D])
        qr_late = sb("qr_late", [2 * D, HQ * NP])
        qr = qr_late[:].rearrange("p (h t) -> p h t", h=HQ)
        mo = qr_late[0:TT, 0:2 * NE * D].rearrange("p (t e d) -> p t e d", t=2, e=NE)
        qT, xgT, hg = (qr_late[0:rows, 2 * NE * D + j * NP:2 * NE * D + (j + 1) * NP] for j, rows in enumerate((D, D, GH)))
        ek = qr_late[0:TT, 2 * NE * D + 3 * NP:2 * NE * D + 3 * NP + 2 * D].rearrange("p (t d) -> p t d", t=2)
        qsq_OT = sb("qsq_OT", [128, HQ * NP])
        qsq = qsq_OT[0:D, :].rearrange("p (h t) -> p h t", h=HQ)
        OT = qsq_OT[:, 0:4 * W].rearrange("p (n w) -> p n w", n=4)
        rq = sb("rq", [TT, 2, HQ])
        m = sb("m", [TT, 2, HQ])
        nb = sb("nb", [TT, 2, HQ])
        den = sb("den", [TT, 2, HQ])
        rden = sb("rden", [TT, 2, HQ])
        P_hid = sb("P_hid", [128, UNITS * W])
        P = P_hid[0:TT, :].rearrange("p (n w) -> p n w", n=UNITS)
        hid = P_hid[:, 0:(NE + 1) * 2 * NP].rearrange("p (e f t) -> p e f t", e=NE + 1, f=2)
        PT = [sb(f"PT{s}", [TT, W]) for s in range(2)]
        O = sb("O", [TT, 2, HQ, D])
        lg = sb("lg", [TT, 2, NE])
        lmax = sb("lmax", [TT, 2])
        el = sb("el", [TT, 2, NE])
        top = sb("top", [TT, 2, 8])
        topi = sb("topi", [TT, 2, 8], U32)
        topf = sb("topf", [TT, 2, 2])
        tsum = sb("tsum", [TT, 2])
        trec = sb("trec", [TT, 2])
        tw = sb("tw", [TT, 2, 2])
        oh = sb("oh", [TT, 2, 2, NE])
        gate = sb("gate", [TT, 2, NE])
        mr = sb("mr", [TT, 2, D])
        kmx = sb("kmx", [D, 1])
        ksum = sb("ksum", [D, 1])
        krec = sb("krec", [D, 1])
        eT = sb("eT", [D, NP])
        ctxs = sb("ctxs", [D, D])
        g = sb("g", [TT, 2, D])
        ps = [ctx.enter_context(nc.psum_tensor(f"ps{s}", [128, 512], F32)) for s in range(4)]

        R = 2 * HV
        HG = 2
        offs = sb("offs", [TILE, HV, TOPK])
        iota = sb("iota", [TILE, NC])
        wk = sb("wk", [D, R * NK])
        xb = sb("xb", [TILE, D])
        xbT = sb("xbT", [D, TILE])
        sims = sb("sims", [TILE, 2 * R * NK])
        sim, sim2 = (sims[:, a * R * NK:(a + 1) * R * NK].rearrange("p (r k) -> p r k", r=R) for a in range(2))
        onehot = sims[:, 0:HG * TOPK * NC].rearrange("p (h k c) -> p h k c", h=HG, k=TOPK)
        ranks = sb("ranks", [TILE, R, TOPK], U32)
        half = [sb(f"half{p}", [TILE, 2, HV, TOPK]) for p in range(2)]
        pairs = sb("pairs", [TILE, 2, HV, NC])
        pairs2 = sb("pairs2", [TILE, HV, NC])
        best = sb("best", [TILE, HV, TOPK])
        place = sb("place", [TILE, HV, TOPK], U32)
        placef = sb("placef", [TILE, HV, TOPK])
        rowf = sb("rowf", [TILE, HV, TOPK])
        rows_at = [sb(f"rows_at{b}", [TILE, HV * TOPK], U32) for b in range(TRIP)]
        ex = sb("ex", [TILE, HV, TOPK])
        ssum = sb("ssum", [TILE, HV])
        weight = [sb(f"weight{b}", [TILE, HV, TOPK]) for b in range(TRIP)]
        G = [sb(f"G{s}", [TILE, TOPK * 2 * D]) for s in range(SLOTS)]
        wpkT = G[0][0:D // 2, 0:R * D].rearrange("p (r d) -> p r d", r=R)
        keysT = G[1][0:D // 2, 0:R * NK].rearrange("p (r k) -> p r k", r=R)
        kv_sum = sb("kv_sum", [TILE, 2, HV, D])
        ps_s = ctx.enter_context(nc.psum_tensor("ps_s", [128, 512], F32))
        ps_kv = ctx.enter_context(nc.psum_tensor("ps_kv", [128, 512], F32))
        RU = HV // 4
        RUNITS = RU + HV // 2
        causal = [sb(f"r_mask{t}", [TT, W], BF16) for t in range(2)]
        r_wq = sb("r_wq", [D, HV * D])
        r_wo = sb("r_wo", [128, HV * D // 128, D])
        r_h = sb("r_h", [TT, 2, D])
        r_x = sb("r_x", [TT, 2, D])
        r_kv = sb("r_kv", [TT, 2, 2, HV * D])
        masks_in = r_kv[:].rearrange("p t a f -> p (t a f)")[:, 0:2 * W].rearrange("p (t w) -> p t w", t=2)
        r_xT = sb("r_xT", [D, NP])
        r_qT_OT = sb("r_qT_OT", [128, HV * NP])
        r_qT = r_qT_OT[0:D, :].rearrange("p (h t) -> p h t", h=HV)
        r_OT = r_qT_OT[:, 0:2 * W].rearrange("p (t w) -> p t w", t=2)
        r_kT = sb("r_kT", [D, HV, NP])
        r_m = sb("r_m", [TT, 2, HV])
        r_nb = sb("r_nb", [TT, 2, HV])
        r_den = sb("r_den", [TT, 2, HV])
        r_rden = sb("r_rden", [TT, 2, HV])
        r_P = sb("r_P", [TT, W])
        r_PT = sb("r_PT", [TT, W])
        r_O = sb("r_O", [TT, 2, HV, D])
        r_y = sb("r_y", [TT, 2, D])
        pr = [ctx.enter_context(nc.psum_tensor(f"ps_r{s}", [128, 512], F32)) for s in range(2)]
        r_in, r_out, rstep = sem("r_in"), sem("r_out"), sem("r_vector_step")
        SR = {s: sem("r_sem_" + s) for s in
              "xT_ps xT q_ps qT k_ps kT s_ps nb p_ready pt_ps pt_ready o_ps o_ready oT_ps oT_ready wo_ps y".split()}

        def read_heads(n):
            return (0, 4 * n, 4) if n < RU else (1, 2 * (n - RU), 2)

        def read_value(p, u, per, n):
            return p * (2 * per) + u * per + n + 1


        x_in, wk_ps, wk_ready = sem("x_in"), sem("wk_ps"), sem("wk_ready")
        xT_ps, xT_ready, sim_ps, sim_in, rows_ready, shifted, exped, weight_ready = (
            sem("b_" + s) for s in ("xT_ps", "xT_ready", "sim_ps", "sim_in", "rows_ready", "shifted", "exped", "weight_ready"))
        landed = [sem(f"landed{hh}") for hh in range(HV)]
        weighed, summed = sem("weighed"), sem("summed")
        kv_ready = [sem(f"kv_ready{q}") for q in range(2)]
        kv_out = sem("kv_out")
        bstep = sem("b_vector_step")

        SETUP = 10
        consts_in, setup = sem("a_consts_in"), sem("a_setup")
        pix_in = [sem(f"pix_in{u}") for u in range(2)]
        rows_out = [sem(f"rows_out{u}") for u in range(2)]
        vstep = sem("a_vector_step")
        astep = sem("a_scalar_step")
        CONSTS = 16 * (len(shapes) + 2 + 4 + 4)
        met = (consts_in, CONSTS)
        S = {}
        NAMES = """emb_sum var1 rstd1 xn1 xT1_ps xT1 kv_ps kss krs kdup kT_ps kT q_ps q_rot q_sq qss rq s_ps nb p_ready
                   pt_ps pt_ready o_ps o_ready oT_ps oT_ready wo_ps var2 rstd2 xn2 xT2_ps xT2 lg_ps lmax el hid_ps hid_ready
                   moe_ps var3 rstd3 xn3 xT3_ps xT3 qkv_ps kmx ek_ready ek_ps ek lin_v ctx_ps ctx lin_ps var5 rstd5 xg xgT_ps xgT
                   hg_ps hg g_ps g_in g_exp og ogT_ps ogT proj_ps var4 rstd4 xn4""".split()
        for s in NAMES:
            S[s] = sem("a_" + s)

        def tok(t):
            return slice(t * TT, (t + 1) * TT)

        def unit_heads(n):
            return (0, 4 * n, 4) if n < QG else (1, 2 * (n - QG), 2)

        with nc.Block() as block:
            @block.sync
            def _(sp):
                for name in shapes:
                    sp.dma_start(k[name][:], c[name]).then_inc(consts_in, 16)
                for t in range(2):
                    sp.dma_start(P[:, t, :], c["mask"][t]).then_inc(consts_in, 16)
                for dst, name in ((wpkT, "wpkT"), (keysT, "keysT"), (offs[:], "offs"), (iota[:], "iota"),
                                  (r_wq[:], "wq_mem"), (r_wo[:], "wo_mem"), (masks_in[:, 0, :], "causal0"), (masks_in[:, 1, :], "causal1")):
                    sp.dma_start(dst, c[name]).then_inc(consts_in, 16)
                sp.wait_ge(consts_in, CONSTS)
                sp.wait_ge(setup, SETUP)

                def load_pixels(i, u):
                    sp.dma_start(pix[u][:], c["pixT"][bass.ds(2 * i + u, 1)].rearrange("o p k t -> (o p) k t")).then_inc(pix_in[u], 16)

                for u in range(2):
                    load_pixels(0, u)

                def pair(i):
                    for u in range(2):
                        yield
                        wait_apart(sp, S["emb_sum"], 2 * i + u + 1, met)
                        load_pixels(i + 1, u)
                        for _ in range(STAGES - 2):
                            yield
                        sp.wait_ge(S["xn4"], i * 2 + u + 1)
                        for src, dst in ((h[u], h3_rows), (xn[u], xn4_rows)):
                            for t, rows in ((0, TT), (1, N - TT)):
                                sp.dma_start(dst[bass.ds((2 * i + u) * N + t * TT, rows), :], src[0:rows, t, :]).then_inc(rows_out[u], 16)
                        yield

                def front(t, b, i):
                    if i is not None:
                        wait_apart(sp, rows_out[0], (i + 2) * 64 if b == 0 else (i + 1) * 64, met)
                        wait_apart(sp, rows_out[1], (i + 1) * 64, met)
                    else:
                        for u in range(2):
                            sp.wait_ge(rows_out[u], 64 * (B // 2))
                    sp.wait_ge(xT_ps, t)
                    sp.dma_start(xb[:], xn4_rows[bass.ds(t * TILE, TILE), :]).then_inc(x_in, 16)
                    for _ in range(PIECES):
                        yield

                def head(t, b, hh):
                    pass

                def after(t, b, hh):
                    if hh == HV - 1:
                        for q in range(2):
                            wait_apart(sp, kv_ready[q], t + 1, met)
                        sp.dma_start(kv_rows[bass.ds(t * TILE, TILE), :], kv_sum[:].rearrange("p a h d -> p (a h d)")).then_inc(kv_out, 16)

                def reader(p, tiles):
                    wait_apart(sp, kv_out, 16 * tiles, met)
                    for u in range(2):
                        wait_apart(sp, SR["y"], 2 * p + u, met)
                        for dst, src in ((r_h[:], h3_rows), (r_x[:], xn4_rows), (r_kv[:].rearrange("p t a f -> p t (a f)"), kv_rows)):
                            sp.dma_start(dst, src[bass.ds((2 * p + u) * N, NP), :].rearrange("(t p) f -> p t f", t=2)).then_inc(r_in, 16)
                        for _ in range(46):
                            yield
                        wait_apart(sp, SR["y"], 2 * p + u + 1, met)
                        for t, rows in ((0, TT), (1, N - TT)):
                            sp.dma_start(out[bass.ds(2 * p + u, 1), t * TT:t * TT + rows, :].rearrange("o p d -> (o p) d"), r_y[0:rows, t, :]).then_inc(r_out, 16)
                        for _ in range(READS - 46):
                            yield

                schedule(sp, pair, front, head, after, reader)
                sp.wait_ge(r_out, 32 * B)
                for u in range(2):
                    sp.wait_ge(pix_in[u], 16 * (B // 2 + 1))

            @block.tensor
            def _(pe):
                pe.wait_ge(consts_in, CONSTS)
                pe.wait_ge(setup, SETUP)

                for r in range(R):
                    mm = nc.tensor.matmul((ps_s, ps_kv)[r // HV][0:D, (r % HV) * NK:(r % HV + 1) * NK], wpkT[:, r, :], keysT[:, r, :], start=True, stop=True)
                mm.then_inc(wk_ps, 1)
                pe.wait_ge(wk_ready, 1)

                def done(mm, name):
                    mm.then_inc(S[name], 1)

                def pair(i):
                    for u in range(2):
                        def need(name, per=1, n=0, met=None):
                            if met:
                                wait_apart(pe, S[name], i * (2 * per) + u * per + n + 1, met)
                            else:
                                pe.wait_ge(S[name], i * (2 * per) + u * per + n + 1)

                        def turn(src, name, ready, bank):
                            need(ready, met=met)
                            for t in range(2):
                                mm = nc.tensor.transpose(ps[bank][0:D, tok(t)], src[:, t, :], k["ident"][0:TT, 0:TT])
                            done(mm, name)

                        pe.wait_ge(pix_in[u], (i + 1) * 16)
                        for t in range(2):
                            for kc in range(KC):
                                mm = nc.tensor.matmul(ps[0][0:TT, t * D:(t + 1) * D], pix[u][:, kc, tok(t)], k["patch_w"][:, kc, :],
                                                      start=(kc == 0), stop=(kc == KC - 1))
                        done(mm, "emb_sum")
                        yield
                        turn(xn[u], "xT1_ps", "xn1", 1)
                        yield
                        need("xT1")
                        for t in range(2):
                            mm = nc.tensor.matmul(ps[0][0:TT, t * 3 * D:(t + 1) * 3 * D], xT[:, tok(t)], k["wkkv"][:], start=True, stop=True)
                        done(mm, "kv_ps")
                        for n in range(HQ // 2):
                            yield
                            if n >= 2:
                                need("q_sq", HQ // 2, n - 2)
                            for a in range(2):
                                mm = nc.tensor.matmul(ps[2 + n % 2][:, a * NP:(a + 1) * NP], k["wqq"][:, 2 * n + a, :], xT[:], start=True, stop=True)
                            done(mm, "q_ps")
                        yield
                        need("kdup")
                        for t in range(2):
                            mm = nc.tensor.transpose(ps[1][:, tok(t)], kdup[:, t].rearrange("p a d -> p (a d)"), k["ident"][0:TT, 0:TT])
                        done(mm, "kT_ps")
                        need("q_sq", HQ // 2, HQ // 2 - 1)
                        for t in range(2):
                            for hh in range(HQ):
                                mm = nc.tensor.matmul(ps[0][0:TT, t * HQ + hh:t * HQ + hh + 1], qsq[:, hh, tok(t)], ones[:], start=True, stop=True)
                        done(mm, "qss")

                        def scores(n):
                            t, h0, nh = unit_heads(n)
                            if n == 0:
                                need("kT")
                                need("q_rot", HQ // 2, HQ // 2 - 1)
                            if n >= 2:
                                need("p_ready", UNITS, n - 2)
                            bank = ps[2 + n % 2]
                            nc.tensor.matmul(bank[0:TT, 0:W], ident_b[0:TT, 0:TT], mask[t][:], start=True, stop=False)
                            w = (t + 1) * TT
                            for a in range(nh):
                                mm = nc.tensor.matmul(bank[0:TT, a * w:(a + 1) * w], qr[:, h0 + a, tok(t)], kT[:, 0:w], start=False, stop=(a == nh - 1))
                            done(mm, "s_ps")

                        def turn_p(n):
                            need("p_ready", UNITS, n)
                            if n >= 1:
                                need("pt_ready", UNITS, n - 1)
                            else:
                                need("rq")
                            for a in range(4):
                                mm = nc.tensor.transpose(ps[0][0:TT, a * TT:(a + 1) * TT], P[:, n, a * TT:(a + 1) * TT], k["ident"][0:TT, 0:TT])
                            done(mm, "pt_ps")

                        def values(n):
                            t, h0, nh = unit_heads(n)
                            need("pt_ready", UNITS, n)
                            if h0 % 8 == 0 and n:
                                need("o_ready", 4, t * 2 + h0 // 8 - 1)
                            if n == 0:
                                need("kT")
                            for a in range(nh):
                                o = ps[1][0:TT, (h0 + a) % 8 * D:((h0 + a) % 8 + 1) * D]
                                for s in range(t + 1):
                                    col = (a * (t + 1) + s) * TT
                                    mm = nc.tensor.matmul(o, PT[n % 2][:, col:col + TT], v[:, s, :], start=(s == 0), stop=(s == t))
                            done(mm, "o_ps")

                        for n in range(UNITS + 3):
                            yield
                            if n < UNITS:
                                scores(n)
                            if 2 <= n <= UNITS + 1:
                                turn_p(n - 2)
                            if n >= 3:
                                values(n - 3)
                        yield
                        for n in range(4):
                            if n % 2 == 0:
                                need("o_ready", 4, 1 + n)
                            if n >= 2:
                                need("oT_ready", 4, n - 2)
                            flat = O[:, n // 2].rearrange("p h d -> p (h d)")
                            for a in range(4):
                                ch = (n % 2) * 4 + a
                                mm = nc.tensor.transpose(ps[2 + n % 2][:, a * TT:(a + 1) * TT], flat[:, ch * 128:(ch + 1) * 128], k["ident"][0:TT, 0:TT])
                            done(mm, "oT_ps")
                        yield
                        need("oT_ready", 4, 3)
                        for t in range(2):
                            for ch in range(8):
                                mm = nc.tensor.matmul(ps[0][0:TT, t * D:(t + 1) * D], OT[:, 2 * t + ch // 4, (ch % 4) * TT:(ch % 4 + 1) * TT],
                                                      k["wo"][:, ch, :], start=(ch == 0), stop=(ch == 7))
                        done(mm, "wo_ps")
                        yield
                        turn(xn[u], "xT2_ps", "xn2", 1)
                        yield
                        need("xT2")
                        for t in range(2):
                            mm = nc.tensor.matmul(ps[0][0:TT, t * NE:(t + 1) * NE], xT[:, tok(t)], k["wr"][:], start=True, stop=True)
                        done(mm, "lg_ps")
                        def second(e):
                            need("hid_ready", NE + 1, e)
                            if e == 0:
                                need("lmax")
                            for t in range(2):
                                out = ps[t][0:TT, e * D:(e + 1) * D] if e < NE else ps[2][0:TT, t * D:(t + 1) * D]
                                for f in range(2):
                                    mm = nc.tensor.matmul(out, hid[:, e, f, tok(t)], k["w2"][:, e, f, :], start=(f == 0), stop=(f == 1))
                            return mm

                        for e in range(NE + 1):
                            if e and e != 2:
                                yield
                            if e >= 2:
                                need("hid_ready", NE + 1, e - 2)
                            for f in range(2):
                                mm = nc.tensor.matmul(ps[2 + e % 2][:, f * NP:(f + 1) * NP], k["w1"][:, e, f * 128:(f + 1) * 128], xT[:], start=True, stop=True)
                            done(mm, "hid_ps")
                            if e >= 2:
                                second(e - 2)
                        yield
                        second(NE - 1)
                        done(second(NE), "moe_ps")
                        yield
                        yield
                        turn(xn[u], "xT3_ps", "xn3", 0)
                        yield
                        need("xT3", met=met)
                        for a in range(2):
                            nc.tensor.matmul(ps[1][0:D, a * NP:(a + 1) * NP], k["wqkv"][:, a * D:(a + 1) * D], xT[:], start=True, stop=True)
                        for t in range(2):
                            mm = nc.tensor.matmul(ps[2][0:TT, t * D:(t + 1) * D], xT[:, tok(t)], k["wqkv"][:, 2 * D:3 * D], start=True, stop=True)
                        done(mm, "qkv_ps")
                        yield
                        turn(g, "xgT_ps", "xg", 0)
                        yield
                        need("xgT", met=met)
                        done(nc.tensor.matmul(ps[3][0:GH, 0:NP], k["wg1"][:], xgT, start=True, stop=True), "hg_ps")
                        need("ek_ready", met=met)
                        need("lin_v", met=met)
                        for t in range(2):
                            mm = nc.tensor.transpose(ps[2][0:TT, t * D:(t + 1) * D], eT[:, tok(t)], k["ident"][0:D, 0:D])
                        done(mm, "ek_ps")
                        yield
                        need("ek")
                        for t in range(2):
                            mm = nc.tensor.matmul(ps[0][0:D, 0:D], ek[:, t, :], v[:, t, :], start=(t == 0), stop=(t == 1))
                        done(mm, "ctx_ps")
                        need("ctx")
                        for t in range(2):
                            mm = nc.tensor.matmul(ps[1][0:TT, t * D:(t + 1) * D], qT[:, tok(t)], ctxs[:], start=True, stop=True)
                        done(mm, "lin_ps")
                        need("hg")
                        for t in range(2):
                            mm = nc.tensor.matmul(ps[2][0:TT, t * D:(t + 1) * D], hg[:, tok(t)], k["wg2"][:], start=True, stop=True)
                        done(mm, "g_ps")
                        yield
                        turn(g, "ogT_ps", "og", 3)
                        yield
                        need("ogT")
                        for t in range(2):
                            mm = nc.tensor.matmul(ps[2][0:TT, t * D:(t + 1) * D], xgT[:, tok(t)], k["wproj"][:], start=True, stop=True)
                        done(mm, "proj_ps")
                        yield
                        yield

                def front(t, b, i):
                    yield
                    wait_apart(pe, x_in, 16 * (t + 1), met)
                    wait_apart(pe, sim_in, 2 * t, met)
                    nc.tensor.transpose(ps_s[0:D, 0:TILE], xb[:], k["ident"][:]).then_inc(xT_ps, 1)
                    yield
                    pe.wait_ge(xT_ready, t + 1)
                    nc.tensor.matmul(ps_s[:], xbT[:], wk[:, 0:512], start=True, stop=True).then_inc(sim_ps, 1)
                    yield
                    yield
                    pe.wait_ge(sim_in, 2 * t + 1)
                    nc.tensor.matmul(ps_s[:], xbT[:], wk[:, 512:1024], start=True, stop=True).then_inc(sim_ps, 1)
                    for _ in range(PIECES - 4):
                        yield

                def head(t, b, hh):
                    pass

                def after(t, b, hh):
                    pe.wait_ge(weighed, t * HV + hh + 1)
                    if hh == 0:
                        pe.wait_ge(kv_ready[1], t)
                    if hh == HV // 2:
                        pe.wait_ge(kv_ready[0], t + 1)
                    for j in range(TOPK):
                        mm = nc.tensor.matmul(ps_kv[:, (hh % 4) * 128:(hh % 4 + 1) * 128], k["ident"][:], G[hh % SLOTS][:, j * 128:(j + 1) * 128],
                                              start=(j == 0), stop=(j == TOPK - 1))
                    mm.then_inc(summed, 1)

                def reader(p, tiles):
                    for u in range(2):
                        def need(name, per=1, n=0, met=None):
                            if met:
                                wait_apart(pe, SR[name], read_value(p, u, per, n), met)
                            else:
                                pe.wait_ge(SR[name], read_value(p, u, per, n))

                        def read_done(mm, name):
                            mm.then_inc(SR[name], 1)

                        yield
                        wait_apart(pe, r_in, 48 * (2 * p + u + 1), met)
                        wait_apart(pe, SR["y"], 2 * p + u, met)
                        for t in range(2):
                            mm = nc.tensor.transpose(pr[0][0:D, tok(t)], r_x[:, t, :], k["ident"][0:TT, 0:TT])
                        read_done(mm, "xT_ps")
                        for g2 in range(HV // 2 + 1):
                            if g2 >= 1:
                                if g2 == 1:
                                    need("xT", met=met)
                                else:
                                    need("qT", HV // 2, g2 - 2, met=met)
                                for a in range(2):
                                    mm = nc.tensor.matmul(pr[0][0:D, a * NP:(a + 1) * NP], r_wq[:, (2 * g2 - 2 + a) * D:(2 * g2 - 1 + a) * D], r_xT[:], start=True, stop=True)
                                read_done(mm, "q_ps")
                            if g2 < HV // 2:
                                if g2:
                                    need("kT", HV // 2, g2 - 1, met=met)
                                for a in range(2):
                                    for t in range(2):
                                        mm = nc.tensor.transpose(pr[1][0:D, (2 * a + t) * TT:(2 * a + t + 1) * TT],
                                                                 r_kv[:, t, 0, (2 * g2 + a) * D:(2 * g2 + a + 1) * D], k["ident"][0:TT, 0:TT])
                                read_done(mm, "k_ps")
                            yield
                            yield
                        for n in range(RUNITS):
                            t, h0, nh = read_heads(n)
                            w = (t + 1) * TT
                            if n == 0:
                                need("qT", HV // 2, HV // 2 - 1)
                                need("kT", HV // 2, HV // 2 - 1)
                            else:
                                need("o_ready", RUNITS, n - 1)
                            nc.tensor.matmul(pr[0][0:TT, 0:W], ident_b[0:TT, 0:TT], causal[t][:], start=True, stop=False)
                            for a in range(nh):
                                mm = nc.tensor.matmul(pr[0][0:TT, a * w:(a + 1) * w], r_qT[:, h0 + a, tok(t)], r_kT[:, h0 + a, 0:w],
                                                      start=False, stop=(a == nh - 1))
                            read_done(mm, "s_ps")
                            yield
                            yield
                            need("p_ready", RUNITS, n)
                            for a in range(4):
                                mm = nc.tensor.transpose(pr[1][0:TT, a * TT:(a + 1) * TT], r_P[:, a * TT:(a + 1) * TT], k["ident"][0:TT, 0:TT])
                            read_done(mm, "pt_ps")
                            yield
                            need("pt_ready", RUNITS, n)
                            for a in range(nh):
                                for s in range(t + 1):
                                    col = (a * (t + 1) + s) * TT
                                    mm = nc.tensor.matmul(pr[0][0:TT, a * D:(a + 1) * D], r_PT[:, col:col + TT],
                                                          r_kv[:, s, 1, (h0 + a) * D:(h0 + a + 1) * D], start=(s == 0), stop=(s == t))
                            read_done(mm, "o_ps")
                            yield
                            yield
                        yield
                        for t in range(2):
                            if t == 0:
                                need("o_ready", RUNITS, RUNITS - 1)
                            else:
                                need("oT_ready", 2, 0)
                            flat = r_O[:, t].rearrange("p h d -> p (h d)")
                            for a in range(4):
                                mm = nc.tensor.transpose(pr[1][:, a * TT:(a + 1) * TT], flat[:, a * 128:(a + 1) * 128], k["ident"][0:TT, 0:TT])
                            read_done(mm, "oT_ps")
                            yield
                        need("oT_ready", 2, 1)
                        for t in range(2):
                            for a in range(4):
                                mm = nc.tensor.matmul(pr[0][0:TT, t * D:(t + 1) * D], r_OT[:, t, a * TT:(a + 1) * TT], r_wo[:, a, :], start=(a == 0), stop=(a == 3))
                        read_done(mm, "wo_ps")
                        for _ in range(4):
                            yield

                schedule(pe, pair, front, head, after, reader)

            @block.scalar
            def _(act):
                act.wait_ge(consts_in, CONSTS)
                act.wait_ge(setup, SETUP)
                act.preload_act_table_set(EXP_LN)
                act.wait_ge(wk_ps, 1)
                for p in range(2):
                    a = nc.scalar.activation(wk[:, p * 512:(p + 1) * 512], (ps_s, ps_kv)[p][0:D, :], ACT.Copy)
                a.then_inc(wk_ready, 1)

                def pair(i):
                    own = Chain(act, astep, i, A_ACT_STEPS)

                    for u in range(2):
                        def need(name, per=1, n=0, met=None):
                            if met:
                                wait_apart(act, S[name], i * (2 * per) + u * per + n + 1, met)
                            else:
                                act.wait_ge(S[name], i * (2 * per) + u * per + n + 1)

                        def inv_root(src, dst, name, ready, scale, bias):
                            need(ready)
                            tmp = logs[:, 0:src.free_size()]
                            own.link(nc.scalar.activation(tmp, src, ACT.Ln, scale=scale, bias=bias[:, 0:1]))
                            nc.scalar.activation(dst, tmp, ACT.Exp, scale=-0.5).then_inc(S[name], 1)

                        def ln_root(j):
                            inv_root(mv[:, :, 1], rstd[:], f"rstd{j}", f"var{j}", 1.0, eps_ln)

                        ln_root(1)
                        yield
                        yield
                        yield
                        inv_root(kss[:], krs[:], "krs", "kss", 1.0 / D, eps_rms)
                        for n in range(HQ // 2):
                            yield
                            need("q_rot", HQ // 2, n)
                            nc.scalar.activation(qsq[:, 2 * n:2 * n + 2, :].rearrange("p a t -> p (a t)"), ps[2 + n % 2][0:D, 0:2 * NP], ACT.Square).then_inc(S["q_sq"], 1)
                        inv_root(ps[0][0:TT, 0:2 * HQ], rq[:].rearrange("p t h -> p (t h)"), "rq", "qss", 1.0 / D, eps_rms)

                        def exps(n):
                            t, h0, nh = unit_heads(n)
                            need("nb", UNITS, n)
                            need("rq")
                            w = (t + 1) * TT
                            for a in range(nh):
                                hh = h0 + a
                                e = nc.scalar.activation(P[:, n, a * w:(a + 1) * w], ps[2 + n % 2][0:TT, a * w:(a + 1) * w], ACT.Exp,
                                                         scale=rq[:, t, hh:hh + 1], bias=nb[:, t, hh:hh + 1], accum_out=den[:, t, hh:hh + 1])
                            e.then_inc(S["p_ready"], 1)

                        def copy_pt(n):
                            need("pt_ps", UNITS, n)
                            if n >= 2:
                                need("o_ps", UNITS, n - 2)
                            nc.scalar.activation(PT[n % 2][:], ps[0][0:TT, 0:W], ACT.Copy).then_inc(S["pt_ready"], 1)

                        for n in range(UNITS + 2):
                            yield
                            if 1 <= n <= UNITS:
                                exps(n - 1)
                            if n >= 2:
                                copy_pt(n - 2)
                        yield
                        yield
                        for n in range(4):
                            need("oT_ps", 4, n)
                            nc.scalar.activation(OT[:, n, :], ps[2 + n % 2][:, 0:W], ACT.Copy).then_inc(S["oT_ready"], 1)
                        yield
                        ln_root(2)
                        yield
                        yield
                        need("lmax")
                        nc.scalar.activation(el[:], lg[:], ACT.Exp).then_inc(S["el"], 1)
                        for e in range(NE + 1):
                            if e != 2:
                                yield
                            need("hid_ps", NE + 1, e)
                            for f in range(2):
                                last = nc.scalar.activation(hid[:, e, f, :], ps[2 + e % 2][:, f * NP:(f + 1) * NP], ACT.Gelu, bias=k["b1"][:, e, f:f + 1])
                            last.then_inc(S["hid_ready"], 1)
                        yield
                        act.preload_act_table_set(EXP_LN)
                        ln_root(3)
                        yield
                        yield
                        ln_root(5)
                        yield
                        need("kmx")
                        nc.scalar.activation(eT[:, 0:N], ps[1][0:D, NP:NP + N], ACT.Exp, bias=kmx[:, 0:1], accum_out=ksum[:, 0:1]).then_inc(S["ek_ready"], 1)
                        yield
                        need("hg_ps")
                        nc.scalar.activation(hg, ps[3][0:GH, 0:NP], ACT.Gelu, bias=k["bg1"][:, 0:1]).then_inc(S["hg"], 1)
                        act.preload_act_table_set(EXP_LN)
                        yield
                        need("g_in")
                        nc.scalar.activation(g[:], g[:], ACT.Exp, scale=-1.0).then_inc(S["g_exp"], 1)
                        yield
                        yield
                        yield
                        ln_root(4)
                        if u == 1:
                            own.close()
                        yield

                def front(t, b, i):
                    yield
                    act.wait_ge(xT_ps, t + 1)
                    nc.scalar.activation(xbT[:], ps_s[0:D, 0:TILE], ACT.Copy).then_inc(xT_ready, 1)
                    for _ in range(2):
                        yield
                    act.wait_ge(rows_ready, t)
                    for p in range(2):
                        act.wait_ge(sim_ps, 2 * t + p + 1)
                        nc.scalar.activation(sim[:, p * HV:(p + 1) * HV, :].rearrange("p r k -> p (r k)"), ps_s[:], ACT.Copy).then_inc(sim_in, 1)
                        yield
                        yield
                    for _ in range(17):
                        yield
                    act.wait_ge(shifted, t + 1)
                    nc.scalar.activation(ex[:], ex[:], ACT.Exp).then_inc(exped, 1)
                    for _ in range(PIECES - 24):
                        yield

                def head(t, b, hh):
                    pass

                def after(t, b, hh):
                    if hh % 4 == 3:
                        q = hh // 4
                        act.wait_ge(summed, SLOTS + HV * t + 4 * (q + 1))
                        act.wait_ge(kv_out, 16 * t)
                        nc.scalar.activation(kv_sum[:, :, 4 * q:4 * q + 4, :], ps_kv[:].rearrange("p (h a d) -> p a h d", h=4, a=2), ACT.Copy).then_inc(kv_ready[q], 1)

                def reader(p, tiles):
                    for u in range(2):
                        def need(name, per=1, n=0):
                            act.wait_ge(SR[name], read_value(p, u, per, n))

                        for _ in range(2):
                            yield
                        for g2 in range(HV // 2 + 1):
                            if g2 < HV // 2:
                                need("k_ps", HV // 2, g2)
                                nc.scalar.activation(r_kT[:, 2 * g2:2 * g2 + 2, :].rearrange("p a t -> p (a t)"), pr[1][0:D, 0:2 * NP], ACT.Copy).then_inc(SR["kT"], 1)
                                yield
                            yield
                        for n in range(RUNITS):
                            t, h0, nh = read_heads(n)
                            w = (t + 1) * TT
                            yield
                            need("nb", RUNITS, n)
                            for a in range(nh):
                                hh = h0 + a
                                e = nc.scalar.activation(r_P[:, a * w:(a + 1) * w], pr[0][0:TT, a * w:(a + 1) * w], ACT.Exp,
                                                         scale=D ** -0.5, bias=r_nb[:, t, hh:hh + 1], accum_out=r_den[:, t, hh:hh + 1])
                            e.then_inc(SR["p_ready"], 1)
                            yield
                            need("pt_ps", RUNITS, n)
                            nc.scalar.activation(r_PT[:], pr[1][0:TT, 0:W], ACT.Copy).then_inc(SR["pt_ready"], 1)
                            yield
                            yield
                            yield
                        yield
                        for t in range(2):
                            need("oT_ps", 2, t)
                            nc.scalar.activation(r_OT[:, t, :], pr[1][:, 0:W], ACT.Copy).then_inc(SR["oT_ready"], 1)
                            yield
                        for _ in range(4):
                            yield

                schedule(act, pair, front, head, after, reader)

            @block.gpsimd
            def _(pool):
                pool.sem_inc(summed, SLOTS)

                def pair(i):
                    for _ in range(2 * STAGES):
                        yield

                def front(t, b, i):
                    for _ in range(PIECES):
                        yield

                def head(t, b, hh):
                    if hh == 0:
                        pool.wait_ge(rows_ready, t + 1)
                    wait_apart(pool, summed, t * HV + hh + 1, met)
                    for j in range(TOPK):
                        pool.indirect_dma_start(G[hh % SLOTS][:, j * 128:(j + 1) * 128], None, c["table"],
                                                bass.IndirectOffsetOnAxis(ap=rows_at[b][:, hh * TOPK + j:hh * TOPK + j + 1], axis=0)).then_inc(landed[hh], 16)

                def after(t, b, hh):
                    pass

                def reader(p, tiles):
                    for _ in range(2 * READS):
                        yield

                schedule(pool, pair, front, head, after, reader)

            @block.vector
            def _(dve):
                dve.wait_ge(consts_in, CONSTS)
                nc.vector.memset(ones[:], 1.0).then_inc(setup, 1)
                for t in range(2):
                    nc.vector.tensor_copy(mask[t][:], P[:, t, :]).then_inc(setup, 1)
                    nc.vector.tensor_copy(causal[t][:], masks_in[:, t, :]).then_inc(setup, 1)
                nc.vector.tensor_copy(ident_b[:], k["ident"][:]).then_inc(setup, 1)
                nc.vector.memset(eps_ln[:], LN_EPS).then_inc(setup, 1)
                nc.vector.memset(eps_rms[:], RMS_EPS).then_inc(setup, 1)
                nc.vector.memset(eT[:], 0.0).then_inc(setup, 1)
                nc.vector.scalar_tensor_tensor(out=knq[:], in0=k["qnw"][:], scalar=D ** -0.5, in1=k["knw"][:], op0=ALU.mult, op1=ALU.mult).then_inc(setup, 1)
                dve.wait_ge(setup, SETUP)
                def pair(i):
                    own = Chain(dve, vstep, i, A_STEPS)

                    for u in range(2):
                        def need(name, per=1, n=0, met=None):
                            if met:
                                wait_apart(dve, S[name], i * (2 * per) + u * per + n + 1, met)
                            else:
                                dve.wait_ge(S[name], i * (2 * per) + u * per + n + 1)

                        def ln_stats(src, j):
                            for t in range(2):
                                own.step(nc.vector.bn_stats(stats[:, t, :], src[:, t, :]))
                            own.wait(met)
                            nc.vector.bn_aggr(mv[:, 0, :], stats[:, 0, :])
                            nc.vector.bn_aggr(mv[:, 1, :], stats[:, 1, :]).then_inc(S[f"var{j}"], 1)

                        def ln_apply(src, dst, j, ready):
                            need(f"rstd{j}")
                            need(f"var{j}")
                            nc.vector.tensor_scalar(dst[:, 0, :], src[:, 0, :], mv[:, 0, 0:1], rstd[:, 0:1], ALU.subtract, ALU.mult)
                            nc.vector.tensor_scalar(dst[:, 1, :], src[:, 1, :], mv[:, 1, 0:1], rstd[:, 1:2], ALU.subtract, ALU.mult).then_inc(S[ready], 1)

                        def copy_xT(j, bank):
                            need(f"xT{j}_ps")
                            nc.vector.tensor_copy(xT[:], ps[bank][0:D, 0:NP]).then_inc(S[f"xT{j}"], 1)

                        need("emb_sum")
                        dve.wait_ge(rows_out[u], i * 64)
                        own.link(nc.vector.tensor_tensor(h[u][:], ps[0][0:TT, 0:2 * D].rearrange("p (t d) -> p t d", t=2), k["embed_add"][:], ALU.add))
                        ln_stats(h[u], 1)
                        yield
                        ln_apply(h[u], xn[u], 1, "xn1")
                        yield
                        copy_xT(1, 1)

                        def rotate_q(n):
                            need("q_ps", HQ // 2, n)
                            nc.vector.tensor_tensor(qr[:, 2 * n:2 * n + 2, :], ps[2 + n % 2][:, 0:2 * NP].rearrange("p (a t) -> p a t", a=2),
                                                    bcast(k["rope_q"][:], 1, [2 * D, 2, NP]), ALU.mult).then_inc(S["q_rot"], 1)
                        yield
                        need("kv_ps")
                        kv = ps[0][0:TT, 0:6 * D].rearrange("p (t d) -> p t d", t=2)
                        own.step(nc.vector.tensor_tensor(kk[:], kv[:, :, 0:2 * D], k["rope_k"][:], ALU.mult))
                        own.link(nc.vector.tensor_copy(v[:], kv[:, :, 2 * D:3 * D]))
                        own.link(nc.vector.tensor_tensor(kr[:], kk[:, :, 0:D], kk[:, :, D:2 * D], ALU.add))
                        own.link(nc.vector.tensor_tensor(ksq[:], kr[:], kr[:], ALU.mult))
                        nc.vector.tensor_reduce(kss[:], ksq[:], AX.X, ALU.add).then_inc(S["kss"], 1)
                        yield
                        rotate_q(0)
                        yield
                        rotate_q(1)
                        need("krs")
                        for t in range(2):
                            own.step(nc.vector.tensor_scalar(kr[:, t, :], kr[:, t, :], krs[:, t:t + 1], None, ALU.mult))
                        own.wait()
                        own.step(nc.vector.tensor_tensor(kdup[:, :, 0, :], kr[:], bcast(knq[:], 1, [TT, 2, D]), ALU.mult))
                        nc.vector.tensor_tensor(kdup[:, :, 1, :], kr[:], bcast(knq[:], 1, [TT, 2, D]), ALU.mult).then_inc(S["kdup"], 1)
                        for n in range(2, HQ // 2):
                            yield
                            rotate_q(n)
                        need("kT_ps")
                        nc.vector.tensor_copy(kT[:], ps[1][:, 0:NP]).then_inc(S["kT"], 1)

                        def unit_max(n):
                            t, h0, nh = unit_heads(n)
                            need("s_ps", UNITS, n)
                            own.link(nc.vector.tensor_reduce(m[:, t, h0:h0 + nh], ps[2 + n % 2][0:TT, 0:W].rearrange("p (a s) -> p a s", a=nh), AX.X, ALU.max))
                            if n == 0:
                                need("rq")
                            nc.vector.scalar_tensor_tensor(out=nb[:, t, h0:h0 + nh], in0=m[:, t, h0:h0 + nh], scalar=-1.0, in1=rq[:, t, h0:h0 + nh],
                                                           op0=ALU.mult, op1=ALU.mult).then_inc(S["nb"], 1)

                        def scale_o(n):
                            t, h0, nh = unit_heads(n)
                            h8 = h0 // 8 * 8
                            need("o_ps", UNITS, n)
                            own.link(nc.vector.reciprocal(rden[:, t, h8:h8 + 8], den[:, t, h8:h8 + 8]))
                            nc.vector.tensor_tensor(O[:, t, h8:h8 + 8, :], ps[1][0:TT, :].rearrange("p (a d) -> p a d", a=8),
                                                    bcast(rden[:, t, h8:h8 + 8], 2, [TT, 8, D]), ALU.mult).then_inc(S["o_ready"], 1)

                        for n in range(UNITS + 4):
                            yield
                            if 1 <= n <= UNITS:
                                unit_max(n - 1)
                            if n >= 4:
                                t, h0, nh = unit_heads(n - 4)
                                if (h0 + nh) % 8 == 0:
                                    scale_o(n - 4)
                        yield
                        need("wo_ps")
                        own.link(nc.vector.tensor_tensor(h[u][:], ps[0][0:TT, 0:2 * D].rearrange("p (t d) -> p t d", t=2), h[u][:], ALU.add))
                        ln_stats(h[u], 2)
                        yield
                        ln_apply(h[u], xn[u], 2, "xn2")
                        yield
                        copy_xT(2, 1)
                        need("lg_ps")
                        l2 = ps[0][0:TT, 0:2 * NE].rearrange("p (t e) -> p t e", t=2)
                        own.link(nc.vector.tensor_reduce(lmax[:], l2, AX.X, ALU.max))
                        nc.vector.tensor_tensor(lg[:], l2, bcast(lmax[:], 2, [TT, 2, NE]), ALU.subtract).then_inc(S["lmax"], 1)
                        yield
                        need("el", met=met)
                        for t in range(2):
                            own.step(nc.vector.max(top[:, t, :], el[:, t, :]))
                        own.wait(met)
                        for t in range(2):
                            own.step(nc.vector.max_index(topi[:, t, :], top[:, t, :], el[:, t, :]))
                        own.link(nc.vector.tensor_tensor(tsum[:], top[:, :, 0], top[:, :, 1], ALU.add))
                        own.step(nc.vector.tensor_copy(topf[:], topi[:, :, 0:2]))
                        own.link(nc.vector.reciprocal(trec[:], tsum[:]))
                        own.step(nc.vector.tensor_tensor(tw[:], top[:, :, 0:2], bcast(trec[:], 2, [TT, 2, 2]), ALU.mult))
                        for t in range(2):
                            own.step(nc.vector.tensor_tensor(oh[:, t], bcast(k["iota8"][:], 1, [TT, 2, NE]), bcast(topf[:, t, :], 2, [TT, 2, NE]), ALU.is_equal))
                        own.wait()
                        own.link(nc.vector.tensor_tensor(oh[:], oh[:], bcast(tw[:], 3, [TT, 2, 2, NE]), ALU.mult))
                        own.step(nc.vector.tensor_tensor(gate[:], oh[:, :, 0, :], oh[:, :, 1, :], ALU.add))
                        own.wait(met)
                        yield
                        yield
                        yield
                        yield
                        yield
                        yield
                        yield
                        yield
                        need("moe_ps")
                        for t in range(2):
                            own.step(nc.vector.tensor_tensor(mo[:, t], ps[t][0:TT, :].rearrange("p (e d) -> p e d", e=NE), k["b2p"][:], ALU.add))
                        own.step(nc.vector.tensor_tensor(h[u][:], ps[2][0:TT, 0:2 * D].rearrange("p (t d) -> p t d", t=2), h[u][:], ALU.add))
                        own.wait()
                        own.step(nc.vector.tensor_tensor(h[u][:], h[u][:], bcast(k["b2s"][:], 1, [TT, 2, D]), ALU.add))
                        for t in range(2):
                            own.step(nc.vector.tensor_tensor(mo[:, t], mo[:, t], bcast(gate[:, t, :], 2, [TT, NE, D]), ALU.mult))
                        own.wait()
                        own.link(nc.vector.tensor_reduce(mr[:], mo.rearrange("p t e d -> p t d e"), AX.X, ALU.add))
                        own.link(nc.vector.tensor_tensor(h[u][:], h[u][:], mr[:], ALU.add))
                        ln_stats(h[u], 3)
                        yield
                        ln_apply(h[u], xn[u], 3, "xn3")
                        yield
                        copy_xT(3, 0)
                        ln_stats(xn[u], 5)
                        yield
                        need("qkv_ps")
                        own.step(nc.vector.tensor_copy(qT, ps[1][0:D, 0:NP]))
                        own.link(nc.vector.tensor_reduce(kmx[:], ps[1][0:D, NP:NP + N], AX.X, ALU.max))
                        nc.vector.tensor_scalar(kmx[:], kmx[:], -1.0, None, ALU.mult).then_inc(S["kmx"], 1)
                        nc.vector.tensor_copy(v[:], ps[2][0:TT, 0:2 * D].rearrange("p (t d) -> p t d", t=2)).then_inc(S["lin_v"], 1)
                        ln_apply(xn[u], g, 5, "xg")
                        yield
                        need("xgT_ps")
                        nc.vector.tensor_scalar(xgT, ps[0][0:D, 0:NP], k["lng"][:, 0:1], k["lnb"][:, 0:1], ALU.mult, ALU.add).then_inc(S["xgT"], 1)
                        need("ek_ps")
                        nc.vector.tensor_copy(ek, ps[2][0:TT, 0:2 * D].rearrange("p (t d) -> p t d", t=2)).then_inc(S["ek"], 1)
                        own.step(nc.vector.reciprocal(krec[:], ksum[:]))
                        own.wait(met)
                        yield
                        need("ctx_ps")
                        nc.vector.scalar_tensor_tensor(out=ctxs[:], in0=ps[0][0:D, 0:D], scalar=krec[:, 0:1], in1=k["blocks"][:],
                                                       op0=ALU.mult, op1=ALU.mult).then_inc(S["ctx"], 1)
                        need("g_ps")
                        nc.vector.tensor_tensor(g[:], ps[2][0:TT, 0:2 * D].rearrange("p (t d) -> p t d", t=2), bcast(k["bg2"][:], 1, [TT, 2, D]), ALU.add).then_inc(S["g_in"], 1)
                        yield
                        need("g_exp")
                        own.link(nc.vector.tensor_scalar(g[:], g[:], 1.0, None, ALU.add))
                        own.link(nc.vector.reciprocal(g[:], g[:]))
                        need("lin_ps")
                        nc.vector.tensor_tensor(g[:], ps[1][0:TT, 0:2 * D].rearrange("p (t d) -> p t d", t=2), g[:], ALU.mult).then_inc(S["og"], 1)
                        yield
                        need("ogT_ps")
                        nc.vector.tensor_copy(xgT, ps[3][0:D, 0:NP]).then_inc(S["ogT"], 1)
                        own.step(nc.vector.tensor_tensor(h[u][:], h[u][:], bcast(k["bproj"][:], 1, [TT, 2, D]), ALU.add))
                        own.wait(met)
                        yield
                        need("proj_ps")
                        own.link(nc.vector.tensor_tensor(h[u][:], ps[2][0:TT, 0:2 * D].rearrange("p (t d) -> p t d", t=2), h[u][:], ALU.add))
                        ln_stats(h[u], 4)
                        ln_apply(h[u], xn[u], 4, "xn4")
                        if u == 1:
                            own.close()
                        yield

                def front(t, b, i):
                    own = Chain(dve, bstep, t, FRONT_STEPS)
                    for _ in range(6):
                        yield
                    wait_apart(dve, sim_in, 2 * t + 2, met)
                    val = [half[p][:, 0] for p in range(2)]
                    for a in range(2):
                        src = sim if a == 0 else sim2
                        cols = slice(8 * a, 8 * a + 8)
                        for r in range(R):
                            own.step(nc.vector.max(val[r // HV][:, r % HV, cols], src[:, r, :]))
                            if r == HV - 1:
                                yield
                        yield
                        own.wait(met)
                        for r in range(R):
                            own.step(nc.vector.max_index(ranks[:, r, cols], val[r // HV][:, r % HV, cols], src[:, r, :]))
                            if r == HV - 1:
                                yield
                        yield
                        if a == 0:
                            for r in range(R):
                                own.step(nc.vector.match_replace(sim2[:, r, :], val[r // HV][:, r % HV, cols], sim[:, r, :], LOWEST))
                                if r == HV - 1:
                                    yield
                            yield
                        own.wait(met if a == 0 else None)
                    own.step(nc.vector.tensor_copy(half[0][:, 1], ranks[:, 0:HV, :]))
                    own.step(nc.vector.scalar_tensor_tensor(out=half[1][:, 1].rearrange("p h k -> p (h k)"), in0=ranks[:, HV:R, :].rearrange("p h k -> p (h k)"), scalar=float(NK),
                                                            in1=offs[:].rearrange("p h k -> p (h k)"), op0=ALU.mult, op1=ALU.add))
                    yield
                    own.wait()
                    f0 = half[0][:].rearrange("p a h k -> p (a h) k")
                    f1 = half[1][:].rearrange("p a h k -> p (a h) k")
                    pr = pairs[:].rearrange("p a h k -> p (a h) k")
                    at = r0 = 0
                    while r0 < TOPK:
                        n = CUTS[r0]
                        rn = CUTS.count(n)
                        out = pr[:, :, at:at + rn * n].rearrange("p g (r n) -> p g r n", r=rn)
                        own.step(nc.vector.tensor_tensor(out, f0[:, :, r0:r0 + rn].unsqueeze(3).to_broadcast([TILE, R, rn, n]),
                                                         f1[:, :, 0:n].unsqueeze(2).to_broadcast([TILE, R, rn, n]), ALU.add))
                        at += rn * n
                        r0 += rn
                    yield
                    own.wait(met)
                    for a in range(2):
                        src = pairs[:, 0] if a == 0 else pairs2[:]
                        cols = slice(8 * a, 8 * a + 8)
                        for hh in range(HV):
                            own.step(nc.vector.max(best[:, hh, cols], src[:, hh, :]))
                        yield
                        own.wait(met)
                        for hh in range(HV):
                            own.step(nc.vector.max_index(place[:, hh, cols], best[:, hh, cols], src[:, hh, :]))
                        if a == 0:
                            yield
                            for hh in range(HV):
                                own.step(nc.vector.match_replace(pairs2[:, hh, :], best[:, hh, cols], pairs[:, 0, hh, :], LOWEST))
                            yield
                        own.wait(met if a == 0 else None)
                    yield
                    own.step(nc.vector.tensor_copy(placef[:], place[:]))
                    nc.vector.tensor_tensor(ex[:], best[:], best[:, :, 0:1].to_broadcast([TILE, HV, TOPK]), ALU.subtract).then_inc(shifted, 1)
                    own.wait()
                    for g0 in range(0, HV, HG):
                        gh = slice(g0, g0 + HG)
                        own.step(nc.vector.tensor_tensor(onehot.rearrange("p h k c -> p (h k) c"), iota[:].unsqueeze(1).to_broadcast([TILE, HG * TOPK, NC]),
                                                         placef[:, gh, :].rearrange("p h k -> p (h k)").unsqueeze(2).to_broadcast([TILE, HG * TOPK, NC]), ALU.is_equal))
                        yield
                        own.wait()
                        own.link(nc.vector.tensor_tensor(onehot, onehot, pairs[:, 1, gh, :].unsqueeze(2).to_broadcast([TILE, HG, TOPK, NC]), ALU.mult))
                        own.step(nc.vector.tensor_reduce(rowf[:, gh, :], onehot, AX.X, ALU.add))
                        if g0 + HG < HV:
                            yield
                        own.wait()
                    nc.vector.tensor_copy(rows_at[b][:], rowf[:].rearrange("p h k -> p (h k)")).then_inc(rows_ready, 1)
                    yield
                    dve.wait_ge(exped, t + 1)
                    own.link(nc.vector.tensor_reduce(ssum[:], ex[:], AX.X, ALU.add))
                    own.link(nc.vector.reciprocal(ssum[:], ssum[:]))
                    nc.vector.tensor_tensor(weight[b][:], ex[:], ssum[:].unsqueeze(2).to_broadcast([TILE, HV, TOPK]), ALU.mult).then_inc(weight_ready, 1)
                    own.close()
                    yield

                def head(t, b, hh):
                    if hh == 0:
                        dve.wait_ge(weight_ready, t + 1)
                    dve.wait_ge(landed[hh], (t + 1) * (16 * TOPK))
                    rows = G[hh % SLOTS][:].rearrange("p (k d) -> p k d", k=TOPK)
                    nc.vector.tensor_tensor(rows, rows, weight[b][:, hh, :].unsqueeze(2).to_broadcast([TILE, TOPK, 2 * D]), ALU.mult).then_inc(weighed, 1)

                def after(t, b, hh):
                    pass

                def reader(p, tiles):
                    own = Chain(dve, rstep, p, R_STEPS)
                    for u in range(2):
                        def need(name, per=1, n=0):
                            dve.wait_ge(SR[name], read_value(p, u, per, n))

                        for _ in range(2):
                            yield
                        need("xT_ps")
                        nc.vector.tensor_copy(r_xT[:], pr[0][0:D, 0:NP]).then_inc(SR["xT"], 1)
                        for g2 in range(HV // 2):
                            yield
                            yield
                            need("q_ps", HV // 2, g2)
                            nc.vector.tensor_copy(r_qT[:, 2 * g2:2 * g2 + 2, :].rearrange("p a t -> p (a t)"), pr[0][0:D, 0:2 * NP]).then_inc(SR["qT"], 1)
                        yield
                        for n in range(RUNITS):
                            t, h0, nh = read_heads(n)
                            heads = slice(h0, h0 + nh)
                            yield
                            need("s_ps", RUNITS, n)
                            own.link(nc.vector.tensor_reduce(r_m[:, t, heads], pr[0][0:TT, 0:W].rearrange("p (a s) -> p a s", a=nh), AX.X, ALU.max))
                            nc.vector.tensor_scalar(r_nb[:, t, heads], r_m[:, t, heads], -(D ** -0.5), None, ALU.mult).then_inc(SR["nb"], 1)
                            yield
                            yield
                            yield
                            need("o_ps", RUNITS, n)
                            own.link(nc.vector.reciprocal(r_rden[:, t, heads], r_den[:, t, heads]))
                            nc.vector.tensor_tensor(r_O[:, t, heads, :], pr[0][0:TT, 0:nh * D].rearrange("p (a d) -> p a d", a=nh),
                                                    bcast(r_rden[:, t, heads], 2, [TT, nh, D]), ALU.mult).then_inc(SR["o_ready"], 1)
                            yield
                        for _ in range(4):
                            yield
                        need("wo_ps")
                        dve.wait_ge(r_out, 32 * (2 * p + u))
                        nc.vector.tensor_tensor(r_y[:], pr[0][0:TT, 0:2 * D].rearrange("p (t d) -> p t d", t=2), r_h[:], ALU.add).then_inc(SR["y"], 1)
                        if u == 1:
                            own.close()
                        for _ in range(3):
                            yield

                schedule(dve, pair, front, head, after, reader)

def vit_tower(nc, c, out):
    h3 = nc.dram_tensor("h3_rows", (ROWS, D), F32, kind="Internal").ap()
    xn4 = nc.dram_tensor("xn4_rows", (ROWS, D), F32, kind="Internal").ap()
    kv = nc.dram_tensor("kv_rows", (ROWS, 2 * HV * D), F32, kind="Internal").ap()
    with nc.sbuf_tensor("pad", [ROWS - B * N, D], F32) as pad, nc.semaphore("pad_set") as pad_set, nc.semaphore("pad_out") as pad_out:
        with nc.Block() as block:
            @block.gpsimd
            def _(pool):
                nc.gpsimd.memset(pad[:], 0.0).then_inc(pad_set, 1)

            @block.sync
            def _(sp):
                sp.wait_ge(pad_set, 1)
                for rows in (h3, xn4):
                    sp.dma_start(rows[B * N:ROWS, :], pad[:]).then_inc(pad_out, 16)
                sp.wait_ge(pad_out, 32)
    tower(nc, c, h3, xn4, kv, out)


def _layout(inp):
    import numpy as np

    a = {k: np.asarray(v) for k, v in inp.items()}
    G = IMG // PATCH
    px = a["x"].reshape(B, CH, G, PATCH, G, PATCH).transpose(0, 1, 3, 5, 2, 4).reshape(B, KC, 128, G * G)
    pixT = np.zeros((B + 2, 128, KC, NP), np.float32)
    pixT[:B, :, :, 1:N] = px.transpose(0, 2, 1, 3)
    rows = lambda v, n: np.repeat(v.reshape(1, -1), n, axis=0)
    add = rows(a["L0_tok_b"], NP)
    add[0] = a["cls_tok"].reshape(-1)
    swap = np.arange(D) ^ 1
    wq = a["L0_attn_wq"].reshape(HQ, D, D)
    wqq = np.concatenate([wq, wq[:, swap]], axis=1).transpose(2, 0, 1)
    wk, wv = a["L0_attn_wkv"][:D], a["L0_attn_wkv"][D:]
    t = np.arange(NP, dtype=np.float32)
    freqs = np.float32(10000.0) ** (np.float32(-2.0) * np.arange(D // 2, dtype=np.float32) / np.float32(D))
    theta = t[:, None] * freqs[None, :]
    cos = np.repeat(np.cos(theta), 2, axis=1)
    sin = np.repeat(np.sin(theta), 2, axis=1) * np.where(np.arange(D) % 2 == 0, np.float32(-1), np.float32(1))
    rope = np.concatenate([cos, sin], axis=1).astype(np.float32)
    tiles = lambda v: v.reshape(2, TT, -1).transpose(1, 0, 2)
    q, s = np.arange(NP)[:, None], np.arange(NP)[None, :]

    def masks(ok):
        m = np.where(ok, np.float32(0), np.float32(NEG))
        return np.stack([np.tile(m[:TT, :TT], (1, 4)), np.tile(m[TT:, :], (1, 2))])
    causal = masks(s <= q)
    w1 = np.concatenate([a["L0_ffn_W1p"], a["L0_ffn_W1s"][None]]).transpose(1, 0, 2)
    b1 = np.concatenate([a["L0_ffn_b1p"], a["L0_ffn_b1s"][None]]).reshape(NE + 1, 2, 128).transpose(2, 0, 1)
    w2 = np.concatenate([a["L0_ffn_W2p"], a["L0_ffn_W2s"][None]]).reshape(NE + 1, 2, 128, D).transpose(2, 0, 1, 3)
    col = lambda v: v.reshape(-1, 1)
    return {k: np.ascontiguousarray(v) for k, v in dict(
        pixT=pixT, patch_w=a["L0_tok_W"].T.reshape(KC, 128, D).transpose(1, 0, 2), embed_add=tiles(add),
        ident=np.eye(128, dtype=np.float32), wqq=wqq,
        wkkv=np.concatenate([wk, wk[swap], wv]).T, rope_q=rope.T, rope_k=tiles(rope),
        wo=a["L0_attn_wo"].T.reshape(HQ * D // 128, 128, D).transpose(1, 0, 2), wr=a["L0_ffn_Wr"], w1=w1, b1=b1, w2=w2,
        b2p=np.repeat(a["L0_ffn_b2p"][None], TT, axis=0), b2s=rows(a["L0_ffn_b2s"], TT),
        iota8=rows(np.arange(NE, dtype=np.float32), TT), wqkv=a["L1_attn_Wqkv"], wproj=a["L1_attn_Wproj"],
        bproj=rows(a["L1_attn_bproj"], TT), lng=col(a["L1_attn_ln_g"]), lnb=col(a["L1_attn_ln_b"]), wg1=a["L1_attn_Wg1"],
        bg1=col(a["L1_attn_bg1"]), wg2=a["L1_attn_Wg2"], bg2=rows(a["L1_attn_bg2"], TT),
        blocks=np.kron(np.eye(8, dtype=np.float32), np.ones((D // 8, D // 8), np.float32)),
        qnw=rows(a["L0_attn_q_norm_w"], TT), knw=rows(a["L0_attn_k_norm_w"], TT),
        mask=masks((s <= q) & (q - s <= WINDOW)), causal0=causal[0], causal1=causal[1],
        wpkT=a["L1_ffn_Wq_pk"].T.reshape(2 * HV, D // 2, D).transpose(1, 0, 2),
        keysT=a["L1_ffn_pk_keys"].transpose(3, 0, 2, 1).reshape(D // 2, 2 * HV, NK),
        offs=np.broadcast_to((np.arange(HV, dtype=np.float32) * (NK * NK))[None, :, None], (TILE, HV, TOPK)),
        iota=rows(np.arange(NC, dtype=np.float32), TILE),
        table=np.concatenate([a["L1_ffn_keys_table"], a["L1_ffn_values_table"]], axis=1),
        wq_mem=a["L1_ffn_Wq"], wo_mem=a["L1_ffn_Wo"].reshape(HV * D // 128, 128, D).transpose(1, 0, 2),
    ).items()}


def kernel(**inputs):
    import concourse.bacc as bacc
    from concourse import mybir as _mybir
    from concourse.bass_utils import run_bass_kernel_spmd as run

    nc = bacc.Bacc("TRN2", target_bir_lowering=False, num_devices=1)
    arrays = _layout(inputs)
    c = {k: nc.dram_tensor("in_" + k, v.shape, _mybir.dt.from_np(v.dtype), kind="ExternalInput").ap() for k, v in arrays.items()}
    out = nc.dram_tensor("out", (B, N, D), F32, kind="ExternalOutput").ap()
    vit_tower(nc, c, out)
    r = run(nc, [{"in_" + k: v for k, v in arrays.items()}], core_ids=[0])
    return r.results[0]["out"]
```
